# Optimizing a Trainium2 kernel written in Bass

```python
import numpy as np
import jax
import jax.numpy as jnp

def _softmax(x, axis=-1):
    return jax.nn.softmax(x, axis=axis)

def _gelu(x):
    return jax.nn.gelu(x, approximate=True)

def _silu(x):
    return jax.nn.silu(x)

def _sigmoid(x):
    return jax.nn.sigmoid(x)

def _layernorm(x, axis=-1, eps=1e-05):
    m = jnp.mean(x, axis=axis, keepdims=True)
    v = jnp.var(x, axis=axis, keepdims=True)
    return (x - m) / jnp.sqrt(v + eps)

def _scatter_add(tgt, idx, src, axis=0):
    return tgt.at[idx].add(src)

def _segment_sum(src, seg, n):
    return jax.ops.segment_sum(src, seg, n)
kernel_name = 'mk_decoder_postln_d1_seqx_r4_68b6b9'

def setup_inputs(seed: int=0):
    np.random.seed(seed)
    _w = jnp.asarray

    def _rec_inputs():
        import jax
        import jax.numpy as jnp
        _rk = jax.random.key(seed)
        x = -0.0003929 + 0.9999 * jax.random.normal(jax.random.fold_in(_rk, 1), (16, 112, 256), jnp.float32)
        _lenS = 112 - jax.random.randint(jax.random.fold_in(_rk, 7), (16,), 0, max(1, 112 // 4) + 1, jnp.int32)
        _lenS2 = 375 - jax.random.randint(jax.random.fold_in(_rk, 8), (16,), 0, max(1, 375 // 4) + 1, jnp.int32)
        _ctx_1024P = jax.random.normal(jax.random.fold_in(_rk, 11), (16, 16, 256), jnp.float32)
        _ctx_1024c = jax.random.dirichlet(jax.random.fold_in(_rk, 511), 0.3 * jnp.ones((16,), jnp.float32), (16, 375))
        _ctx_1024t = jnp.einsum('bsk,bkd->bsd', _ctx_1024c, _ctx_1024P)
        _ctx_1024t = _ctx_1024t * jax.lax.rsqrt(jnp.mean(jnp.square(_ctx_1024t)) + 1e-12) * 0.953939
        ctx_1024 = 2.81802e-05 + 1.00001 * (_ctx_1024t + 0.3 * jax.random.normal(jax.random.fold_in(_rk, 611), (16, 375, 256), jnp.float32))
        return (x, ctx_1024)
    x, ctx_1024 = _rec_inputs()

    def _L0_attn_setup():
        import jax, jax.numpy as jnp
        import numpy as np
        from jax import lax
        L, B, T, C, F = (4, 4, 512, 256, 1024)
        EPS = 1e-05

        def layernorm(x, w, b):
            m = jnp.mean(x, axis=-1, keepdims=True)
            v = jnp.var(x, axis=-1, keepdims=True)
            return (x - m) * lax.rsqrt(v + EPS) * w + b

        def time_shift(x):
            return jnp.pad(x, ((0, 0), (1, 0), (0, 0)))[:, :-1]

        def wkv(time_decay, time_first, k, v):
            w = -jnp.exp(time_decay)
            u = time_first
            kt = jnp.swapaxes(k, 0, 1)
            vt = jnp.swapaxes(v, 0, 1)
            Bn, Cn = (k.shape[0], k.shape[2])
            init = (jnp.zeros((Bn, Cn), k.dtype), jnp.zeros((Bn, Cn), k.dtype), jnp.full((Bn, Cn), -1e+38, k.dtype))

            def step(carry, kv):
                aa, bb, pp = carry
                kk, vv = kv
                ww = u + kk
                qq = jnp.maximum(pp, ww)
                e1 = jnp.exp(pp - qq)
                e2 = jnp.exp(ww - qq)
                out = (e1 * aa + e2 * vv) / (e1 * bb + e2)
                ww2 = pp + w
                qq2 = jnp.maximum(ww2, kk)
                e1b = jnp.exp(ww2 - qq2)
                e2b = jnp.exp(kk - qq2)
                return ((e1b * aa + e2b * vv, e1b * bb + e2b, qq2), out)
            _, out = lax.scan(step, init, (kt, vt))
            return jnp.swapaxes(out, 0, 1)
        key = jax.random.key(seed)
        ks = jax.random.split(key, 16)
        s = 0.02
        d = {}
        d['x'] = jax.random.normal(ks[0], (B, T, C), jnp.float32)
        d['ln0_w'] = jnp.ones((C,), jnp.float32)
        d['ln0_b'] = jnp.zeros((C,), jnp.float32)
        d['ln1_w'] = jnp.ones((L, C), jnp.float32)
        d['ln1_b'] = jnp.zeros((L, C), jnp.float32)
        d['ln2_w'] = jnp.ones((L, C), jnp.float32)
        d['ln2_b'] = jnp.zeros((L, C), jnp.float32)
        d['time_decay'] = jax.random.normal(ks[1], (L, C), jnp.float32) * 0.5
        d['time_first'] = jax.random.normal(ks[2], (L, C), jnp.float32) * 0.5 + jnp.float32(np.log(0.3))
        d['tmk'] = jax.random.uniform(ks[3], (L, C), jnp.float32)
        d['tmv'] = jax.random.uniform(ks[4], (L, C), jnp.float32)
        d['tmr'] = jax.random.uniform(ks[5], (L, C), jnp.float32)
        d['Wk'] = jax.random.normal(ks[6], (L, C, C), jnp.float32) * s
        d['Wv'] = jax.random.normal(ks[7], (L, C, C), jnp.float32) * s
        d['Wr'] = jax.random.normal(ks[8], (L, C, C), jnp.float32) * s
        d['Wo'] = jax.random.normal(ks[9], (L, C, C), jnp.float32) * s
        d['cmk'] = jax.random.uniform(ks[10], (L, C), jnp.float32)
        d['cmr'] = jax.random.uniform(ks[11], (L, C), jnp.float32)
        d['Wck'] = jax.random.normal(ks[12], (L, F, C), jnp.float32) * s
        d['Wcv'] = jax.random.normal(ks[13], (L, C, F), jnp.float32) * s
        d['Wcr'] = jax.random.normal(ks[14], (L, C, C), jnp.float32) * s
        return d
    _L0_attn_all = _L0_attn_setup()
    _L0_attn_in = {k: v for k, v in _L0_attn_all.items() if k in ('ln0_w', 'ln0_b', 'ln1_w', 'ln1_b', 'ln2_w', 'ln2_b', 'time_decay', 'time_first', 'tmk', 'tmv', 'tmr', 'Wk', 'Wv', 'Wr', 'Wo', 'cmk', 'cmr', 'Wck', 'Wcv', 'Wcr')}
    del _L0_attn_all

    def _L0_xattn_setup():
        import jax, jax.numpy as jnp
        import numpy as np
        B, T, C, H = (4, 1024, 256, 16)
        D = C // H

        def _heads(t):
            b, n, c = t.shape
            return t.reshape(b, n, H, D).transpose(0, 2, 1, 3)
        key = jax.random.key(seed)
        ks = jax.random.split(key, 10)
        s = 1.0 / np.sqrt(C)
        return {'x': jax.random.normal(ks[0], (B, T, C), jnp.float32), 'y': jax.random.normal(ks[1], (B, T, C), jnp.float32), 'Wq': jax.random.normal(ks[2], (C, C), jnp.float32) * s, 'bq': jnp.zeros((C,), jnp.float32), 'Wk': jax.random.normal(ks[3], (C, C), jnp.float32) * s, 'bk': jnp.zeros((C,), jnp.float32), 'Wv': jax.random.normal(ks[4], (C, C), jnp.float32) * s, 'bv': jnp.zeros((C,), jnp.float32), 'Wp': jax.random.normal(ks[5], (C, C), jnp.float32) * s, 'bp': jnp.zeros((C,), jnp.float32)}
    _L0_xattn_all = _L0_xattn_setup()
    _L0_xattn_in = {k: v for k, v in _L0_xattn_all.items() if k in ('Wq', 'bq', 'Wk', 'bk', 'Wv', 'bv', 'Wp', 'bp')}
    del _L0_xattn_all

    def _L0_ffn_setup():
        import jax, jax.numpy as jnp
        import numpy as np
        B, S, H = (2, 256, 256)
        E, F = (8, 1024)
        GATE_TEMP = 0.1
        key = jax.random.key(seed)
        ks = jax.random.split(key, 6)
        s_h = 1.0 / np.sqrt(H)
        s_f = 1.0 / np.sqrt(F)
        return {'hidden_states': jax.random.normal(ks[0], (B, S, H), dtype=jnp.float32), 'w_router': jax.random.normal(ks[1], (H, E), dtype=jnp.float32) * s_h, 'w_gating': jax.random.normal(ks[2], (H, E), dtype=jnp.float32) * s_h, 'w_gate': jax.random.normal(ks[3], (E, H, F), dtype=jnp.float32) * s_h, 'w_up': jax.random.normal(ks[4], (E, H, F), dtype=jnp.float32) * s_h, 'w_down': jax.random.normal(ks[5], (E, F, H), dtype=jnp.float32) * s_f}
    _L0_ffn_all = _L0_ffn_setup()
    _L0_ffn_in = {k: v for k, v in _L0_ffn_all.items() if k in ('w_router', 'w_gating', 'w_gate', 'w_up', 'w_down')}
    del _L0_ffn_all
    return {'x': x, 'ctx_1024': ctx_1024, 'L0_attn_ln0_w': _L0_attn_in['ln0_w'], 'L0_attn_ln0_b': _L0_attn_in['ln0_b'], 'L0_attn_ln1_w': _L0_attn_in['ln1_w'], 'L0_attn_ln1_b': _L0_attn_in['ln1_b'], 'L0_attn_ln2_w': _L0_attn_in['ln2_w'], 'L0_attn_ln2_b': _L0_attn_in['ln2_b'], 'L0_attn_time_decay': _L0_attn_in['time_decay'], 'L0_attn_time_first': _L0_attn_in['time_first'], 'L0_attn_tmk': _L0_attn_in['tmk'], 'L0_attn_tmv': _L0_attn_in['tmv'], 'L0_attn_tmr': _L0_attn_in['tmr'], 'L0_attn_Wk': _L0_attn_in['Wk'], 'L0_attn_Wv': _L0_attn_in['Wv'], 'L0_attn_Wr': _L0_attn_in['Wr'], 'L0_attn_Wo': _L0_attn_in['Wo'], 'L0_attn_cmk': _L0_attn_in['cmk'], 'L0_attn_cmr': _L0_attn_in['cmr'], 'L0_attn_Wck': _L0_attn_in['Wck'], 'L0_attn_Wcv': _L0_attn_in['Wcv'], 'L0_attn_Wcr': _L0_attn_in['Wcr'], 'L0_xattn_Wq': _L0_xattn_in['Wq'], 'L0_xattn_bq': _L0_xattn_in['bq'], 'L0_xattn_Wk': _L0_xattn_in['Wk'], 'L0_xattn_bk': _L0_xattn_in['bk'], 'L0_xattn_Wv': _L0_xattn_in['Wv'], 'L0_xattn_bv': _L0_xattn_in['bv'], 'L0_xattn_Wp': _L0_xattn_in['Wp'], 'L0_xattn_bp': _L0_xattn_in['bp'], 'L0_ffn_w_router': _L0_ffn_in['w_router'], 'L0_ffn_w_gating': _L0_ffn_in['w_gating'], 'L0_ffn_w_gate': _L0_ffn_in['w_gate'], 'L0_ffn_w_up': _L0_ffn_in['w_up'], 'L0_ffn_w_down': _L0_ffn_in['w_down']}

def reference(x, ctx_1024, L0_attn_ln0_w, L0_attn_ln0_b, L0_attn_ln1_w, L0_attn_ln1_b, L0_attn_ln2_w, L0_attn_ln2_b, L0_attn_time_decay, L0_attn_time_first, L0_attn_tmk, L0_attn_tmv, L0_attn_tmr, L0_attn_Wk, L0_attn_Wv, L0_attn_Wr, L0_attn_Wo, L0_attn_cmk, L0_attn_cmr, L0_attn_Wck, L0_attn_Wcv, L0_attn_Wcr, L0_xattn_Wq, L0_xattn_bq, L0_xattn_Wk, L0_xattn_bk, L0_xattn_Wv, L0_xattn_bv, L0_xattn_Wp, L0_xattn_bp, L0_ffn_w_router, L0_ffn_w_gating, L0_ffn_w_gate, L0_ffn_w_up, L0_ffn_w_down):
    import jax
    import jax.numpy as jnp

    def _L0_attn_ref(x, ln0_w, ln0_b, ln1_w, ln1_b, ln2_w, ln2_b, time_decay, time_first, tmk, tmv, tmr, Wk, Wv, Wr, Wo, cmk, cmr, Wck, Wcv, Wcr):
        import jax, jax.numpy as jnp
        import numpy as np
        from jax import lax
        L, B, T, C, F = (4, 4, 512, 256, 1024)
        EPS = 1e-05

        def layernorm(x, w, b):
            m = jnp.mean(x, axis=-1, keepdims=True)
            v = jnp.var(x, axis=-1, keepdims=True)
            return (x - m) * lax.rsqrt(v + EPS) * w + b

        def time_shift(x):
            return jnp.pad(x, ((0, 0), (1, 0), (0, 0)))[:, :-1]

        def wkv(time_decay, time_first, k, v):
            w = -jnp.exp(time_decay)
            u = time_first
            kt = jnp.swapaxes(k, 0, 1)
            vt = jnp.swapaxes(v, 0, 1)
            Bn, Cn = (k.shape[0], k.shape[2])
            init = (jnp.zeros((Bn, Cn), k.dtype), jnp.zeros((Bn, Cn), k.dtype), jnp.full((Bn, Cn), -1e+38, k.dtype))

            def step(carry, kv):
                aa, bb, pp = carry
                kk, vv = kv
                ww = u + kk
                qq = jnp.maximum(pp, ww)
                e1 = jnp.exp(pp - qq)
                e2 = jnp.exp(ww - qq)
                out = (e1 * aa + e2 * vv) / (e1 * bb + e2)
                ww2 = pp + w
                qq2 = jnp.maximum(ww2, kk)
                e1b = jnp.exp(ww2 - qq2)
                e2b = jnp.exp(kk - qq2)
                return ((e1b * aa + e2b * vv, e1b * bb + e2b, qq2), out)
            _, out = lax.scan(step, init, (kt, vt))
            return jnp.swapaxes(out, 0, 1)
        x = layernorm(x, ln0_w, ln0_b)
        for l in range(L):
            h = layernorm(x, ln1_w[l], ln1_b[l])
            hh = time_shift(h)
            xk = h * tmk[l] + hh * (1 - tmk[l])
            xv = h * tmv[l] + hh * (1 - tmv[l])
            xr = h * tmr[l] + hh * (1 - tmr[l])
            k = jnp.einsum('btc,oc->bto', xk, Wk[l])
            v = jnp.einsum('btc,oc->bto', xv, Wv[l])
            sr = jax.nn.sigmoid(jnp.einsum('btc,oc->bto', xr, Wr[l]))
            rwkv = sr * wkv(time_decay[l], time_first[l], k, v)
            x = x + jnp.einsum('bto,co->btc', rwkv, Wo[l])
            h = layernorm(x, ln2_w[l], ln2_b[l])
            hh = time_shift(h)
            xk = h * cmk[l] + hh * (1 - cmk[l])
            xr = h * cmr[l] + hh * (1 - cmr[l])
            kf = jnp.einsum('btc,fc->btf', xk, Wck[l])
            kf = jnp.square(jax.nn.relu(kf))
            kv = jnp.einsum('btf,cf->btc', kf, Wcv[l])
            x = x + jax.nn.sigmoid(jnp.einsum('btc,oc->bto', xr, Wcr[l])) * kv
        return x

    def _L0_xattn_ref(x, y, Wq, bq, Wk, bk, Wv, bv, Wp, bp):
        import jax, jax.numpy as jnp
        import numpy as np
        B, T, C, H = (4, 1024, 256, 16)
        D = C // H

        def _heads(t):
            b, n, c = t.shape
            return t.reshape(b, n, H, D).transpose(0, 2, 1, 3)
        q = jax.nn.softmax(_heads(x @ Wq.T + bq), axis=-1)
        k = jax.nn.softmax(_heads(y @ Wk.T + bk), axis=-1)
        v = _heads(y @ Wv.T + bv)
        k_cumsum = jnp.sum(k, axis=-2, keepdims=True)
        D_inv = 1.0 / jnp.sum(q * k_cumsum, axis=-1, keepdims=True)
        kv = jnp.einsum('bhnd,bhne->bhde', k, v)
        out = q + jnp.einsum('bhnd,bhde->bhne', q, kv) * D_inv
        out = out.transpose(0, 2, 1, 3).reshape(x.shape[0], x.shape[1], C)
        return out @ Wp.T + bp

    def _L0_ffn_ref(hidden_states, w_router, w_gating, w_gate, w_up, w_down):
        import jax, jax.numpy as jnp
        import numpy as np
        B, S, H = (2, 256, 256)
        E, F = (8, 1024)
        GATE_TEMP = 0.1
        x = hidden_states
        router_probs = jax.nn.softmax(jnp.einsum('bsh,he->bse', x, w_router), axis=-1)
        gate_weights = jax.nn.softmax(jnp.einsum('bsh,he->bse', x, w_gating) / GATE_TEMP, axis=-1)
        g = jnp.einsum('bsh,ehf->ebsf', x, w_gate)
        u = jnp.einsum('bsh,ehf->ebsf', x, w_up)
        h = jax.nn.silu(g) * u
        expert_out = jnp.einsum('ebsf,efh->ebsh', h, w_down)
        cw = router_probs * gate_weights
        cw = cw / (jnp.sum(cw, axis=-1, keepdims=True) + 1e-09)
        out = jnp.einsum('ebsh,bse->bsh', expert_out, cw)
        return out
    x = _layernorm(x + _L0_attn_ref(x, L0_attn_ln0_w, L0_attn_ln0_b, L0_attn_ln1_w, L0_attn_ln1_b, L0_attn_ln2_w, L0_attn_ln2_b, L0_attn_time_decay, L0_attn_time_first, L0_attn_tmk, L0_attn_tmv, L0_attn_tmr, L0_attn_Wk, L0_attn_Wv, L0_attn_Wr, L0_attn_Wo, L0_attn_cmk, L0_attn_cmr, L0_attn_Wck, L0_attn_Wcv, L0_attn_Wcr), axis=-1)
    x = _layernorm(x + _L0_xattn_ref(x, ctx_1024, L0_xattn_Wq, L0_xattn_bq, L0_xattn_Wk, L0_xattn_bk, L0_xattn_Wv, L0_xattn_bv, L0_xattn_Wp, L0_xattn_bp), axis=-1)
    x = _layernorm(x + _L0_ffn_ref(x, L0_ffn_w_router, L0_ffn_w_gating, L0_ffn_w_gate, L0_ffn_w_up, L0_ffn_w_down), axis=-1)
    return x

_drawn_inputs = setup_inputs


def setup_inputs(seed=0):
    import zlib

    import numpy as np

    out = dict(_drawn_inputs(seed))
    spreads = {'L0_attn_ln0_w': (1.0, 0.2),
     'L0_attn_ln0_b': (0.0, 0.1),
     'L0_attn_ln1_w': (1.0, 0.6),
     'L0_attn_ln1_b': (0.0, 0.8),
     'L0_attn_ln2_w': (1.0, 0.6),
     'L0_attn_ln2_b': (0.0, 0.8),
     'L0_xattn_bq': (0.0, 0.613),
     'L0_xattn_bk': (0.0, 0.8),
     'L0_xattn_bv': (0.0, 0.1),
     'L0_xattn_bp': (0.0, 0.1)}
    factors = {'L0_attn_time_decay': 5.882,
     'L0_attn_time_first': 8.0,
     'L0_attn_tmk': 8.0,
     'L0_attn_tmv': 4.44,
     'L0_attn_tmr': 8.0,
     'L0_attn_Wk': 8.0,
     'L0_attn_Wr': 8.0,
     'L0_attn_cmr': 8.0,
     'L0_attn_Wcr': 8.0}
    for name, (base, spread) in spreads.items():
        noise = np.random.default_rng([zlib.crc32(name.encode()), seed]).standard_normal(out[name].shape)
        drawn = base * np.exp(spread * noise) if base else spread * noise
        out[name] = jnp.asarray(drawn.astype(out[name].dtype))
    for name, factor in factors.items():
        out[name] = (out[name] * factor).astype(out[name].dtype)
    return out
```

```python
from contextlib import ExitStack

import concourse.bass as bass
from concourse import mybir
from concourse.alu_op_type import AluOpType as ALU

FP32 = mybir.dt.float32
F32R = mybir.dt.float32r
ACT = mybir.ActivationFunctionType
AX = mybir.AxisListType

P = 128
B, T, C = 16, 112, 256
L, F = 4, 1024
CB = C // P
G = 4
GROUPS = B // G
STEPS = L * GROUPS
T1 = T + 1
EPS = 1e-5
NEVER = -1e38
SAT = 38.0
NAMES = ["ln1w", "ln1b", "tmk", "tmv", "tmr", "td", "u", "ln2w", "ln2b", "cmk", "cmr", "w"]
PRM = {n: i for i, n in enumerate(NAMES)}
NPRM = len(NAMES)
S = 375
STILES = 3
ST = S // STILES
CG = 4
H, D = 16, 16
E = 8
FB = F // P // 2
WH = 2 * CB * FB * P + FB * C
GATE_TEMP = 0.1

def rwkv_phase(nc, g, io):
    ctx = ExitStack()
    with ctx:
        def sb(name, shape, dt=FP32):
            return ctx.enter_context(nc.sbuf_tensor(name, shape, dt))

        def sem(name):
            return ctx.enter_context(nc.semaphore(name))

        x = g["x"]
        ident = g["ident"]
        wk, wv, wr, wo, wcr = (sb(n, [P, CB, C]) for n in ("wk", "wv", "wr", "wo", "wcr"))
        wck = sb("wck", [P, CB, F])
        wcv = sb("wcv", [P, F // P, C])
        prm = sb("prm", [P, L, CB, NPRM])
        ln0w, ln0b = sb("ln0w", [T, C]), sb("ln0b", [T, C])
        eps, sat = sb("eps", [P, 1]), sb("sat", [P, 1])
        xn = {1: sb("xn1", [T, G, C]), 2: sb("xn2", [T, G, C])}
        st = {k: sb(f"st{k}", [T, G, 6]) for k in (0, 1, 2)}
        mv = {k: sb(f"mv{k}", [T, G, 2]) for k in (0, 1, 2)}
        lnv = {k: sb(f"lnv{k}", [T, G]) for k in (0, 1, 2)}
        y0 = {k: sb(f"y0{k}", [T, G]) for k in (0, 1, 2)}
        yy = {k: sb(f"yy{k}", [T, G]) for k in (0, 1, 2)}
        rstd = {k: sb(f"rstd{k}", [T, G]) for k in (0, 1, 2)}
        h = {1: sb("h1", [P, CB, G, T1]), 2: sb("h2", [P, CB, G, T1])}
        diff = {1: sb("diff1", [P, CB, G, T]), 2: sb("diff2", [P, CB, G, T])}
        mixed = {n: sb("mix_" + n, [P, CB, G, T]) for n in ("k", "v", "r", "ck", "cr")}
        kp = sb("kp", [P, CB, G, T1])
        v = sb("v", [P, CB, G, T])
        rs = sb("rs", [P, CB, G, T])
        er = sb("er", [P, CB, G, T])
        pp = sb("pp", [P, CB, G, T1])
        reset = sb("reset", [P, G, T1])
        decay = sb("decay", [P, CB, G, T1])
        a1, a2 = sb("a1", [P, CB, G, T]), sb("a2", [P, CB, G, T])
        a3, a4 = sb("a3", [P, CB, G, T]), sb("a4", [P, CB, G, T])
        e1b, e2b = sb("e1b", [P, CB, G, T1]), sb("e2b", [P, CB, G, T1])
        ev = sb("ev", [P, CB, G, T1])
        aa, bb = sb("aa", [P, CB, G, T1]), sb("bb", [P, CB, G, T1])
        e1, e2 = sb("e1", [P, CB, G, T]), sb("e2", [P, CB, G, T])
        rw = sb("rw", [P, CB, G, T])
        relu = sb("relu", [P, 2, G * T])
        kf = sb("kf", [P, F // P, G * T])
        crs, cer, cs, clog, crec, cq = (sb(n, [T, 2, 2, C]) for n in ("crs", "cer", "cs", "clog", "crec", "cq"))

        bank = [ctx.enter_context(nc.psum_tensor(f"bank{i}", [P, 512], FP32)) for i in range(8)]

        params_in = sem("params_in")
        x_in = [sem(f"x_in{c}") for c in range(GROUPS)]
        wexp_done, w_ready = sem("wexp_done"), sem("w_ready")
        w_in = {n: sem("w_in_" + n) for n in ("k", "v", "r", "o", "ck", "cr", "cv")}
        const_set = sem("const_set")
        lnstat = {k: sem(f"lnstat{k}") for k in (0, 1, 2)}
        lnlog = {k: sem(f"lnlog{k}") for k in (0, 1, 2)}
        lny0 = {k: sem(f"lny0{k}") for k in (0, 1, 2)}
        xn_ready = {k: sem(f"xn_ready{k}") for k in (1, 2)}
        turned = {k: sem(f"turned{k}") for k in (1, 2)}
        h_ready = {k: sem(f"h_ready{k}") for k in (1, 2)}
        mix1_ready, mix2_ready = sem("mix1_ready"), sem("mix2_ready")
        kvr_done, kvr_out = sem("kvr_done"), sem("kvr_out")
        rs_done = sem("rs_done")
        arg_ready, exp_ready = sem("arg_ready"), sem("exp_ready")
        den_ready, denlog, rec_ready = sem("den_ready"), sem("denlog"), sem("rec_ready")
        wkv_ready = sem("wkv_ready")
        wo_done = sem("wo_done")
        ck_done, relu_done, kf_ready = sem("ck_done"), sem("relu_done"), sem("kf_ready")
        cr_done, crs_done, cer_ready = sem("cr_done"), sem("crs_done"), sem("cer_ready")
        cs_ready, clog_done, crec_ready = sem("cs_ready"), sem("clog_done"), sem("crec_ready")
        cv_done, x_done = sem("cv_done"), sem("x_done")
        dve_step = sem("dve_step")

        def valid(m):
            return 0 <= m < STEPS

        block = ctx.enter_context(nc.Block())

        @block.gpsimd
        def _(pool):
            for t in (h[1], h[2], e1b, e2b, ev):
                pool.memset(t[:, :, :, 0:1], 0.0).then_inc(const_set, 1)
            pool.memset(kp[:, :, :, 0:1], NEVER).then_inc(const_set, 1)
            pool.memset(eps[:], EPS).then_inc(const_set, 1)
            pool.memset(sat[:], SAT).then_inc(const_set, 1)
            pool.memset(reset[:], 0.0).then_inc(const_set, 1)
            pool.memset(ident[:], 0.0).then_inc(const_set, 1)
            pool.wait_ge(const_set, 10)
            pool.memset(reset[:, :, 0:1], 2 * NEVER).then_inc(const_set, 1)
            pool.affine_select(out=ident[:], in_=ident[:], compare_op=ALU.not_equal, fill=1.0, base=0,
                               pattern=[[-1, P]], channel_multiplier=1).then_inc(const_set, 1)

        @block.sync
        def _(sp):
            xv = io["x"].rearrange("b t c -> t b c")
            for c in range(GROUPS):
                sp.dma_start(x[:, c * G:(c + 1) * G, :], xv[:, c * G:(c + 1) * G, :]).then_inc(x_in[c], 16)
                if c == 0:
                    sp.dma_start(ln0w[:], io["ln0_w"].partition_broadcast(T)).then_inc(params_in, 16)
                    sp.dma_start(ln0b[:], io["ln0_b"].partition_broadcast(T)).then_inc(params_in, 16)
                    sp.dma_start(prm[:, :, :, 0:NPRM - 1], io["prm"]).then_inc(params_in, 16)
            uses = (("k", wk, kvr_done, 6), ("v", wv, kvr_done, 6), ("r", wr, kvr_done, 6), ("o", wo, wo_done, 2),
                    ("ck", wck, ck_done, 8), ("cr", wcr, cr_done, 2), ("cv", wcv, cv_done, 2))
            for l in range(STEPS // GROUPS):
                for n, tile, used, per in uses:
                    if l:
                        sp.wait_ge(used, per * GROUPS * l)
                    sp.dma_start(tile[:], io["w_" + n][l]).then_inc(w_in[n], 16)

        @block.vector
        def _(dve):
            steps = [0]

            def did(ins):
                ins.then_inc(dve_step, 1)
                steps[0] += 1
                return steps[0]

            def after(n):
                dve.wait_ge(dve_step, n)

            def chunk(m):
                c = m % GROUPS
                return x[:, c * G:(c + 1) * G, :]

            def param(m, b, name):
                return prm[:, m // GROUPS, b, PRM[name]:PRM[name] + 1]

            def stats(k, xc):
                for i in range(G):
                    n = did(dve.bn_stats(st[k][:, i, :], xc[:, i, :]))
                after(n)
                for i in range(G):
                    last = dve.bn_aggr(mv[k][:, i, :], st[k][:, i, :])
                    if i < G - 1:
                        did(last)
                last.then_inc(lnstat[k], 1)

            def finish(k, m, out, xc, done=None):
                dve.wait_ge(lny0[k], m + 1)
                n = did(dve.tensor_tensor(yy[k][:], y0[k][:], y0[k][:], ALU.mult))
                after(n)
                n = did(dve.scalar_tensor_tensor(yy[k][:], mv[k][:, :, 1], EPS, yy[k][:], ALU.add, ALU.mult))
                after(n)
                n = did(dve.tensor_scalar(yy[k][:], yy[k][:], -0.5, 1.5, ALU.mult, ALU.add))
                after(n)
                n = did(dve.tensor_tensor(rstd[k][:], yy[k][:], y0[k][:], ALU.mult))
                after(n)
                for i in range(G):
                    last = dve.tensor_scalar(out[:, i, :], xc[:, i, :], mv[k][:, i, 0:1], rstd[k][:, i:i + 1],
                                             ALU.subtract, ALU.mult)
                    if i < G - 1 or done is None:
                        n = did(last)
                if done is not None:
                    last.then_inc(done, 1)
                return n

            def first_norm(m):
                xc = chunk(m)
                dve.wait_ge(x_in[m], 16)
                stats(0, xc)
                after(finish(0, m, xc, xc))
                dve.wait_ge(params_in, 48)
                n = did(dve.tensor_tensor(xc, xc, ln0w[:].unsqueeze(1).broadcast_to([T, G, C]), ALU.mult))
                after(n)
                after(did(dve.tensor_tensor(xc, xc, ln0b[:].unsqueeze(1).broadcast_to([T, G, C]), ALU.add)))

            def mix(k, m, names, params, done):
                n = 0
                for b in range(CB):
                    dve.wait_ge(h_ready[k], CB * m + b + 1)
                    n = did(dve.tensor_tensor(diff[k][:, b], h[k][:, b, :, 1:T1], h[k][:, b, :, 0:T], ALU.subtract))
                for name, mu in zip(names, params):
                    for b in range(CB):
                        if name == names[0]:
                            after(n - CB + 1 + b)
                        dve.scalar_tensor_tensor(mixed[name][:, b], diff[k][:, b], param(m, b, mu),
                                                 h[k][:, b, :, 0:T], ALU.mult, ALU.add).then_inc(done, 1)

            def wkv(m):
                flat = "p g t -> p (g t)"
                n = [0] * CB
                if m % GROUPS == 0:
                    for b in range(CB):
                        n[b] = did(dve.tensor_scalar(decay[:, b], reset[:], param(m, b, "w"), None, ALU.add))
                for b in range(CB):
                    if n[b]:
                        after(n[b])
                    dve.wait_ge(kvr_out, 6 * m + b + 1)
                    n[b] = did(dve.tensor_tensor_scan(pp[:, b].rearrange(flat), decay[:, b].rearrange(flat),
                                                      kp[:, b].rearrange(flat), 0.0, ALU.add, ALU.max))
                for b in range(CB):
                    after(n[b])
                    dve.tensor_tensor(a1[:, b], pp[:, b, :, 0:T], pp[:, b, :, 1:T1], ALU.subtract).then_inc(arg_ready, 1)
                for b in range(CB):
                    dve.tensor_tensor(a2[:, b], kp[:, b, :, 1:T1], pp[:, b, :, 1:T1], ALU.subtract).then_inc(arg_ready, 1)
                for b in range(CB):
                    n[b] = did(dve.scalar_tensor_tensor(aa[:, b, :, 0:T], kp[:, b, :, 1:T1], param(m, b, "u"),
                                                        pp[:, b, :, 0:T], ALU.add, ALU.subtract))
                for b in range(CB):
                    after(n[b])
                    dve.tensor_scalar(a3[:, b], aa[:, b, :, 0:T], 0.0, None, ALU.max).then_inc(arg_ready, 1)
                for b in range(CB):
                    dve.tensor_scalar(a4[:, b], aa[:, b, :, 0:T], 0.0, None, ALU.min).then_inc(arg_ready, 1)
                sb_, sv = [0] * CB, [0] * CB
                for b in range(CB):
                    dve.wait_ge(exp_ready, 8 * m + CB + b + 1)
                    sb_[b] = did(dve.tensor_tensor_scan(bb[:, b].rearrange(flat), e1b[:, b].rearrange(flat),
                                                        e2b[:, b].rearrange(flat), 0.0, ALU.mult, ALU.add))
                for b in range(CB):
                    dve.wait_ge(kvr_out, 6 * m + CB + b + 1)
                    sv[b] = did(dve.tensor_tensor(ev[:, b, :, 1:T1], e2b[:, b, :, 1:T1], v[:, b], ALU.mult))
                for b in range(CB):
                    after(sv[b])
                    n[b] = did(dve.tensor_tensor_scan(aa[:, b].rearrange(flat), e1b[:, b].rearrange(flat),
                                                      ev[:, b].rearrange(flat), 0.0, ALU.mult, ALU.add))
                q = [0] * CB
                for b in range(CB):
                    dve.wait_ge(exp_ready, 8 * m + 3 * CB + b + 1)
                    q[b] = did(dve.tensor_tensor(a1[:, b], e1[:, b], bb[:, b, :, 0:T], ALU.mult))
                for b in range(CB):
                    after(q[b])
                    q[b] = did(dve.tensor_tensor(a1[:, b], a1[:, b], e2[:, b], ALU.add))
                s = [0] * CB
                for b in range(CB):
                    dve.wait_ge(kvr_out, 6 * m + 2 * CB + b + 1)
                    s[b] = did(dve.tensor_scalar(a4[:, b], er[:, b], 1.0, None, ALU.add))
                for b in range(CB):
                    after(s[b])
                    dve.tensor_tensor(a2[:, b], a1[:, b], a4[:, b], ALU.mult).then_inc(den_ready, 1)
                for b in range(CB):
                    n[b] = did(dve.tensor_tensor(a3[:, b], e1[:, b], aa[:, b, :, 0:T], ALU.mult))
                for b in range(CB):
                    dve.wait_ge(den_ready, CB * m + b + 1)
                    q[b] = did(dve.tensor_tensor(a1[:, b], e2[:, b], v[:, b], ALU.mult))
                for b in range(CB):
                    after(q[b])
                    n[b] = did(dve.tensor_tensor(a3[:, b], a3[:, b], a1[:, b], ALU.add))
                for b in range(CB):
                    dve.wait_ge(rec_ready, CB * m + b + 1)
                    q[b] = did(dve.tensor_tensor(a4[:, b], a2[:, b], er[:, b], ALU.mult))
                for b in range(CB):
                    after(q[b])
                    q[b] = did(dve.scalar_tensor_tensor(a4[:, b], a4[:, b], 2.0, er[:, b], ALU.subtract, ALU.mult))
                for b in range(CB):
                    after(q[b])
                    dve.scalar_tensor_tensor(rw[:, b], a3[:, b], -1.0, a4[:, b], ALU.mult, ALU.mult).then_inc(wkv_ready, 1)

            def add_wkv(m):
                xc = chunk(m)
                for i in range(2):
                    dve.wait_ge(wo_done, 2 * m + i + 1)
                    n = did(dve.tensor_tensor(xc[:, 2 * i:2 * i + 2, :], xc[:, 2 * i:2 * i + 2, :],
                                              bank[i][0:T, :].rearrange("p (g c) -> p g c", c=C), ALU.add))
                return n

            def channel_gate(m):
                for i in range(2):
                    dve.wait_ge(cer_ready, 2 * m + i + 1)
                    dve.tensor_scalar(cs[:, i], cer[:, i], 1.0, None, ALU.add).then_inc(cs_ready, 1)

            def add_channel(m):
                xc = chunk(m)
                q = [0, 0]
                for i in range(2):
                    dve.wait_ge(crec_ready, 2 * m + i + 1)
                    q[i] = did(dve.tensor_tensor(cq[:, i], cs[:, i], crec[:, i], ALU.mult))
                for i in range(2):
                    after(q[i])
                    q[i] = did(dve.scalar_tensor_tensor(cq[:, i], cq[:, i], 2.0, crec[:, i], ALU.subtract, ALU.mult))
                for i in range(2):
                    after(q[i])
                    dve.wait_ge(cv_done, 2 * m + i + 1)
                    q[i] = did(dve.scalar_tensor_tensor(cq[:, i], bank[6 + i][0:T, :].rearrange("p (g c) -> p g c", c=C),
                                                        -1.0, cq[:, i], ALU.mult, ALU.mult))
                for i in range(2):
                    after(q[i])
                    dve.tensor_tensor(xc[:, 2 * i:2 * i + 2, :], xc[:, 2 * i:2 * i + 2, :], cq[:, i],
                                      ALU.add).then_inc(x_done, 1)

            dve.wait_ge(const_set, 12)
            dve.wait_ge(wexp_done, 1)
            pw = PRM["w"]
            dve.tensor_scalar(prm[:, :, :, pw:pw + 1], prm[:, :, :, pw:pw + 1], -1.0, None, ALU.mult).then_inc(w_ready, 1)
            dve.wait_ge(w_ready, 1)
            for s in range(-2, STEPS + 1):
                if valid(s - 1):
                    add_channel(s - 1)
                if valid(s):
                    after(add_wkv(s))
                    stats(2, chunk(s))
                if valid(s + 2):
                    if s + 2 < GROUPS:
                        first_norm(s + 2)
                    else:
                        dve.wait_ge(x_done, 2 * (s + 2 - GROUPS + 1))
                    stats(1, chunk(s + 2))
                if valid(s):
                    finish(2, s, xn[2], chunk(s), xn_ready[2])
                if valid(s + 2):
                    finish(1, s + 2, xn[1], chunk(s + 2), xn_ready[1])
                if valid(s):
                    mix(2, s, ("ck", "cr"), ("cmk", "cmr"), mix2_ready)
                if valid(s + 1):
                    wkv(s + 1)
                if valid(s):
                    channel_gate(s)
                if valid(s + 2):
                    mix(1, s + 2, ("k", "v", "r"), ("tmk", "tmv", "tmr"), mix1_ready)

        @block.scalar
        def _(act):
            def param(m, b, name):
                return prm[:, m // GROUPS, b, PRM[name]:PRM[name] + 1]

            def padded(t):
                return t.rearrange("p (g t) -> p g t", t=T)

            def rsqrt0(k, m):
                act.wait_ge(lnstat[k], m + 1)
                act.activation(lnv[k][:], mv[k][:, :, 1], ACT.Ln, bias=eps[0:T, :]).then_inc(lnlog[k], 1)
                act.wait_ge(lnlog[k], m + 1)
                act.activation(y0[k][:], lnv[k][:], ACT.Exp, scale=-0.5).then_inc(lny0[k], 1)

            def norm_out(k, m, first_bank, w, b_):
                for b in range(CB):
                    act.wait_ge(turned[k], CB * m + b + 1)
                    act.activation(h[k][:, b, :, 1:T1], padded(bank[first_bank + b][:, 0:G * T]), ACT.Identity,
                                   bias=param(m, b, b_), scale=param(m, b, w)).then_inc(h_ready[k], 1)

            def kv_out(m, which):
                for b in range(CB):
                    act.wait_ge(kvr_done, 6 * m + CB * which + b + 1)
                    dst = kp[:, b, :, 1:T1] if which == 0 else v[:, b]
                    act.activation(dst, padded(bank[2 + CB * which + b][:, 0:G * T]), ACT.Copy).then_inc(kvr_out, 1)

            def r_out(m):
                for b in range(CB):
                    act.wait_ge(kvr_done, 6 * m + 2 * CB + b + 1)
                    act.activation(rs[:, b], padded(bank[6 + b][:, 0:G * T]), ACT.Relu, bias=sat[:]).then_inc(rs_done, 1)
                for b in range(CB):
                    act.wait_ge(rs_done, CB * m + b + 1)
                    act.activation(er[:, b], rs[:, b], ACT.Exp, bias=sat[:], scale=-1.0).then_inc(kvr_out, 1)

            def square(m, j):
                act.wait_ge(relu_done, 8 * m + j + 1)
                act.activation(kf[:, j, :], relu[:, j % 2, :], ACT.Square).then_inc(kf_ready, 1)

            def relu_of(m, j):
                act.wait_ge(ck_done, 8 * m + j + 1)
                act.activation(relu[:, j % 2, :], bank[(2 + j) % 8][:, 0:G * T], ACT.Relu).then_inc(relu_done, 1)

            def kf_out(m, j0, j1):
                for j in range(j0, j1):
                    relu_of(m, j)
                    square(m, j)

            def wkv_exp(m, what):
                for b in range(CB):
                    act.wait_ge(arg_ready, 8 * m + CB * what + b + 1)
                    if what == 0:
                        ins = act.activation(e1b[:, b, :, 1:T1], a1[:, b], ACT.Exp, bias=param(m, b, "w"))
                    elif what == 1:
                        ins = act.activation(e2b[:, b, :, 1:T1], a2[:, b], ACT.Exp)
                    elif what == 2:
                        ins = act.activation(e1[:, b], a3[:, b], ACT.Exp, scale=-1.0)
                    else:
                        ins = act.activation(e2[:, b], a4[:, b], ACT.Exp)
                    ins.then_inc(exp_ready, 1)

            def reciprocal0(m):
                for b in range(CB):
                    act.wait_ge(den_ready, CB * m + b + 1)
                    act.activation(rs[:, b], a2[:, b], ACT.Ln).then_inc(denlog, 1)
                for b in range(CB):
                    act.wait_ge(denlog, CB * m + b + 1)
                    act.activation(er[:, b], rs[:, b], ACT.Exp, scale=-1.0).then_inc(rec_ready, 1)

            def gate_exp(m):
                for i in range(2):
                    act.wait_ge(cr_done, 2 * m + i + 1)
                    act.activation(crs[:, i], bank[4 + i][0:T, :].rearrange("p (g c) -> p g c", c=C), ACT.Relu,
                                   bias=sat[0:T, :]).then_inc(crs_done, 1)
                for i in range(2):
                    act.wait_ge(crs_done, 2 * m + i + 1)
                    act.activation(cer[:, i], crs[:, i], ACT.Exp, bias=sat[0:T, :], scale=-1.0).then_inc(cer_ready, 1)

            def gate_reciprocal0(m):
                for i in range(2):
                    act.wait_ge(cs_ready, 2 * m + i + 1)
                    act.activation(clog[:, i], cs[:, i], ACT.Ln).then_inc(clog_done, 1)
                for i in range(2):
                    act.wait_ge(clog_done, 2 * m + i + 1)
                    act.activation(crec[:, i], clog[:, i], ACT.Exp, scale=-1.0).then_inc(crec_ready, 1)

            act.preload_act_table_set("natural_log_exp_and_others")
            act.wait_ge(const_set, 12)
            act.wait_ge(params_in, 48)
            act.activation(prm[:, :, :, PRM["w"]:PRM["w"] + 1], prm[:, :, :, PRM["td"]:PRM["td"] + 1],
                           ACT.Exp).then_inc(wexp_done, 1)
            act.wait_ge(w_ready, 1)
            for s in range(-2, STEPS + 1):
                if valid(s + 1):
                    kv_out(s + 1, 0)
                if valid(s):
                    rsqrt0(2, s)
                if valid(s + 2):
                    if s + 2 < GROUPS:
                        rsqrt0(0, s + 2)
                    rsqrt0(1, s + 2)
                if valid(s + 1):
                    kv_out(s + 1, 1)
                    r_out(s + 1)
                if valid(s):
                    norm_out(2, s, 0, "ln2w", "ln2b")
                    kf_out(s, 0, 2)
                if valid(s + 1):
                    wkv_exp(s + 1, 0)
                    wkv_exp(s + 1, 1)
                if valid(s):
                    kf_out(s, 2, 4)
                if valid(s + 1):
                    wkv_exp(s + 1, 2)
                    wkv_exp(s + 1, 3)
                if valid(s):
                    kf_out(s, 4, 8)
                if valid(s + 2):
                    norm_out(1, s + 2, 2, "ln1w", "ln1b")
                if valid(s + 1):
                    reciprocal0(s + 1)
                if valid(s):
                    gate_exp(s)
                    gate_reciprocal0(s)

        @block.tensor
        def _(pe):
            pe.wait_ge(const_set, 12)

            def turn(k, m, first_bank):
                pe.wait_ge(xn_ready[k], m + 1)
                for b in range(CB):
                    for i in range(G):
                        ins = pe.transpose(bank[first_bank + b][:, i * T:(i + 1) * T], xn[k][:, i, b * P:(b + 1) * P],
                                           ident[0:T, 0:T])
                    ins.then_inc(turned[k], 1)

            def project(m, which, w, src, name):
                l = m // GROUPS
                pe.wait_ge(w_in[name], 16 * (l + 1))
                for o in range(CB):
                    for b in range(CB):
                        if o == 0:
                            pe.wait_ge(mix1_ready, 6 * m + CB * which + b + 1)
                        ins = pe.matmul(bank[2 + CB * which + o][:, 0:G * T], w[:, b, o * P:(o + 1) * P],
                                        src[:, b].rearrange("p g t -> p (g t)"), start=b == 0, stop=b == CB - 1)
                    ins.then_inc(kvr_done, 1)

            for s in range(-2, STEPS + 1):
                m = s
                if valid(m):
                    pe.wait_ge(w_in["o"], 16 * (m // GROUPS + 1))
                    for i in range(G):
                        for b in range(CB):
                            if i == 0:
                                pe.wait_ge(wkv_ready, CB * m + b + 1)
                            ins = pe.matmul(bank[i // 2][0:T, (i % 2) * C:(i % 2 + 1) * C], rw[:, b, i, :], wo[:, b, :],
                                            start=b == 0, stop=b == CB - 1)
                        if i % 2:
                            ins.then_inc(wo_done, 1)
                m = s + 1
                if valid(m):
                    project(m, 0, wk, mixed["k"], "k")
                    if m >= 2:
                        pe.wait_ge(crs_done, 2 * (m - 1))
                    project(m, 1, wv, mixed["v"], "v")
                    if m >= 2:
                        pe.wait_ge(x_done, 2 * (m - 1))
                    project(m, 2, wr, mixed["r"], "r")
                m = s
                if valid(m):
                    turn(2, m, 0)
                    pe.wait_ge(w_in["ck"], 16 * (m // GROUPS + 1))
                    for j in range(F // P):
                        if j < 6 and valid(m + 1):
                            if j < 4:
                                pe.wait_ge(kvr_out, 6 * (m + 1) + j + 1)
                            else:
                                pe.wait_ge(rs_done, CB * (m + 1) + j - 3)
                        elif j < 6 and j >= 4 and m >= 1:
                            pe.wait_ge(x_done, 2 * m)
                        elif j in (2, 3) and m >= 1:
                            pe.wait_ge(crs_done, 2 * m)
                        for b in range(CB):
                            if j == 0:
                                pe.wait_ge(mix2_ready, 4 * m + b + 1)
                            ins = pe.matmul(bank[(2 + j) % 8][:, 0:G * T], wck[:, b, j * P:(j + 1) * P],
                                            mixed["ck"][:, b].rearrange("p g t -> p (g t)"), start=b == 0,
                                            stop=b == CB - 1)
                        ins.then_inc(ck_done, 1)
                m = s + 2
                if valid(m):
                    if valid(s):
                        pe.wait_ge(kf_ready, 8 * s + 2)
                    turn(1, m, 2)
                m = s
                if valid(m):
                    pe.wait_ge(w_in["cr"], 16 * (m // GROUPS + 1))
                    pe.wait_ge(kf_ready, 8 * m + 4)
                    for i in range(G):
                        for b in range(CB):
                            if i == 0:
                                pe.wait_ge(mix2_ready, 4 * m + CB + b + 1)
                            ins = pe.matmul(bank[4 + i // 2][0:T, (i % 2) * C:(i % 2 + 1) * C], mixed["cr"][:, b, i, :],
                                            wcr[:, b, :], start=b == 0, stop=b == CB - 1)
                        if i % 2:
                            ins.then_inc(cr_done, 1)
                    pe.wait_ge(w_in["cv"], 16 * (m // GROUPS + 1))
                    pe.wait_ge(kf_ready, 8 * m + 6)
                    for i in range(G):
                        for j in range(F // P):
                            if i == 0 and j >= 6:
                                pe.wait_ge(kf_ready, 8 * m + j + 1)
                            ins = pe.matmul(bank[6 + i // 2][0:T, (i % 2) * C:(i % 2 + 1) * C],
                                            kf[:, j, i * T:(i + 1) * T], wcv[:, j, :], start=j == 0, stop=j == F // P - 1)
                        if i % 2:
                            ins.then_inc(cv_done, 1)

def context_phase(nc, g, io):
    ctx = ExitStack()
    with ctx:
        def sb(name, shape, dt=FP32):
            return ctx.enter_context(nc.sbuf_tensor(name, shape, dt))

        def sem(name):
            return ctx.enter_context(nc.semaphore(name))

        kvbd, kcbd = g["kvbd"], g["kcbd"]
        wkv = sb("wkv", [P, CB, 2 * C])
        bk = sb("bk", [ST, C])
        bv = sb("bv", [P, C])
        mask = sb("mask", [P, P])
        bvm = sb("bvm", [P, CB, P])
        ct = [sb(f"ct{i}", [P, CB, CG * S]) for i in range(2)]
        k = [sb(f"k{i}", [ST, STILES, C]) for i in range(2)]
        v = [sb(f"v{i}", [ST, STILES, CB, P + 1]) for i in range(2)]
        top, total, rec = (sb(n, [ST, STILES * H]) for n in ("top", "total", "rec"))
        kc = sb("kc", [P, CB])
        kvm = sb("kvm", [P, CB, P])
        proj = [ctx.enter_context(nc.psum_tensor(f"proj{i}", [P, STILES, 512], FP32)) for i in range(2)]
        kvp = [ctx.enter_context(nc.psum_tensor(f"kvp{i}", [P, 512], FP32)) for i in range(2)]

        w_in, b_in = sem("w_in"), sem("b_in")
        ct_in = [sem(f"ct_in{i}") for i in range(2)]
        const_set, mask_set, bvm_ready = sem("const_set"), sem("mask_set"), sem("bvm_ready")
        proj_done, kv_done = sem("proj_done"), sem("kv_done")
        v_ready, arg_ready, exp_ready, k_ready = sem("v_ready"), sem("arg_ready"), sem("exp_ready"), sem("k_ready")
        kbias_done = sem("kbias_done")
        kc_ready, bd_ready = sem("kc_ready"), sem("bd_ready")
        dve_step = sem("dve_step")

        block = ctx.enter_context(nc.Block())

        @block.gpsimd
        def _(pool):
            pool.memset(mask[:], 1.0).then_inc(mask_set, 1)
            for i in range(2):
                pool.memset(v[i][:, :, :, P:P + 1], 1.0).then_inc(const_set, 1)
            m = mask[:].rearrange("p (a b) -> p a b", b=D)
            pool.wait_ge(mask_set, 1)
            pool.affine_select(out=m, in_=m, compare_op=ALU.is_ge, fill=0.0, base=0, pattern=[[-D, P // D], [0, D]],
                               channel_multiplier=1).then_inc(mask_set, 1)
            pool.wait_ge(mask_set, 2)
            pool.affine_select(out=m, in_=m, compare_op=ALU.is_ge, fill=0.0, base=D - 1,
                               pattern=[[D, P // D], [0, D]], channel_multiplier=-1).then_inc(mask_set, 1)

        @block.sync
        def _(sp):
            sp.dma_start(wkv[:], io["wkv"]).then_inc(w_in, 16)
            for j in range(B // CG):
                if j >= 2:
                    sp.wait_ge(proj_done, CG * (j - 1))
                sp.dma_start(ct[j % 2][:], io["ctx_t"][:, :, j * CG * S:(j + 1) * CG * S]).then_inc(ct_in[j % 2], 16)
                if j == 0:
                    sp.dma_start(bk[:], io["bk"].partition_broadcast(ST)).then_inc(b_in, 16)
                    sp.dma_start(bv[:], io["bv"].partition_broadcast(P)).then_inc(b_in, 16)

        @block.vector
        def _(dve):
            steps = [0]

            def did(ins):
                ins.then_inc(dve_step, 1)
                steps[0] += 1
                return steps[0]

            def after(n):
                dve.wait_ge(dve_step, n)

            def heads(t):
                return t.rearrange("p t (h d) -> p (t h) d", d=D)

            def spread(t):
                return t[:].unsqueeze(2).broadcast_to([ST, STILES * H, D])

            def block_diagonals(s):
                ps = kvp[s % 2][:, 0:CB * (P + 1)].rearrange("p (b n) -> p b n", b=CB)
                dve.wait_ge(kc_ready, s + 1)
                if s:
                    dve.wait_ge(bd_ready, 2 * s)
                n = did(dve.tensor_tensor(kvm[:], ps[:, :, 0:P], mask[:].unsqueeze(1).broadcast_to([P, CB, P]), ALU.mult))
                for b in range(CB):
                    did(dve.tensor_scalar(kcbd[:, s, b, :], mask[:], kc[:, b:b + 1], None, ALU.mult))
                after(n)
                for b in range(CB):
                    dve.scalar_tensor_tensor(kvbd[:, s, b, :], bvm[:, b, :], kc[:, b:b + 1], kvm[:, b, :],
                                             ALU.mult, ALU.add).then_inc(bd_ready, 1)

            dve.wait_ge(mask_set, 3)
            dve.wait_ge(b_in, 32)
            dve.tensor_tensor(bvm[:], bv[:].rearrange("p (b c) -> p b c", b=CB),
                              mask[:].unsqueeze(1).broadcast_to([P, CB, P]), ALU.mult).then_inc(bvm_ready, 1)
            dve.wait_ge(bvm_ready, 1)
            for s in range(B):
                ks = k[s % 2]
                dve.wait_ge(v_ready, s + 1)
                if s >= 2:
                    dve.wait_ge(kv_done, s - 1)
                dve.tensor_tensor(ks[:], proj[s % 2][0:ST, :, 0:C], bk[:].unsqueeze(1).broadcast_to([ST, STILES, C]),
                                  ALU.add).then_inc(kbias_done, 1)
                dve.wait_ge(kbias_done, s + 1)
                n = did(dve.tensor_reduce(top[:], heads(ks[:]), AX.X, ALU.max))
                after(n)
                dve.tensor_tensor(heads(ks[:]), heads(ks[:]), spread(top), ALU.subtract).then_inc(arg_ready, 1)
                if s:
                    block_diagonals(s - 1)
                dve.wait_ge(exp_ready, s + 1)
                n = did(dve.tensor_reduce(total[:], heads(ks[:]), AX.X, ALU.add))
                after(n)
                n = did(dve.reciprocal(rec[:], total[:]))
                after(n)
                dve.tensor_tensor(heads(ks[:]), heads(ks[:]), spread(rec), ALU.mult).then_inc(k_ready, 1)
                dve.wait_ge(k_ready, s + 1)
            block_diagonals(B - 1)

        @block.scalar
        def _(act):
            act.wait_ge(const_set, 2)

            def sums_out(s):
                act.wait_ge(kv_done, s + 1)
                if s:
                    act.wait_ge(bd_ready, 2 * s)
                act.activation(kc[:], kvp[s % 2][:, P:2 * P + 2:P + 1], ACT.Copy).then_inc(kc_ready, 1)

            for s in range(B):
                act.wait_ge(proj_done, s + 1)
                if s >= 2:
                    act.wait_ge(kv_done, s - 1)
                act.activation(v[s % 2][:, :, :, 0:P], proj[s % 2][0:ST, :, C:2 * C].rearrange("p t (b c) -> p t b c", b=CB),
                               ACT.Copy).then_inc(v_ready, 1)
                if s:
                    sums_out(s - 1)
                act.wait_ge(arg_ready, s + 1)
                act.activation(k[s % 2][:], k[s % 2][:], ACT.Exp).then_inc(exp_ready, 1)
            sums_out(B - 1)

        @block.tensor
        def _(pe):
            def project(s):
                if s % CG == 0:
                    j = s // CG
                    pe.wait_ge(ct_in[j % 2], 16 * (j // 2 + 1))
                if s >= 2:
                    pe.wait_ge(kbias_done, s - 1)
                    pe.wait_ge(v_ready, s - 1)
                c0 = (s % CG) * S
                for t in range(STILES):
                    for b in range(CB):
                        ins = pe.matmul(proj[s % 2][0:ST, t, :], ct[(s // CG) % 2][:, b, c0 + t * ST:c0 + (t + 1) * ST],
                                        wkv[:, b, :], start=b == 0, stop=b == CB - 1)
                ins.then_inc(proj_done, 1)

            pe.wait_ge(w_in, 16)
            project(0)
            for s in range(B):
                if s + 1 < B:
                    project(s + 1)
                pe.wait_ge(k_ready, s + 1)
                pe.wait_ge(v_ready, s + 1)
                if s >= 2:
                    pe.wait_ge(bd_ready, 2 * (s - 1))
                for b in range(CB):
                    for t in range(STILES):
                        ins = pe.matmul(kvp[s % 2][:, b * (P + 1):(b + 1) * (P + 1)], k[s % 2][:, t, b * P:(b + 1) * P],
                                        v[s % 2][:, t, b, :], start=t == 0, stop=t == STILES - 1)
                ins.then_inc(kv_done, 1)

def attention_phase(nc, g, io):
    ctx = ExitStack()
    with ctx:
        def sb(name, shape, dt=FP32):
            return ctx.enter_context(nc.sbuf_tensor(name, shape, dt))

        def sem(name):
            return ctx.enter_context(nc.semaphore(name))

        x, ident, kvbd, kcbd = g["x"], g["ident"], g["kvbd"], g["kcbd"]
        wq, wp = sb("wq", [P, CB, C]), sb("wp", [P, CB, C])
        bq, bp = sb("bq", [T, C]), sb("bp", [T, C])
        eps = sb("eps3", [P, 1])
        xin = [sb(f"xin{i}", [T, G, C]) for i in range(2)]
        st = {k: sb(f"ast{k}", [T, G, 6]) for k in (1, 4)}
        mv = {k: sb(f"amv{k}", [T, G, 2]) for k in (1, 4)}
        lnv = {k: sb(f"alnv{k}", [T, G]) for k in (1, 4)}
        y0 = {k: sb(f"ay0{k}", [T, G]) for k in (1, 4)}
        yy = {k: sb(f"ayy{k}", [T, G]) for k in (1, 4)}
        rstd = {k: sb(f"arstd{k}", [T, G]) for k in (1, 4)}
        xt = sb("xt", [P, CB, G * T])
        q = sb("q", [T, G, C])
        top, total, rec = (sb(n, [T, G * H]) for n in ("qtop", "qtotal", "qrec"))
        qt = [sb(f"qt{i}", [P, CB, G * T]) for i in range(2)]
        rden = sb("rden", [P, CB, G * T])
        ot = sb("ot", [P, CB, G * T])
        pj = sb("pj", [T, G, C])
        bank = [ctx.enter_context(nc.psum_tensor(f"abank{i}", [P, 512], FP32)) for i in range(8)]

        w_in, eps_set = sem("aw_in"), sem("eps_set")
        xin_in = [sem(f"xin_in{i}") for i in range(2)]
        sum_done = sem("sum_done")
        lnstat = {k: sem(f"alnstat{k}") for k in (1, 4)}
        lnlog = {k: sem(f"alnlog{k}") for k in (1, 4)}
        lny0 = {k: sem(f"alny0{k}") for k in (1, 4)}
        x1_ready, x1_turned, xt_ready = sem("x1_ready"), sem("x1_turned"), sem("xt_ready")
        q_done, qbias_done, arg_ready, exp_ready, q_ready = (sem(n) for n in (
            "q_done", "qbias_done", "qarg_ready", "qexp_ready", "q_ready"))
        q_turned, qt_ready, num_done, den_done = sem("q_turned"), sem("qt_ready"), sem("num_done"), sem("den_done")
        den_read, ot_ready, pj_done, x2_ready = sem("den_read"), sem("ot_ready"), sem("pj_done"), sem("x2_ready")
        pj_read = sem("pj_read")
        dve_step = sem("adve_step")
        NS = GROUPS

        def valid(c):
            return 0 <= c < NS

        block = ctx.enter_context(nc.Block())

        @block.gpsimd
        def _(pool):
            pool.memset(eps[:], EPS).then_inc(eps_set, 1)

        @block.sync
        def _(sp):
            xv = io["x"].rearrange("b t c -> t b c")
            for c in range(NS):
                if c >= 2:
                    sp.wait_ge(sum_done, c - 1)
                sp.dma_start(xin[c % 2][:], xv[:, c * G:(c + 1) * G, :]).then_inc(xin_in[c % 2], 16)
                if c == 0:
                    sp.dma_start(wq[:], io["wq"]).then_inc(w_in, 16)
                    sp.dma_start(bq[:], io["bq"].partition_broadcast(T)).then_inc(w_in, 16)
                    sp.dma_start(wp[:], io["wp"]).then_inc(w_in, 16)
                    sp.dma_start(bp[:], io["bp"].partition_broadcast(T)).then_inc(w_in, 16)

        @block.vector
        def _(dve):
            steps = [0]

            def did(ins):
                ins.then_inc(dve_step, 1)
                steps[0] += 1
                return steps[0]

            def after(n):
                dve.wait_ge(dve_step, n)

            def chunk(c):
                return x[:, c * G:(c + 1) * G, :]

            def tiles(i):
                return bank[i][0:T, :].rearrange("p (g c) -> p g c", c=C)

            def over_tokens(t, n):
                return t[:].unsqueeze(1).broadcast_to([T, n, C])

            def heads(t):
                return t.rearrange("p g (h d) -> p (g h) d", d=D)

            def spread(t):
                return t[:].unsqueeze(2).broadcast_to([T, G * H, D])

            def layernorm(k, c, out, done):
                xc = chunk(c)
                for i in range(G):
                    n = did(dve.bn_stats(st[k][:, i, :], xc[:, i, :]))
                after(n)
                for i in range(G):
                    last = dve.bn_aggr(mv[k][:, i, :], st[k][:, i, :])
                    if i < G - 1:
                        did(last)
                last.then_inc(lnstat[k], 1)
                dve.wait_ge(lny0[k], c + 1)
                after(did(dve.tensor_tensor(yy[k][:], y0[k][:], y0[k][:], ALU.mult)))
                after(did(dve.scalar_tensor_tensor(yy[k][:], mv[k][:, :, 1], EPS, yy[k][:], ALU.add, ALU.mult)))
                after(did(dve.tensor_scalar(yy[k][:], yy[k][:], -0.5, 1.5, ALU.mult, ALU.add)))
                after(did(dve.tensor_tensor(rstd[k][:], yy[k][:], y0[k][:], ALU.mult)))
                for i in range(G):
                    last = dve.tensor_scalar(out[:, i, :], xc[:, i, :], mv[k][:, i, 0:1], rstd[k][:, i:i + 1],
                                             ALU.subtract, ALU.mult)
                    if i < G - 1:
                        did(last)
                last.then_inc(done, 1)

            def make_x1(c):
                dve.wait_ge(xin_in[c % 2], 16 * (c // 2 + 1))
                dve.tensor_tensor(chunk(c), chunk(c), xin[c % 2][:], ALU.add).then_inc(sum_done, 1)
                dve.wait_ge(sum_done, c + 1)
                layernorm(1, c, chunk(c), x1_ready)

            def q_softmax(c):
                if c:
                    dve.wait_ge(q_turned, CB * c)
                for i in range(2):
                    dve.wait_ge(q_done, 2 * c + i + 1)
                    dve.tensor_tensor(q[:, 2 * i:2 * i + 2, :], tiles(2 + i), over_tokens(bq, 2), ALU.add)\
                        .then_inc(qbias_done, 1)
                dve.wait_ge(qbias_done, 2 * c + 2)
                after(did(dve.tensor_reduce(top[:], heads(q[:]), AX.X, ALU.max)))
                dve.tensor_tensor(heads(q[:]), heads(q[:]), spread(top), ALU.subtract).then_inc(arg_ready, 1)
                dve.wait_ge(exp_ready, c + 1)
                after(did(dve.tensor_reduce(total[:], heads(q[:]), AX.X, ALU.add)))
                after(did(dve.reciprocal(rec[:], total[:])))
                dve.tensor_tensor(heads(q[:]), heads(q[:]), spread(rec), ALU.mult).then_inc(q_ready, 1)

            def attend(c):
                for b in range(CB):
                    dve.wait_ge(den_done, CB * c + b + 1)
                    if c:
                        dve.wait_ge(ot_ready, CB * c)
                    dve.reciprocal(rden[:, b, :], bank[b][:, 0:G * T]).then_inc(den_read, 1)
                n = [0] * CB
                for b in range(CB):
                    dve.wait_ge(den_read, CB * c + b + 1)
                    dve.wait_ge(num_done, CB * c + b + 1)
                    n[b] = did(dve.tensor_tensor(rden[:, b, :], rden[:, b, :], bank[6 + b][:, 0:G * T], ALU.mult))
                for b in range(CB):
                    after(n[b])
                    if c:
                        dve.wait_ge(pj_done, 2 * c)
                    dve.tensor_tensor(ot[:, b, :], rden[:, b, :], qt[c % 2][:, b, :], ALU.add).then_inc(ot_ready, 1)

            def make_x2(c):
                xc = chunk(c)
                if c:
                    dve.wait_ge(x2_ready, c)
                for i in range(2):
                    dve.wait_ge(pj_done, 2 * c + i + 1)
                    dve.tensor_tensor(pj[:, 2 * i:2 * i + 2, :], tiles(4 + i), over_tokens(bp, 2), ALU.add)\
                        .then_inc(pj_read, 1)
                dve.wait_ge(pj_read, 2 * c + 2)
                after(did(dve.tensor_tensor(xc, xc, pj[:], ALU.add)))
                layernorm(4, c, xc, x2_ready)

            dve.wait_ge(w_in, 64)
            for s in range(NS + 3):
                if valid(s):
                    make_x1(s)
                if valid(s - 2):
                    attend(s - 2)
                if valid(s - 1):
                    q_softmax(s - 1)
                if valid(s - 3):
                    make_x2(s - 3)

        @block.scalar
        def _(act):
            def rsqrt0(k, c):
                act.wait_ge(lnstat[k], c + 1)
                act.activation(lnv[k][:], mv[k][:, :, 1], ACT.Ln, bias=eps[0:T, :]).then_inc(lnlog[k], 1)
                act.wait_ge(lnlog[k], c + 1)
                act.activation(y0[k][:], lnv[k][:], ACT.Exp, scale=-0.5).then_inc(lny0[k], 1)

            act.preload_act_table_set("natural_log_exp_and_others")
            act.wait_ge(eps_set, 1)
            for s in range(NS + 3):
                c = s - 1
                if valid(s):
                    rsqrt0(1, s)
                if valid(c):
                    act.wait_ge(arg_ready, c + 1)
                    act.activation(q[:], q[:], ACT.Exp).then_inc(exp_ready, 1)
                if valid(s):
                    for b in range(CB):
                        act.wait_ge(x1_turned, CB * s + b + 1)
                        act.activation(xt[:, b, :], bank[b][:, 0:G * T], ACT.Copy).then_inc(xt_ready, 1)
                if valid(c):
                    for b in range(CB):
                        act.wait_ge(q_turned, CB * c + b + 1)
                        act.activation(qt[c % 2][:, b, :], bank[4 + b][:, 0:G * T], ACT.Copy).then_inc(qt_ready, 1)
                if valid(s - 3):
                    rsqrt0(4, s - 3)

        @block.tensor
        def _(pe):
            def turn(src, first_bank, done):
                for b in range(CB):
                    for i in range(G):
                        ins = pe.transpose(bank[first_bank + b][:, i * T:(i + 1) * T], src[:, i, b * P:(b + 1) * P],
                                           ident[0:T, 0:T])
                    ins.then_inc(done, 1)

            def tokens_out(first_bank, src, w, done):
                for i in range(G):
                    for b in range(CB):
                        ins = pe.matmul(bank[first_bank + i // 2][0:T, (i % 2) * C:(i % 2 + 1) * C],
                                        src[:, b, i * T:(i + 1) * T], w[:, b, :], start=b == 0, stop=b == CB - 1)
                    if i % 2:
                        ins.then_inc(done, 1)

            pe.wait_ge(w_in, 64)
            for s in range(NS + 3):
                if valid(s):
                    if s >= 2:
                        pe.wait_ge(den_read, CB * (s - 1))
                    pe.wait_ge(x1_ready, s + 1)
                    turn(x[:, s * G:(s + 1) * G, :], 0, x1_turned)
                c = s - 1
                if valid(c) and valid(s):
                    pe.wait_ge(qbias_done, 2 * s)
                if valid(s):
                    pe.wait_ge(xt_ready, CB * (s + 1))
                    tokens_out(2, xt, wq, q_done)
                if valid(c):
                    pe.wait_ge(q_ready, c + 1)
                    if c >= 2:
                        pe.wait_ge(pj_read, 2 * (c - 1))
                    turn(q, 4, q_turned)
                    pe.wait_ge(qt_ready, CB * (c + 1))
                    if c:
                        pe.wait_ge(ot_ready, CB * c)
                    if not valid(s):
                        pe.wait_ge(xt_ready, CB * NS)
                    for mat, first_bank, done in ((kcbd, 0, den_done), (kvbd, 6, num_done)):
                        for b in range(CB):
                            for i in range(G):
                                ins = pe.matmul(bank[first_bank + b][:, i * T:(i + 1) * T], mat[:, c * G + i, b, :],
                                                qt[c % 2][:, b, i * T:(i + 1) * T], start=True, stop=True)
                            ins.then_inc(done, 1)
                c = s - 2
                if valid(c):
                    pe.wait_ge(ot_ready, CB * (c + 1))
                    if not valid(s - 1):
                        pe.wait_ge(qt_ready, CB * NS)
                        pe.wait_ge(pj_read, 2 * c)
                    tokens_out(4, ot, wp, pj_done)

def expert_phase(nc, g, io):
    ctx = ExitStack()
    with ctx:
        def sb(name, shape, dt=FP32):
            return ctx.enter_context(nc.sbuf_tensor(name, shape, dt))

        def sem(name):
            return ctx.enter_context(nc.semaphore(name))

        x, ident = g["x"], g["ident"]
        wrt = sb("wrt", [P, CB, 2 * E])
        eps = sb("eps4", [P, 1])
        xt = sb("fxt", [P, CB, G * T])
        xh, xl = sb("xh", [P, CB, B * T], F32R), sb("xl", [P, CB, B * T], F32R)
        logit = sb("logit", [T, B, 2, E])
        top, total, rec = (sb(n, [T, B * 2]) for n in ("ltop", "ltotal", "lrec"))
        cw = sb("cw", [T, B, E])
        cws, cwr = sb("cws", [T, B]), sb("cwr", [T, B])
        raw = [sb(f"raw{i}", [P, WH]) for i in range(2)]
        wh = [sb(f"wh{i}", [P, WH], F32R) for i in range(2)]
        wl = [sb(f"wl{i}", [P, WH], F32R) for i in range(2)]
        sil = [sb(f"sil{i}", [P, G * T]) for i in range(2)]
        hf = [sb(f"hf{i}", [P, G * T]) for i in range(2)]
        hh = [sb(f"hh{i}", [P, FB, G * T], F32R) for i in range(2)]
        hl = [sb(f"hl{i}", [P, FB, G * T], F32R) for i in range(2)]
        acc = sb("acc", [T, B, C])
        st, mv = sb("fst", [T, G, 6]), sb("fmv", [T, G, 2])
        lnv, y0, yy, rstd = (sb(n, [T, G]) for n in ("flnv", "fy0", "fyy", "frstd"))
        bank = [ctx.enter_context(nc.psum_tensor(f"fbank{i}", [P, 512], FP32)) for i in range(8)]

        r_in, eps_set = sem("r_in"), sem("feps_set")
        raw_in = [sem(f"raw_in{i}") for i in range(2)]
        x_turned, xt_ready, xh_ready, xl_ready = sem("x_turned"), sem("fxt_ready"), sem("xh_ready"), sem("xl_ready")
        r_done, logit_ready = sem("r_done"), sem("logit_ready")
        larg_ready, lexp_ready, cw_ready = sem("larg_ready"), sem("lexp_ready"), sem("cw_ready")
        wh_ready, wl_ready = sem("wh_ready"), sem("wl_ready")
        gu_done, sil_ready, hf_ready, hh_ready, hl_ready = (sem(n) for n in (
            "gu_done", "sil_ready", "hf_ready", "hh_ready", "hl_ready"))
        down_done, acc_done = sem("down_done"), sem("acc_done")
        lnstat, lnlog, lny0, out_ready, out_stored = (sem(n) for n in (
            "flnstat", "flnlog", "flny0", "out_ready", "out_stored"))
        dve_step = sem("fdve_step")

        HALVES = 2 * E
        NT = HALVES * GROUPS
        GATE, UP, DOWN = 0, CB * FB * P, 2 * CB * FB * P

        def part(w, j):
            return w[:, j * UP:(j + 1) * UP]

        block = ctx.enter_context(nc.Block())

        @block.gpsimd
        def _(pool):
            pool.memset(eps[:], EPS).then_inc(eps_set, 1)

        @block.sync
        def _(sp):
            sp.dma_start(wrt[:], io["wrt"]).then_inc(r_in, 16)
            for he in range(HALVES):
                e, f0 = he // 2, (he % 2) * FB
                if he >= 2:
                    sp.wait_ge(wh_ready, 3 * (he - 1))
                    sp.wait_ge(wl_ready, 3 * (he - 1))
                r = raw[he % 2]
                for j, name in enumerate(("w_gate", "w_up")):
                    sp.dma_start(part(r, j).rearrange("p (b f) -> p b f", b=CB),
                                 io[name][e].rearrange("(b p) f -> p b f", p=P)[:, :, f0 * P:(f0 + FB) * P])\
                        .then_inc(raw_in[he % 2], 16)
                sp.dma_start(part(r, 2).rearrange("p (f c) -> p f c", f=FB),
                             io["w_down"][e].rearrange("(f p) c -> p f c", p=P)[:, f0:f0 + FB, :])\
                    .then_inc(raw_in[he % 2], 16)
            for c in range(GROUPS):
                sp.wait_ge(out_ready, c + 1)
                sp.dma_start(io["out"].rearrange("b t c -> t b c")[:, c * G:(c + 1) * G, :],
                             acc[:, c * G:(c + 1) * G, :]).then_inc(out_stored, 16)
            sp.wait_ge(out_stored, 16 * GROUPS)

        @block.vector
        def _(dve):
            steps = [0]

            def did(ins):
                ins.then_inc(dve_step, 1)
                steps[0] += 1
                return steps[0]

            def after(n):
                dve.wait_ge(dve_step, n)

            def split_x(c):
                cols = slice(c * G * T, (c + 1) * G * T)
                dve.wait_ge(xt_ready, CB * (c + 1))
                n = did(dve.tensor_copy(xh[:, :, cols], xt[:]))
                after(n)
                dve.tensor_tensor(xl[:, :, cols], xt[:], xh[:, :, cols], ALU.subtract).then_inc(xl_ready, 1)

            def low_weights(he, j):
                if j == 0:
                    dve.wait_ge(raw_in[he % 2], 48 * (he // 2 + 1))
                dve.wait_ge(wh_ready, 3 * he + j + 1)
                if he >= 2:
                    dve.wait_ge(down_done, 2 * GROUPS * (he - 1))
                dve.tensor_tensor(part(wl[he % 2], j), part(raw[he % 2], j), part(wh[he % 2], j),
                                  ALU.subtract).then_inc(wl_ready, 1)

            def combine_weights():
                lf = logit[:].rearrange("t b k e -> t (b k) e")
                dve.wait_ge(logit_ready, GROUPS)
                after(did(dve.tensor_scalar(logit[:, :, 1, :], logit[:, :, 1, :], 1.0 / GATE_TEMP, None, ALU.mult)))
                after(did(dve.tensor_reduce(top[:], lf, AX.X, ALU.max)))
                dve.tensor_tensor(lf, lf, top[:].unsqueeze(2).broadcast_to([T, 2 * B, E]), ALU.subtract)\
                    .then_inc(larg_ready, 1)
                dve.wait_ge(lexp_ready, 1)
                after(did(dve.tensor_reduce(total[:], lf, AX.X, ALU.add)))
                after(did(dve.reciprocal(rec[:], total[:])))
                after(did(dve.tensor_tensor(lf, lf, rec[:].unsqueeze(2).broadcast_to([T, 2 * B, E]), ALU.mult)))
                after(did(dve.tensor_tensor(cw[:], logit[:, :, 0, :], logit[:, :, 1, :], ALU.mult)))
                after(did(dve.tensor_reduce(cws[:], cw[:], AX.X, ALU.add)))
                after(did(dve.tensor_scalar(cws[:], cws[:], 1e-9, None, ALU.add)))
                after(did(dve.reciprocal(cwr[:], cws[:])))
                dve.tensor_tensor(cw[:], cw[:], cwr[:].unsqueeze(2).broadcast_to([T, B, E]), ALU.mult)\
                    .then_inc(cw_ready, 1)
                dve.wait_ge(cw_ready, 1)

            def times_up(ft):
                i = ft % 2
                dve.wait_ge(sil_ready, ft + 1)
                dve.wait_ge(gu_done, 2 * ft + 2)
                if ft >= 2:
                    dve.wait_ge(hh_ready, ft - 1)
                    dve.wait_ge(hl_ready, ft - 1)
                dve.tensor_tensor(hf[i][:], sil[i][:], bank[2 * i + 1][:, 0:G * T], ALU.mult).then_inc(hf_ready, 1)

            def low_h(ft):
                t, f = ft // FB, ft % FB
                dve.wait_ge(hh_ready, ft + 1)
                dve.tensor_tensor(hl[t % 2][:, f, :], hf[ft % 2][:], hh[t % 2][:, f, :], ALU.subtract)\
                    .then_inc(hl_ready, 1)

            def accumulate(t):
                he, c = t // GROUPS, t % GROUPS
                for i in range(G):
                    if i % 2 == 0:
                        dve.wait_ge(down_done, 2 * t + i // 2 + 1)
                    ps = bank[4 + 2 * (t % 2) + i // 2][0:T, (i % 2) * C:(i % 2 + 1) * C]
                    a, w = acc[:, c * G + i, :], cw[:, c * G + i, he // 2:he // 2 + 1]
                    if he == 0:
                        ins = dve.tensor_scalar(a, ps, w, None, ALU.mult)
                    else:
                        if i == 0:
                            dve.wait_ge(acc_done, G * (t - GROUPS + 1))
                        ins = dve.scalar_tensor_tensor(a, ps, w, a, ALU.mult, ALU.add)
                    ins.then_inc(acc_done, 1)

            def final_norm(c):
                xc, ac = x[:, c * G:(c + 1) * G, :], acc[:, c * G:(c + 1) * G, :]
                dve.wait_ge(acc_done, G * (NT - GROUPS + c + 1))
                after(did(dve.tensor_tensor(xc, xc, ac, ALU.add)))
                for i in range(G):
                    n = did(dve.bn_stats(st[:, i, :], xc[:, i, :]))
                after(n)
                for i in range(G):
                    last = dve.bn_aggr(mv[:, i, :], st[:, i, :])
                    if i < G - 1:
                        did(last)
                last.then_inc(lnstat, 1)
                dve.wait_ge(lny0, c + 1)
                after(did(dve.tensor_tensor(yy[:], y0[:], y0[:], ALU.mult)))
                after(did(dve.scalar_tensor_tensor(yy[:], mv[:, :, 1], EPS, yy[:], ALU.add, ALU.mult)))
                after(did(dve.tensor_scalar(yy[:], yy[:], -0.5, 1.5, ALU.mult, ALU.add)))
                after(did(dve.tensor_tensor(rstd[:], yy[:], y0[:], ALU.mult)))
                for i in range(G):
                    last = dve.tensor_scalar(ac[:, i, :], xc[:, i, :], mv[:, i, 0:1], rstd[:, i:i + 1],
                                             ALU.subtract, ALU.mult)
                    if i < G - 1:
                        did(last)
                last.then_inc(out_ready, 1)
                dve.wait_ge(out_ready, c + 1)

            for c in range(GROUPS):
                split_x(c)
            for j in range(3):
                low_weights(0, j)
            combine_weights()
            for t in range(NT):
                he, c = t // GROUPS, t % GROUPS
                for f in range(FB):
                    times_up(t * FB + f)
                    if t * FB + f:
                        low_h(t * FB + f - 1)
                    if f == 1 and t:
                        accumulate(t - 1)
                if c < 3 and he + 1 < HALVES:
                    low_weights(he + 1, c)
            low_h(NT * FB - 1)
            accumulate(NT - 1)
            for c in range(GROUPS):
                final_norm(c)

        @block.scalar
        def _(act):
            def high_weights(he, j):
                if j == 0:
                    act.wait_ge(raw_in[he % 2], 48 * (he // 2 + 1))
                if he >= 2:
                    act.wait_ge(down_done, 2 * GROUPS * (he - 1))
                act.activation(part(wh[he % 2], j), part(raw[he % 2], j), ACT.Copy).then_inc(wh_ready, 1)

            def high_h(ft):
                t, f = ft // FB, ft % FB
                if t >= 2 and f == 0:
                    act.wait_ge(down_done, 2 * (t - 1))
                act.wait_ge(hf_ready, ft + 1)
                act.activation(hh[t % 2][:, f, :], hf[ft % 2][:], ACT.Copy).then_inc(hh_ready, 1)

            act.preload_act_table_set("natural_log_exp_and_others")
            for c in range(GROUPS):
                for b in range(CB):
                    act.wait_ge(x_turned, CB * c + b + 1)
                    if c and b == 0:
                        act.wait_ge(xl_ready, c)
                        act.wait_ge(r_done, c)
                    act.activation(xt[:, b, :], bank[b][:, 0:G * T], ACT.Copy).then_inc(xt_ready, 1)
                act.wait_ge(r_done, c + 1)
                act.activation(logit[:, c * G:(c + 1) * G].rearrange("t b k e -> t (b k e)"),
                               bank[2][0:T, 0:G * 2 * E], ACT.Copy).then_inc(logit_ready, 1)
            for j in range(3):
                high_weights(0, j)
            act.wait_ge(larg_ready, 1)
            lf = logit[:].rearrange("t b k e -> t (b k e)")
            act.activation(lf, lf, ACT.Exp).then_inc(lexp_ready, 1)
            for t in range(NT):
                he, c = t // GROUPS, t % GROUPS
                for f in range(FB):
                    ft = t * FB + f
                    act.wait_ge(gu_done, 2 * ft + 1)
                    if ft >= 2:
                        act.wait_ge(hf_ready, ft - 1)
                    act.activation(sil[ft % 2][:], bank[2 * (ft % 2)][:, 0:G * T], ACT.Silu).then_inc(sil_ready, 1)
                    if ft:
                        high_h(ft - 1)
                if c < 3 and he + 1 < HALVES:
                    high_weights(he + 1, c)
            high_h(NT * FB - 1)
            act.wait_ge(eps_set, 1)
            for c in range(GROUPS):
                act.wait_ge(lnstat, c + 1)
                act.activation(lnv[:], mv[:, :, 1], ACT.Ln, bias=eps[0:T, :]).then_inc(lnlog, 1)
                act.wait_ge(lnlog, c + 1)
                act.activation(y0[:], lnv[:], ACT.Exp, scale=-0.5).then_inc(lny0, 1)

        @block.tensor
        def _(pe):
            def down(t):
                he = t // GROUPS
                for i in range(G):
                    n = 0
                    for f in range(FB):
                        if i == 0:
                            pe.wait_ge(hl_ready, t * FB + f + 1)
                        for a, w in ((hh, wh), (hh, wl), (hl, wh)):
                            ins = pe.matmul(bank[4 + 2 * (t % 2) + i // 2][0:T, (i % 2) * C:(i % 2 + 1) * C],
                                            a[t % 2][:, f, i * T:(i + 1) * T],
                                            w[he % 2][:, DOWN + f * C:DOWN + (f + 1) * C], start=n == 0,
                                            stop=n == 3 * FB - 1)
                            n += 1
                    if i % 2:
                        ins.then_inc(down_done, 1)

            for c in range(GROUPS):
                if c:
                    pe.wait_ge(xt_ready, CB * c)
                for b in range(CB):
                    for i in range(G):
                        ins = pe.transpose(bank[b][:, i * T:(i + 1) * T], x[:, c * G + i, b * P:(b + 1) * P],
                                           ident[0:T, 0:T])
                    ins.then_inc(x_turned, 1)
                if c == 0:
                    pe.wait_ge(r_in, 16)
                else:
                    pe.wait_ge(logit_ready, c)
                pe.wait_ge(xt_ready, CB * (c + 1))
                for i in range(G):
                    for b in range(CB):
                        ins = pe.matmul(bank[2][0:T, i * 2 * E:(i + 1) * 2 * E], xt[:, b, i * T:(i + 1) * T], wrt[:, b, :],
                                        start=b == 0, stop=b == CB - 1)
                ins.then_inc(r_done, 1)
            pe.wait_ge(logit_ready, GROUPS)
            for t in range(NT):
                he, c = t // GROUPS, t % GROUPS
                if he == 0:
                    pe.wait_ge(xl_ready, c + 1)
                if c == 0:
                    pe.wait_ge(wl_ready, 3 * (he + 1))
                cols = slice(c * G * T, (c + 1) * G * T)
                for f in range(FB):
                    ft = t * FB + f
                    if ft >= 2:
                        pe.wait_ge(hf_ready, ft - 1)
                    for k, w0 in ((0, GATE), (1, UP)):
                        n = 0
                        for a, w in ((xh, wh), (xl, wh), (xh, wl)):
                            for b in range(CB):
                                o = w0 + b * FB * P + f * P
                                ins = pe.matmul(bank[2 * (ft % 2) + k][:, 0:G * T], w[he % 2][:, o:o + P],
                                                a[:, b, cols], start=n == 0, stop=n == 3 * CB - 1)
                                n += 1
                        ins.then_inc(gu_done, 1)
                if t:
                    if t >= 3:
                        pe.wait_ge(acc_done, G * (t - 2))
                    down(t - 1)
            if NT >= 3:
                pe.wait_ge(acc_done, G * (NT - 2))
            down(NT - 1)

def build(nc, io):
    with ExitStack() as ctx:
        g = {
            "x": ctx.enter_context(nc.sbuf_tensor("x", [T, B, C], FP32)),
            "ident": ctx.enter_context(nc.sbuf_tensor("ident", [P, P], FP32)),
        }
        rwkv_phase(nc, g, io)
        with ExitStack() as held:
            for n in ("kvbd", "kcbd"):
                g[n] = held.enter_context(nc.sbuf_tensor(n, [P, B, CB, P], FP32))
            context_phase(nc, g, io)
            attention_phase(nc, g, io)
        expert_phase(nc, g, io)

def lay_out(inputs):
    import numpy as np

    def rows(w):
        *lead, k, n = w.shape
        return np.ascontiguousarray(np.moveaxis(w.reshape(*lead, k // P, P, n), -3, -2))

    a = {k.removeprefix("L0_"): np.asarray(v) for k, v in inputs.items()}
    out = {"x": a["x"], "ln0_w": a["attn_ln0_w"], "ln0_b": a["attn_ln0_b"]}
    for n, name in (("k", "Wk"), ("v", "Wv"), ("r", "Wr"), ("o", "Wo"), ("ck", "Wck"), ("cr", "Wcr"), ("cv", "Wcv")):
        out["w_" + n] = rows(np.swapaxes(a["attn_" + name], -1, -2))
    prm = [a["attn_" + n] for n in ("ln1_w", "ln1_b", "tmk", "tmv", "tmr", "time_decay", "time_first", "ln2_w",
                                    "ln2_b", "cmk", "cmr")]
    out["prm"] = np.ascontiguousarray(np.stack(prm).reshape(len(prm), L, CB, P).transpose(3, 1, 2, 0))
    out["ctx_t"] = np.ascontiguousarray(a["ctx_1024"].reshape(B * S, CB, P).transpose(2, 1, 0))
    out["wkv"] = np.concatenate([rows(a["xattn_Wk"].T), rows(a["xattn_Wv"].T)], axis=-1)
    out["wq"], out["wp"] = rows(a["xattn_Wq"].T), rows(a["xattn_Wp"].T)
    for n in "kvqp":
        out["b" + n] = a["xattn_b" + n]
    out["wrt"] = np.concatenate([rows(a["ffn_w_router"]), rows(a["ffn_w_gating"])], axis=-1)
    for n in ("w_gate", "w_up", "w_down"):
        out[n] = a["ffn_" + n]
    return out

def kernel(**inputs):
    import concourse.bacc as bacc
    from concourse.bass_utils import run_bass_kernel_spmd

    nc = bacc.Bacc("TRN2", target_bir_lowering=False, num_devices=1)
    arrays = lay_out(inputs)
    io = {n: nc.dram_tensor(f"in_{n}", a.shape, mybir.dt.from_np(a.dtype), kind="ExternalInput").ap()
          for n, a in arrays.items()}
    io["out"] = nc.dram_tensor("out_x", (B, T, C), FP32, kind="ExternalOutput").ap()
    build(nc, io)
    r = run_bass_kernel_spmd(nc, [{f"in_{n}": a for n, a in arrays.items()}], core_ids=[0])
    return r.results[0]["out_x"]
```

```python
from contextlib import ExitStack

import concourse.bass as bass
from concourse import mybir
from concourse.alu_op_type import AluOpType as ALU

FP32 = mybir.dt.float32
F32R = mybir.dt.float32r
ACT = mybir.ActivationFunctionType
AX = mybir.AxisListType

P = 128
B, T, C = 16, 112, 256
L, F = 4, 1024
CB = C // P
G = 4
GROUPS = B // G
STEPS = L * GROUPS
T1 = T + 1
EPS = 1e-5
NEVER = -1e38
LN_EXP, EXP_TANH = "natural_log_exp_and_others", "exp_and_others"
SPLIT = 2
NAMES = ["ln1w", "ln1b", "tmk", "tmv", "tmr", "td", "u", "ln2w", "ln2b", "cmk", "cmr", "w"]
PRM = {n: i for i, n in enumerate(NAMES)}
NPRM = len(NAMES)
S = 375
STILES = 3
ST = S // STILES
CG = 4
H, D = 16, 16
E = 8
FB = F // P // 2
WH = 2 * CB * FB * P + FB * C
GATE_TEMP = 0.1
N = B * T
TILES = N // P
COLS = 512

def load_half(engine, raw, io, e, h, loaded):
    f = slice(h * FB * P, (h + 1) * FB * P)
    for j, name in enumerate(("w_gate", "w_up")):
        w = io[name].rearrange("e (b p) f -> p e b f", p=P)
        engine.dma_start(raw[:, j * CB * FB * P:(j + 1) * CB * FB * P].rearrange("p (b f) -> p b f", b=CB),
                         w[:, e, :, f]).then_inc(loaded, 16)
    w = io["w_down"].rearrange("e (f p) c -> p e f c", p=P)
    engine.dma_start(raw[:, 2 * CB * FB * P:WH].rearrange("p (f c) -> p f c", f=FB),
                     w[:, e, h * FB:(h + 1) * FB, :]).then_inc(loaded, 16)

def rwkv_phase(nc, g, io):
    ctx = ExitStack()
    with ctx:
        def sb(name, shape, dt=FP32):
            return ctx.enter_context(nc.sbuf_tensor(name, shape, dt))

        def sem(name):
            return ctx.enter_context(nc.semaphore(name))

        x = g["x"]
        ident = g["ident"]
        wk, wv, wr, wo, wcr = (sb(n, [P, CB, C]) for n in ("wk", "wv", "wr", "wo", "wcr"))
        stage = sb("stage", [P, CB * F])
        wckh, wckl = sb("wckh", [P, CB * F], F32R), sb("wckl", [P, CB * F], F32R)
        wcvh, wcvl = sb("wcvh", [P, SPLIT * C], F32R), sb("wcvl", [P, SPLIT * C], F32R)
        wcv = sb("wcv", [P, (F // P - SPLIT) * C])
        prm = sb("prm", [P, L, CB, NPRM])
        ln0w, ln0b = sb("ln0w", [T, C]), sb("ln0b", [T, C])
        eps = sb("eps", [P, 1])
        xn = {1: sb("xn1", [T, G, C]), 2: sb("xn2", [T, G, C])}
        st = {k: sb(f"st{k}", [T, G, 6]) for k in (0, 1, 2)}
        mv = {k: sb(f"mv{k}", [T, G, 2]) for k in (0, 1, 2)}
        lnv = {k: sb(f"lnv{k}", [T, G]) for k in (0, 1, 2)}
        y0 = {k: sb(f"y0{k}", [T, G]) for k in (0, 1, 2)}
        yy = {k: sb(f"yy{k}", [T, G]) for k in (0, 1, 2)}
        rstd = {k: sb(f"rstd{k}", [T, G]) for k in (0, 1, 2)}
        shift = sb("shift", [T, G])
        h = {1: sb("h1", [P, CB, G, T1]), 2: sb("h2", [P, CB, G, T1])}
        diff = sb("diff", [P, CB, G, T])
        mixed = {n: sb("mix_" + n, [P, CB, G, T]) for n in ("k", "v", "r", "ck", "cr")}
        kp = sb("kp", [P, CB, G, T1])
        v = sb("v", [P, CB, G, T])
        th = sb("th", [P, CB, G, T])
        pp = sb("pp", [P, CB, G, T1])
        reset = sb("reset", [P, G, T1])
        decay = sb("decay", [P, CB, G, T1])
        dp, dk = sb("dp", [P, CB, G, T]), sb("dk", [P, CB, G, T])
        rw = [sb(f"rw{i}", [P, CB, G, T]) for i in range(2)]
        e1, e2 = sb("e1", [P, CB, G, T]), sb("e2", [P, CB, G, T])
        e1b, e2b = sb("e1b", [P, CB, G, T1]), sb("e2b", [P, CB, G, T1])
        lnden, rec = e2b[:, :, :, 1:T1], e1b[:, :, :, 1:T1]
        aa = sb("aa", [P, CB, G, T1])
        bb = sb("bb", [P, CB, G, T1])
        ckh, ckl = sb("ckh", [P, CB, G * T], F32R), sb("ckl", [P, CB, G * T], F32R)
        kf = [sb(f"kf{i}", [P, 2, G * T]) for i in range(4)]
        kfh, kfl = sb("kfh", [P, SPLIT, G * T], F32R), sb("kfl", [P, SPLIT, G * T], F32R)
        cth = sb("cth", [T, G, C])

        pair = [ctx.enter_context(nc.psum_tensor(f"pair{i}", [P, 2, 512], FP32)) for i in range(4)]

        params_in = sem("params_in")
        x_in = [sem(f"x_in{c}") for c in range(GROUPS)]
        wexp_done, w_ready = sem("wexp_done"), sem("w_ready")
        w_in = {n: sem("w_in_" + n) for n in ("k", "v", "r", "o", "cr", "cv")}
        stage_in, whi_ready, wlo_ready = sem("stage_in"), sem("whi_ready"), sem("wlo_ready")
        const_set = sem("const_set")
        lnstat = {k: sem(f"lnstat{k}") for k in (0, 1, 2)}
        lnlog = {k: sem(f"lnlog{k}") for k in (0, 1, 2)}
        lny0 = {k: sem(f"lny0{k}") for k in (0, 1, 2)}
        xn_ready = {k: sem(f"xn_ready{k}") for k in (1, 2)}
        turned = {k: sem(f"turned{k}") for k in (1, 2)}
        h_ready = {k: sem(f"h_ready{k}") for k in (1, 2)}
        shift_ready = sem("shift_ready")
        mix1_ready, mix2_ready = sem("mix1_ready"), sem("mix2_ready")
        ckh_ready, ckl_ready = sem("ckh_ready"), sem("ckl_ready")
        kvr_done, k_out, v_out, th_ready = sem("kvr_done"), sem("k_out"), sem("v_out"), sem("th_ready")
        arg_ready, side_ready, exp_ready = sem("arg_ready"), sem("side_ready"), sem("exp_ready")
        den_ready, num_ready, denlog, rec_ready = sem("den_ready"), sem("num_ready"), sem("denlog"), sem("rec_ready")
        wkv_ready = sem("wkv_ready")
        wo_done = sem("wo_done")
        ck_done, relu_done, square_done = sem("ck_done"), sem("relu_done"), sem("square_done")
        kfh_ready, kfl_ready = sem("kfh_ready"), sem("kfl_ready")
        cr_done, cth_ready = sem("cr_done"), sem("cth_ready")
        cv_done, cq_done, x_done = sem("cv_done"), sem("cq_done"), sem("x_done")
        dve_step = sem("dve_step")

        KVR = (1, 2, 0)
        HIDDEN = (1, 0, 2, 1)

        def valid(m):
            return 0 <= m < STEPS

        block = ctx.enter_context(nc.Block())

        @block.gpsimd
        def _(pool):
            for t in (h[1], h[2], e1b, e2b, aa):
                pool.memset(t[:, :, :, 0:1], 0.0).then_inc(const_set, 1)
            pool.memset(kp[:, :, :, 0:1], NEVER).then_inc(const_set, 1)
            pool.memset(eps[:], EPS).then_inc(const_set, 1)
            pool.memset(reset[:], 0.0).then_inc(const_set, 1)
            pool.memset(ident[:], 0.0).then_inc(const_set, 1)
            pool.wait_ge(const_set, 9)
            pool.memset(reset[:, :, 0:1], 2 * NEVER).then_inc(const_set, 1)
            pool.affine_select(out=ident[:], in_=ident[:], compare_op=ALU.not_equal, fill=1.0, base=0,
                               pattern=[[-1, P]], channel_multiplier=1).then_inc(const_set, 1)

        @block.sync
        def _(sp):
            xv = io["x"].rearrange("b t c -> t b c")
            for c in range(GROUPS):
                sp.dma_start(x[:, c * G:(c + 1) * G, :], xv[:, c * G:(c + 1) * G, :]).then_inc(x_in[c], 16)
                if c == 0:
                    sp.dma_start(ln0w[:], io["ln0_w"].partition_broadcast(T)).then_inc(params_in, 16)
                    sp.dma_start(ln0b[:], io["ln0_b"].partition_broadcast(T)).then_inc(params_in, 16)
                    sp.dma_start(prm[:, :, :, 0:NPRM - 1], io["prm"]).then_inc(params_in, 16)
            uses = (("k", wk, kvr_done, 3), ("v", wv, kvr_done, 3), ("r", wr, kvr_done, 3), ("o", wo, wo_done, 1),
                    ("cr", wcr, cr_done, 1), ("cv", wcv, cv_done, 2))

            def load_stage(l, name):
                n = 2 * l + (name == "cv")
                if n:
                    sp.wait_ge(whi_ready, n)
                    sp.wait_ge(wlo_ready, n)
                w = io["w_" + name][l].rearrange("p b c -> p (b c)")
                if name == "cv":
                    w = w[:, 0:SPLIT * C]
                sp.dma_start(stage[:, 0:w.shape[1]], w).then_inc(stage_in, 16)

            for l in range(STEPS // GROUPS):
                if l:
                    load_stage(l, "ck")
                for n, tile, used, per in uses:
                    if l:
                        sp.wait_ge(used, per * GROUPS * l)
                    w = io["w_" + n][l].rearrange("p b c -> p (b c)")
                    t = tile if n == "cv" else tile[:].rearrange("p b c -> p (b c)")
                    sp.dma_start(t[:, :], w[:, -t.shape[1]:]).then_inc(w_in[n], 16)
                    if l == 0 and n == "r":
                        load_stage(l, "ck")
                load_stage(l, "cv")

        @block.vector
        def _(dve):
            steps = [0]

            def did(ins):
                ins.then_inc(dve_step, 1)
                steps[0] += 1
                return steps[0]

            def after(n):
                dve.wait_ge(dve_step, n)

            def chunk(m):
                c = m % GROUPS
                return x[:, c * G:(c + 1) * G, :]

            def param(m, b, name):
                return prm[:, m // GROUPS, b, PRM[name]:PRM[name] + 1]

            def stats(k, xc):
                for i in range(G):
                    n = did(dve.bn_stats(st[k][:, i, :], xc[:, i, :]))
                after(n)
                for i in range(G):
                    last = dve.bn_aggr(mv[k][:, i, :], st[k][:, i, :])
                    if i < G - 1:
                        did(last)
                last.then_inc(lnstat[k], 1)

            def rsqrt(k, m):
                dve.wait_ge(lny0[k], m + 1)
                after(did(dve.tensor_tensor(yy[k][:], y0[k][:], y0[k][:], ALU.mult)))
                after(did(dve.scalar_tensor_tensor(yy[k][:], mv[k][:, :, 1], EPS, yy[k][:], ALU.add, ALU.mult)))
                after(did(dve.tensor_scalar(yy[k][:], yy[k][:], -0.5, 1.5, ALU.mult, ALU.add)))
                after(did(dve.tensor_tensor(rstd[k][:], yy[k][:], y0[k][:], ALU.mult)))

            def normalise(k, out, xc, done=None):
                for i in range(G):
                    last = dve.tensor_scalar(out[:, i, :], xc[:, i, :], mv[k][:, i, 0:1], rstd[k][:, i:i + 1],
                                             ALU.subtract, ALU.mult)
                    if i < G - 1 or done is None:
                        n = did(last)
                if done is not None:
                    last.then_inc(done, 1)
                return n

            def set_shift(m):
                dve.scalar_tensor_tensor(shift[:], mv[1][:, :, 0], -1.0, rstd[1][:], ALU.mult, ALU.mult)\
                    .then_inc(shift_ready, 1)

            def first_norm(m):
                xc = chunk(m)
                dve.wait_ge(x_in[m], 16)
                stats(0, xc)
                rsqrt(0, m)
                after(normalise(0, xc, xc))
                dve.wait_ge(params_in, 48)
                n = did(dve.tensor_tensor(xc, xc, ln0w[:].unsqueeze(1).broadcast_to([T, G, C]), ALU.mult))
                after(n)
                after(did(dve.tensor_tensor(xc, xc, ln0b[:].unsqueeze(1).broadcast_to([T, G, C]), ALU.add)))

            def difference(k, m):
                n = 0
                if m:
                    dve.wait_ge(*((kvr_done, 3 * m) if k == 1 else (cr_done, m)))
                if k == 2:
                    dve.wait_ge(mix1_ready, 6 * min(m + 3, STEPS))
                for b in range(CB):
                    dve.wait_ge(h_ready[k], CB * m + b + 1)
                    n = did(dve.tensor_tensor(diff[:, b], h[k][:, b, :, 1:T1], h[k][:, b, :, 0:T], ALU.subtract))
                return n

            def mix(k, m, names, params, done, n):
                after(n)
                for name, mu in zip(names, params):
                    for b in range(CB):
                        dve.scalar_tensor_tensor(mixed[name][:, b], diff[:, b], param(m, b, mu),
                                                 h[k][:, b, :, 0:T], ALU.mult, ALU.add).then_inc(done, 1)

            def flat(t):
                return t[:].rearrange("p b g t -> p (b g t)")

            def at(t, first):
                return t[:, :, :, first:first + T].rearrange("p b g t -> p (b g) t")

            def tokens(t):
                return t[:].rearrange("p b g t -> p (b g) t")

            def wkv_arguments(m):
                n = 0
                if m % GROUPS == 0:
                    for b in range(CB):
                        n = did(dve.tensor_scalar(decay[:, b], reset[:], param(m, b, "w"), None, ALU.add))
                    after(n)
                dve.wait_ge(k_out, m + 1)
                n = did(dve.tensor_tensor_scan(flat(pp), flat(decay), flat(kp), 0.0, ALU.add, ALU.max))
                du = rw[m % 2]
                after(n)
                dve.tensor_tensor(tokens(dp), at(pp, 0), at(pp, 1), ALU.subtract).then_inc(arg_ready, 1)
                dve.tensor_tensor(tokens(dk), at(kp, 1), at(pp, 1), ALU.subtract).then_inc(arg_ready, 1)
                for b in range(CB):
                    dve.scalar_tensor_tensor(du[:, b], kp[:, b, :, 1:T1], param(m, b, "u"),
                                             pp[:, b, :, 0:T], ALU.add, ALU.subtract).then_inc(arg_ready, 1)

            def wkv_sums(m):
                dve.wait_ge(exp_ready, 5 * m + 3)
                did(dve.tensor_tensor_scan(flat(bb), flat(e1b), flat(e2b), 0.0, ALU.mult, ALU.add))
                dve.wait_ge(v_out, m + 1)
                n = did(dve.tensor_tensor(at(aa, 1), at(e2b, 1), tokens(v), ALU.mult))
                after(n)
                did(dve.tensor_tensor_scan(flat(aa), flat(e1b), flat(aa), 0.0, ALU.mult, ALU.add))

            def wkv_denominator(m):
                dve.wait_ge(exp_ready, 5 * m + 5)
                n = did(dve.tensor_tensor(tokens(dp), tokens(e1), at(bb, 0), ALU.mult))
                after(n)
                dve.tensor_tensor(dp[:], dp[:], e2[:], ALU.add).then_inc(den_ready, 1)

            def wkv_numerator(m):
                du = rw[m % 2]
                n = did(dve.tensor_tensor(tokens(dk), tokens(e2), tokens(v), ALU.mult))
                n = did(dve.tensor_tensor(tokens(du), tokens(e1), at(aa, 0), ALU.mult))
                after(n)
                n = did(dve.tensor_tensor(du[:], du[:], dk[:], ALU.add))
                dve.wait_ge(th_ready, m + 1)
                after(n)
                dve.scalar_tensor_tensor(du[:], th[:], 1.0, du[:], ALU.add, ALU.mult).then_inc(num_ready, 1)

            def wkv_out(m):
                q = [0] * CB
                for b in range(CB):
                    dve.wait_ge(rec_ready, CB * m + b + 1)
                    q[b] = did(dve.tensor_tensor(dk[:, b], dp[:, b], rec[:, b], ALU.mult))
                for b in range(CB):
                    after(q[b])
                    q[b] = did(dve.scalar_tensor_tensor(dk[:, b], dk[:, b], 2.0, rec[:, b], ALU.subtract, ALU.mult))
                dve.wait_ge(num_ready, m + 1)
                for b in range(CB):
                    after(q[b])
                    dve.scalar_tensor_tensor(rw[m % 2][:, b], rw[m % 2][:, b], -0.5, dk[:, b], ALU.mult, ALU.mult).then_inc(wkv_ready, 1)

            def add_wkv(m):
                xc = chunk(m)
                dve.wait_ge(wo_done, m + 1)
                return did(dve.tensor_tensor(xc.rearrange("p (i g) c -> p i (g c)", i=2),
                                             xc.rearrange("p (i g) c -> p i (g c)", i=2), pair[0][0:T], ALU.add))

            def low_ck(m):
                dve.wait_ge(ckh_ready, m + 1)
                dve.tensor_tensor(ckl[:], mixed["ck"][:].rearrange("p b g t -> p b (g t)"), ckh[:], ALU.subtract)\
                    .then_inc(ckl_ready, 1)

            def low_kf(m, j):
                dve.wait_ge(kfh_ready, SPLIT // 2 * m + j + 1)
                dve.tensor_tensor(kfl[:, 2 * j:2 * j + 2], kf[j][:], kfh[:, 2 * j:2 * j + 2], ALU.subtract)\
                    .then_inc(kfl_ready, 1)

            def low_weights(n, tile, high, used, count):
                dve.wait_ge(whi_ready, n + 1)
                if count:
                    dve.wait_ge(used, count)
                dve.tensor_tensor(tile[:], stage[:, 0:tile.shape[1]], high[:], ALU.subtract).then_inc(wlo_ready, 1)

            def gate_channel(m):
                for i in range(2):
                    g2 = slice(2 * i, 2 * i + 2)
                    if i == 0:
                        dve.wait_ge(cth_ready, m + 1)
                    dve.wait_ge(cv_done, 2 * m + i + 1)
                    dve.scalar_tensor_tensor(cth[:, g2], cth[:, g2], 1.0,
                                             pair[3][0:T, i].rearrange("p (g c) -> p g c", c=C),
                                             ALU.add, ALU.mult).then_inc(cq_done, 1)

            def add_channel(m):
                xc = chunk(m)
                for i in range(2):
                    g2 = slice(2 * i, 2 * i + 2)
                    dve.wait_ge(cq_done, 2 * m + i + 1)
                    dve.scalar_tensor_tensor(xc[:, g2], cth[:, g2], 0.5, xc[:, g2], ALU.mult, ALU.add)\
                        .then_inc(x_done, 1)

            dve.wait_ge(const_set, 11)
            dve.wait_ge(wexp_done, 1)
            pw = PRM["w"]
            dve.tensor_scalar(prm[:, :, :, pw:pw + 1], prm[:, :, :, pw:pw + 1], -1.0, None, ALU.mult).then_inc(w_ready, 1)
            dve.wait_ge(w_ready, 1)
            for s in range(-3, STEPS + 1):
                if valid(s):
                    after(add_wkv(s))
                    stats(2, chunk(s))
                    if s % GROUPS == 0:
                        l = s // GROUPS
                        low_weights(2 * l, wckl, wckh, ck_done, 4 * GROUPS * l)
                if valid(s + 1):
                    wkv_denominator(s + 1)
                if valid(s):
                    rsqrt(2, s)
                    normalise(2, xn[2], chunk(s), xn_ready[2])
                if valid(s + 2):
                    n = difference(1, s + 2)
                    mix(1, s + 2, ("k", "v", "r"), ("tmk", "tmv", "tmr"), mix1_ready, n)
                if valid(s):
                    n = difference(2, s)
                    mix(2, s, ("cr",), ("cmr",), mix2_ready, n)
                if valid(s - 1):
                    gate_channel(s - 1)
                if valid(s):
                    mix(2, s, ("ck",), ("cmk",), mix2_ready, n)
                if valid(s + 1):
                    wkv_numerator(s + 1)
                if valid(s - 1):
                    add_channel(s - 1)
                if valid(s):
                    low_ck(s)
                if valid(s + 3):
                    if s + 3 < GROUPS:
                        first_norm(s + 3)
                    else:
                        dve.wait_ge(x_done, 2 * (s + 3 - GROUPS + 1))
                    stats(1, chunk(s + 3))
                if valid(s + 1):
                    wkv_out(s + 1)
                if valid(s + 2):
                    wkv_arguments(s + 2)
                if valid(s) and s % GROUPS == 0:
                    l = s // GROUPS
                    low_weights(2 * l + 1, wcvl, wcvh, cv_done, 2 * GROUPS * l)
                if valid(s):
                    low_kf(s, 0)
                if valid(s + 3):
                    rsqrt(1, s + 3)
                    set_shift(s + 3)
                if valid(s):
                    for j in range(1, SPLIT // 2):
                        low_kf(s, j)
                if valid(s + 2):
                    wkv_sums(s + 2)

        @block.scalar
        def _(act):
            def param(m, b, name):
                return prm[:, m // GROUPS, b, PRM[name]:PRM[name] + 1]

            def padded(t):
                return t.rearrange("p (g t) -> p g t", t=T)

            def rsqrt0(k, m):
                act.wait_ge(lnstat[k], m + 1)
                act.activation(lnv[k][:], mv[k][:, :, 1], ACT.Ln, bias=eps[0:T, :]).then_inc(lnlog[k], 1)
                act.wait_ge(lnlog[k], m + 1)
                act.activation(y0[k][:], lnv[k][:], ACT.Exp, scale=-0.5).then_inc(lny0[k], 1)

            def norm_out(k, m, banks, w, b_):
                for b in range(CB):
                    act.wait_ge(turned[k], CB * m + b + 1)
                    act.activation(h[k][:, b, :, 1:T1], padded(banks[:, b, 0:G * T]), ACT.Identity,
                                   bias=param(m, b, b_), scale=param(m, b, w)).then_inc(h_ready[k], 1)

            def normalise1(m):
                act.wait_ge(shift_ready, m + 1)
                xc = x[:, (m % GROUPS) * G:(m % GROUPS + 1) * G, :]
                for i in range(G):
                    ins = act.activation(xn[1][:, i, :], xc[:, i, :], ACT.Identity, bias=shift[:, i:i + 1],
                                         scale=rstd[1][:, i:i + 1])
                ins.then_inc(xn_ready[1], 1)

            def out(m, which, dst, done, func=ACT.Copy, scale=1.0):
                act.wait_ge(kvr_done, 3 * m + which + 1)
                act.activation(dst, pair[KVR[which]][:, :, 0:G * T].rearrange("p b (g t) -> p b g t", t=T), func,
                               scale=scale).then_inc(done, 1)

            def high_ck(m):
                act.wait_ge(mix2_ready, 4 * m + 4)
                act.activation(ckh[:], mixed["ck"][:].rearrange("p b g t -> p b (g t)"), ACT.Copy).then_inc(ckh_ready, 1)

            def hidden(m, j):
                act.wait_ge(ck_done, 4 * m + j + 1)
                split = 2 * j < SPLIT
                if m and split:
                    act.wait_ge(kfl_ready, SPLIT // 2 * (m - 1) + j + 1)
                if m and not split:
                    act.wait_ge(cv_done, 2 * m)
                t = kf[j]
                act.activation(t[:], pair[HIDDEN[j]][:, :, 0:G * T], ACT.Relu).then_inc(relu_done, 1)
                act.wait_ge(relu_done, 4 * m + j + 1)
                act.activation(t[:], t[:], ACT.Square).then_inc(square_done, 1)
                if not split:
                    return
                act.wait_ge(square_done, 4 * m + j + 1)
                if m and j == 0:
                    act.wait_ge(cv_done, 2 * m)
                act.activation(kfh[:, 2 * j:2 * j + 2], t[:], ACT.Copy).then_inc(kfh_ready, 1)

            def high_weights(n, tile, used, count):
                act.wait_ge(stage_in, 16 * (n + 1))
                if count:
                    act.wait_ge(used, count)
                act.activation(tile[:], stage[:, 0:tile.shape[1]], ACT.Copy).then_inc(whi_ready, 1)

            def wkv_exp(m, what):
                if what < 2:
                    act.wait_ge(arg_ready, 4 * m + what + 1)
                if what == 0:
                    for b in range(CB):
                        act.activation(e1b[:, b, :, 1:T1], dp[:, b], ACT.Exp, bias=param(m, b, "w")).then_inc(exp_ready, 1)
                elif what == 1:
                    act.activation(e2b[:, :, :, 1:T1], dk[:], ACT.Exp).then_inc(exp_ready, 1)
                else:
                    act.wait_ge(arg_ready, 4 * m + 4)
                    for t, sign in ((e1, 1.0), (e2, -1.0)):
                        act.activation(t[:], rw[m % 2][:], ACT.Relu, scale=sign).then_inc(side_ready, 1)
                    for i, t in enumerate((e1, e2)):
                        act.wait_ge(side_ready, 2 * m + i + 1)
                        act.activation(t[:], t[:], ACT.Exp, scale=-1.0).then_inc(exp_ready, 1)

            def reciprocal0(m):
                act.wait_ge(den_ready, m + 1)
                for b in range(CB):
                    act.activation(lnden[:, b], dp[:, b], ACT.Ln).then_inc(denlog, 1)
                for b in range(CB):
                    act.wait_ge(denlog, CB * m + b + 1)
                    act.activation(rec[:, b], lnden[:, b], ACT.Exp, scale=-1.0).then_inc(rec_ready, 1)

            def gate(m):
                act.wait_ge(cr_done, m + 1)
                if m:
                    act.wait_ge(x_done, 2 * m)
                act.activation(cth[:], pair[3][0:T].rearrange("p i (g c) -> p (i g) c", c=C), ACT.Tanh,
                               scale=0.5).then_inc(cth_ready, 1)

            act.wait_ge(const_set, 11)
            act.wait_ge(params_in, 48)
            act.preload_act_table_set(LN_EXP)
            act.activation(prm[:, :, :, PRM["w"]:PRM["w"] + 1], prm[:, :, :, PRM["td"]:PRM["td"] + 1],
                           ACT.Exp).then_inc(wexp_done, 1)
            act.wait_ge(w_ready, 1)
            for s in range(-3, STEPS + 1):
                if valid(s) and s % GROUPS == 0:
                    l = s // GROUPS
                    high_weights(2 * l, wckh, ck_done, 4 * GROUPS * l)
                if valid(s + 1):
                    wkv_exp(s + 1, 2)
                if valid(s):
                    rsqrt0(2, s)
                if valid(s + 1):
                    reciprocal0(s + 1)
                if valid(s + 2):
                    norm_out(1, s + 2, pair[2], "ln1w", "ln1b")
                if valid(s):
                    norm_out(2, s, pair[0], "ln2w", "ln2b")
                if valid(s + 2):
                    out(s + 2, 0, kp[:, :, :, 1:T1], k_out)
                    if s + 2:
                        act.wait_ge(num_ready, s + 2)
                    out(s + 2, 1, v[:], v_out)
                if valid(s):
                    high_ck(s)
                if valid(s + 2) or valid(s):
                    act.preload_act_table_set(EXP_TANH)
                if valid(s + 2):
                    out(s + 2, 2, th[:], th_ready, ACT.Tanh, 0.5)
                if valid(s):
                    gate(s)
                if valid(s + 2) or valid(s):
                    act.preload_act_table_set(LN_EXP)
                if valid(s + 3):
                    if s + 3 < GROUPS:
                        rsqrt0(0, s + 3)
                    rsqrt0(1, s + 3)
                if valid(s):
                    hidden(s, 0)
                if valid(s + 2):
                    wkv_exp(s + 2, 0)
                if valid(s) and s % GROUPS == 0:
                    l = s // GROUPS
                    high_weights(2 * l + 1, wcvh, cv_done, 2 * GROUPS * l)
                if valid(s):
                    hidden(s, 1)
                if valid(s + 2):
                    wkv_exp(s + 2, 1)
                if valid(s):
                    hidden(s, 2)
                    hidden(s, 3)
                if valid(s + 3):
                    normalise1(s + 3)

        @block.tensor
        def _(pe):
            pe.wait_ge(const_set, 11)

            def turn(k, m, banks):
                pe.wait_ge(xn_ready[k], m + 1)
                for b in range(CB):
                    for i in range(G):
                        ins = pe.transpose(banks[:, b, i * T:(i + 1) * T], xn[k][:, i, b * P:(b + 1) * P],
                                           ident[0:T, 0:T])
                    ins.then_inc(turned[k], 1)

            def project(m, which, w, src, name):
                pe.wait_ge(w_in[name], 16 * (m // GROUPS + 1))
                for o in range(CB):
                    for b in range(CB):
                        if o == 0:
                            pe.wait_ge(mix1_ready, 6 * m + CB * which + b + 1)
                        ins = pe.matmul(pair[KVR[which]][:, o, 0:G * T], w[:, b, o * P:(o + 1) * P],
                                        src[:, b].rearrange("p g t -> p (g t)"), start=b == 0, stop=b == CB - 1)
                ins.then_inc(kvr_done, 1)

            def tokens_out(banks, src, w, ready, count):
                for i in range(G):
                    for b in range(CB):
                        if i == 0:
                            pe.wait_ge(ready, count + b + 1)
                        ins = pe.matmul(banks[0:T, i // 2, (i % 2) * C:(i % 2 + 1) * C], src[:, b, i, :], w[:, b, :],
                                        start=b == 0, stop=b == CB - 1)
                return ins

            def hidden(m, j):
                banks = pair[HIDDEN[j]]
                for i in range(2):
                    n = 0
                    o = (2 * j + i) * P
                    for w, a in ((wckh, ckh), (wckl, ckh), (wckh, ckl)):
                        if i == 0 and j == 0 and a is ckl:
                            pe.wait_ge(ckl_ready, m + 1)
                        for b in range(CB):
                            ins = pe.matmul(banks[:, i, 0:G * T], w[:, b * F + o:b * F + o + P], a[:, b, :],
                                            start=n == 0, stop=n == 3 * CB - 1)
                            n += 1
                ins.then_inc(ck_done, 1)

            def channel_out(m, sequences):
                for i in sequences:
                    n = 0
                    for j in range(F // P):
                        if i == 0 and j % 2 == 0 and j < SPLIT:
                            pe.wait_ge(kfl_ready, SPLIT // 2 * m + j // 2 + 1)
                        elif i == 0 and j % 2 == 0:
                            pe.wait_ge(square_done, 4 * m + j // 2 + 1)
                        if j < SPLIT:
                            parts = [(a[:, j], w[:, j * C:(j + 1) * C]) for a, w in ((kfh, wcvh), (kfh, wcvl), (kfl, wcvh))]
                        else:
                            parts = [(kf[j // 2][:, j % 2], wcv[:, (j - SPLIT) * C:(j - SPLIT + 1) * C])]
                        for a, w in parts:
                            ins = pe.matmul(pair[3][0:T, i // 2, (i % 2) * C:(i % 2 + 1) * C], a[:, i * T:(i + 1) * T],
                                            w, start=n == 0, stop=j == F // P - 1)
                            n += 1
                    if i % 2:
                        ins.then_inc(cv_done, 1)

            for s in range(-3, STEPS + 1):
                m = s
                if valid(m):
                    pe.wait_ge(w_in["o"], 16 * (m // GROUPS + 1))
                    if m:
                        pe.wait_ge(relu_done, 4 * m - 2)
                    else:
                        pe.wait_ge(th_ready, 2)
                    tokens_out(pair[0], rw[m % 2], wo, wkv_ready, CB * m).then_inc(wo_done, 1)
                m = s - 1
                if valid(m):
                    pe.wait_ge(wlo_ready, 2 * (m // GROUPS) + 2)
                    pe.wait_ge(w_in["cv"], 16 * (m // GROUPS + 1))
                    pe.wait_ge(cth_ready, m + 1)
                    channel_out(m, (0, 1))
                m = s + 2
                if valid(m):
                    if m and s < 1:
                        pe.wait_ge(v_out, m)
                    turn(1, m, pair[2])
                m = s - 1
                if valid(m):
                    channel_out(m, (2, 3))
                m = s
                if valid(m):
                    turn(2, m, pair[0])
                m = s + 2
                if valid(m):
                    if m == 1:
                        pe.wait_ge(k_out, 1)
                    project(m, 0, wk, mixed["k"], "k")
                    project(m, 1, wv, mixed["v"], "v")
                    if m >= 2:
                        pe.wait_ge(h_ready[2], CB * (s + 1))
                    elif m:
                        pe.wait_ge(th_ready, 1)
                    project(m, 2, wr, mixed["r"], "r")
                m = s
                if valid(m):
                    pe.wait_ge(w_in["cr"], 16 * (m // GROUPS + 1))
                    if m:
                        pe.wait_ge(cq_done, 2 * m)
                    tokens_out(pair[3], mixed["cr"], wcr, mix2_ready, 4 * m).then_inc(cr_done, 1)
                    pe.wait_ge(wlo_ready, 2 * (m // GROUPS) + 1)
                    pe.wait_ge(ckh_ready, m + 1)
                    if valid(m + 2):
                        pe.wait_ge(k_out, m + 3)
                    hidden(m, 0)
                    if valid(m + 2):
                        pe.wait_ge(th_ready, m + 3)
                    hidden(m, 1)
                    if valid(m + 2):
                        pe.wait_ge(v_out, m + 3)
                    hidden(m, 2)
                    pe.wait_ge(relu_done, 4 * m + 1)
                    hidden(m, 3)

def context_phase(nc, g, io):
    ctx = ExitStack()
    with ctx:
        def sb(name, shape, dt=FP32):
            return ctx.enter_context(nc.sbuf_tensor(name, shape, dt))

        def sem(name):
            return ctx.enter_context(nc.semaphore(name))

        kvbd, kcbd = g["kvbd"], g["kcbd"]
        wkv = sb("wkv", [P, CB, 2 * C])
        bk = sb("bk", [ST, C])
        bv = sb("bv", [P, C])
        mask = sb("mask", [P, P])
        bvm = sb("bvm", [P, CB, P])
        ct = [sb(f"ct{i}", [P, CB, CG * S]) for i in range(2)]
        k = [sb(f"k{i}", [ST, STILES, C]) for i in range(2)]
        v = [sb(f"v{i}", [ST, STILES, CB, P + 1]) for i in range(2)]
        top, total, rec = (sb(n, [ST, STILES * H]) for n in ("top", "total", "rec"))
        kc = sb("kc", [P, CB])
        kvm = sb("kvm", [P, CB, P])
        proj = [ctx.enter_context(nc.psum_tensor(f"proj{i}", [P, STILES, 512], FP32)) for i in range(2)]
        kvp = [ctx.enter_context(nc.psum_tensor(f"kvp{i}", [P, 512], FP32)) for i in range(2)]

        w_in, b_in = sem("w_in"), sem("b_in")
        ct_in = [sem(f"ct_in{i}") for i in range(2)]
        const_set, mask_set, bvm_ready = sem("const_set"), sem("mask_set"), sem("bvm_ready")
        proj_done, kv_done = sem("proj_done"), sem("kv_done")
        v_ready, arg_ready, exp_ready, k_ready = sem("v_ready"), sem("arg_ready"), sem("exp_ready"), sem("k_ready")
        kbias_done = sem("kbias_done")
        kc_ready, bd_ready = sem("kc_ready"), sem("bd_ready")
        dve_step = sem("dve_step")

        block = ctx.enter_context(nc.Block())

        @block.gpsimd
        def _(pool):
            pool.memset(mask[:], 1.0).then_inc(mask_set, 1)
            for i in range(2):
                pool.memset(v[i][:, :, :, P:P + 1], 1.0).then_inc(const_set, 1)
            m = mask[:].rearrange("p (a b) -> p a b", b=D)
            pool.wait_ge(mask_set, 1)
            pool.affine_select(out=m, in_=m, compare_op=ALU.is_ge, fill=0.0, base=0, pattern=[[-D, P // D], [0, D]],
                               channel_multiplier=1).then_inc(mask_set, 1)
            pool.wait_ge(mask_set, 2)
            pool.affine_select(out=m, in_=m, compare_op=ALU.is_ge, fill=0.0, base=D - 1,
                               pattern=[[D, P // D], [0, D]], channel_multiplier=-1).then_inc(mask_set, 1)

        @block.sync
        def _(sp):
            sp.dma_start(wkv[:], io["wkv"]).then_inc(w_in, 16)
            for j in range(B // CG):
                if j >= 2:
                    sp.wait_ge(proj_done, CG * (j - 1))
                sp.dma_start(ct[j % 2][:], io["ctx_t"][:, :, j * CG * S:(j + 1) * CG * S]).then_inc(ct_in[j % 2], 16)
                if j == 0:
                    sp.dma_start(bk[:], io["bk"].partition_broadcast(ST)).then_inc(b_in, 16)
                    sp.dma_start(bv[:], io["bv"].partition_broadcast(P)).then_inc(b_in, 16)

        @block.vector
        def _(dve):
            steps = [0]

            def did(ins):
                ins.then_inc(dve_step, 1)
                steps[0] += 1
                return steps[0]

            def after(n):
                dve.wait_ge(dve_step, n)

            def heads(t):
                return t.rearrange("p t (h d) -> p (t h) d", d=D)

            def spread(t):
                return t[:].unsqueeze(2).broadcast_to([ST, STILES * H, D])

            def block_diagonals(s):
                ps = kvp[s % 2][:, 0:CB * (P + 1)].rearrange("p (b n) -> p b n", b=CB)
                dve.wait_ge(kc_ready, s + 1)
                if s:
                    dve.wait_ge(bd_ready, 2 * s)
                n = did(dve.tensor_tensor(kvm[:], ps[:, :, 0:P], mask[:].unsqueeze(1).broadcast_to([P, CB, P]), ALU.mult))
                for b in range(CB):
                    did(dve.tensor_scalar(kcbd[:, s, b, :], mask[:], kc[:, b:b + 1], None, ALU.mult))
                after(n)
                for b in range(CB):
                    dve.scalar_tensor_tensor(kvbd[:, s, b, :], bvm[:, b, :], kc[:, b:b + 1], kvm[:, b, :],
                                             ALU.mult, ALU.add).then_inc(bd_ready, 1)

            dve.wait_ge(mask_set, 3)
            dve.wait_ge(b_in, 32)
            dve.tensor_tensor(bvm[:], bv[:].rearrange("p (b c) -> p b c", b=CB),
                              mask[:].unsqueeze(1).broadcast_to([P, CB, P]), ALU.mult).then_inc(bvm_ready, 1)
            dve.wait_ge(bvm_ready, 1)
            for s in range(B):
                ks = k[s % 2]
                dve.wait_ge(v_ready, s + 1)
                if s >= 2:
                    dve.wait_ge(kv_done, s - 1)
                dve.tensor_tensor(ks[:], proj[s % 2][0:ST, :, 0:C], bk[:].unsqueeze(1).broadcast_to([ST, STILES, C]),
                                  ALU.add).then_inc(kbias_done, 1)
                dve.wait_ge(kbias_done, s + 1)
                n = did(dve.tensor_reduce(top[:], heads(ks[:]), AX.X, ALU.max))
                after(n)
                dve.tensor_tensor(heads(ks[:]), heads(ks[:]), spread(top), ALU.subtract).then_inc(arg_ready, 1)
                if s:
                    block_diagonals(s - 1)
                dve.wait_ge(exp_ready, s + 1)
                n = did(dve.tensor_reduce(total[:], heads(ks[:]), AX.X, ALU.add))
                after(n)
                n = did(dve.reciprocal(rec[:], total[:]))
                after(n)
                dve.tensor_tensor(heads(ks[:]), heads(ks[:]), spread(rec), ALU.mult).then_inc(k_ready, 1)
                dve.wait_ge(k_ready, s + 1)
            block_diagonals(B - 1)

        @block.scalar
        def _(act):
            act.wait_ge(const_set, 2)

            def sums_out(s):
                act.wait_ge(kv_done, s + 1)
                if s:
                    act.wait_ge(bd_ready, 2 * s)
                act.activation(kc[:], kvp[s % 2][:, P:2 * P + 2:P + 1], ACT.Copy).then_inc(kc_ready, 1)

            for s in range(B):
                act.wait_ge(proj_done, s + 1)
                if s >= 2:
                    act.wait_ge(kv_done, s - 1)
                act.activation(v[s % 2][:, :, :, 0:P], proj[s % 2][0:ST, :, C:2 * C].rearrange("p t (b c) -> p t b c", b=CB),
                               ACT.Copy).then_inc(v_ready, 1)
                if s:
                    sums_out(s - 1)
                act.wait_ge(arg_ready, s + 1)
                act.activation(k[s % 2][:], k[s % 2][:], ACT.Exp).then_inc(exp_ready, 1)
            sums_out(B - 1)

        @block.tensor
        def _(pe):
            def project(s):
                if s % CG == 0:
                    j = s // CG
                    pe.wait_ge(ct_in[j % 2], 16 * (j // 2 + 1))
                if s >= 2:
                    pe.wait_ge(kbias_done, s - 1)
                    pe.wait_ge(v_ready, s - 1)
                c0 = (s % CG) * S
                for t in range(STILES):
                    for b in range(CB):
                        ins = pe.matmul(proj[s % 2][0:ST, t, :], ct[(s // CG) % 2][:, b, c0 + t * ST:c0 + (t + 1) * ST],
                                        wkv[:, b, :], start=b == 0, stop=b == CB - 1)
                ins.then_inc(proj_done, 1)

            pe.wait_ge(w_in, 16)
            project(0)
            for s in range(B):
                if s + 1 < B:
                    project(s + 1)
                pe.wait_ge(k_ready, s + 1)
                pe.wait_ge(v_ready, s + 1)
                if s >= 2:
                    pe.wait_ge(bd_ready, 2 * (s - 1))
                for b in range(CB):
                    for t in range(STILES):
                        ins = pe.matmul(kvp[s % 2][:, b * (P + 1):(b + 1) * (P + 1)], k[s % 2][:, t, b * P:(b + 1) * P],
                                        v[s % 2][:, t, b, :], start=t == 0, stop=t == STILES - 1)
                ins.then_inc(kv_done, 1)

def attention_phase(nc, g, io):
    ctx = ExitStack()
    with ctx:
        def sb(name, shape, dt=FP32):
            return ctx.enter_context(nc.sbuf_tensor(name, shape, dt))

        def sem(name):
            return ctx.enter_context(nc.semaphore(name))

        x, ident, kvbd, kcbd = g["x"], g["ident"], g["kvbd"], g["kcbd"]
        wq, wp = sb("wq", [P, CB, C]), sb("wp", [P, CB, C])
        bq, bp = sb("bq", [T, C]), sb("bp", [T, C])
        eps = sb("eps3", [P, 1])
        xin = [sb(f"xin{i}", [T, G, C]) for i in range(2)]
        st = {k: sb(f"ast{k}", [T, G, 6]) for k in (1, 4)}
        mv = {k: sb(f"amv{k}", [T, G, 2]) for k in (1, 4)}
        lnv = {k: sb(f"alnv{k}", [T, G]) for k in (1, 4)}
        y0 = {k: sb(f"ay0{k}", [T, G]) for k in (1, 4)}
        yy = {k: sb(f"ayy{k}", [T, G]) for k in (1, 4)}
        rstd = {k: sb(f"arstd{k}", [T, G]) for k in (1, 4)}
        xt = sb("xt", [P, CB, G * T])
        q = sb("q", [T, G, C])
        top, total, rec = (sb(n, [T, G * H]) for n in ("qtop", "qtotal", "qrec"))
        qt = [sb(f"qt{i}", [P, CB, G * T]) for i in range(2)]
        rden = sb("rden", [P, CB, G * T])
        ot = sb("ot", [P, CB, G * T])
        pj = sb("pj", [T, G, C])
        bank = [ctx.enter_context(nc.psum_tensor(f"abank{i}", [P, 512], FP32)) for i in range(8)]

        w_in, eps_set = sem("aw_in"), sem("eps_set")
        xin_in = [sem(f"xin_in{i}") for i in range(2)]
        sum_done = sem("sum_done")
        lnstat = {k: sem(f"alnstat{k}") for k in (1, 4)}
        lnlog = {k: sem(f"alnlog{k}") for k in (1, 4)}
        lny0 = {k: sem(f"alny0{k}") for k in (1, 4)}
        x1_ready, x1_turned, xt_ready = sem("x1_ready"), sem("x1_turned"), sem("xt_ready")
        q_done, qbias_done, arg_ready, exp_ready, q_ready = (sem(n) for n in (
            "q_done", "qbias_done", "qarg_ready", "qexp_ready", "q_ready"))
        q_turned, qt_ready, num_done, den_done = sem("q_turned"), sem("qt_ready"), sem("num_done"), sem("den_done")
        den_read, ot_ready, pj_done, x2_ready = sem("den_read"), sem("ot_ready"), sem("pj_done"), sem("x2_ready")
        pj_read = sem("pj_read")
        dve_step = sem("adve_step")
        NS = GROUPS

        def valid(c):
            return 0 <= c < NS

        block = ctx.enter_context(nc.Block())

        @block.gpsimd
        def _(pool):
            pool.memset(eps[:], EPS).then_inc(eps_set, 1)

        @block.sync
        def _(sp):
            xv = io["x"].rearrange("b t c -> t b c")
            for c in range(NS):
                if c >= 2:
                    sp.wait_ge(sum_done, c - 1)
                sp.dma_start(xin[c % 2][:], xv[:, c * G:(c + 1) * G, :]).then_inc(xin_in[c % 2], 16)
                if c == 0:
                    sp.dma_start(wq[:], io["wq"]).then_inc(w_in, 16)
                    sp.dma_start(bq[:], io["bq"].partition_broadcast(T)).then_inc(w_in, 16)
                    sp.dma_start(wp[:], io["wp"]).then_inc(w_in, 16)
                    sp.dma_start(bp[:], io["bp"].partition_broadcast(T)).then_inc(w_in, 16)
            for h in range(2):
                load_half(sp, g["raw"][h], io, 0, h, g["raw_in"][h])
            for c in range(NS):
                sp.wait_ge(x2_ready, c + 1)
                sp.dma_start(io["x2"].rearrange("(s t) c -> t s c", t=T)[:, c * G:(c + 1) * G, :],
                             x[:, c * G:(c + 1) * G, :]).then_inc(g["x2_kept"], 16)

        @block.vector
        def _(dve):
            steps = [0]

            def did(ins):
                ins.then_inc(dve_step, 1)
                steps[0] += 1
                return steps[0]

            def after(n):
                dve.wait_ge(dve_step, n)

            def chunk(c):
                return x[:, c * G:(c + 1) * G, :]

            def tiles(i):
                return bank[i][0:T, :].rearrange("p (g c) -> p g c", c=C)

            def over_tokens(t, n):
                return t[:].unsqueeze(1).broadcast_to([T, n, C])

            def heads(t):
                return t.rearrange("p g (h d) -> p (g h) d", d=D)

            def spread(t):
                return t[:].unsqueeze(2).broadcast_to([T, G * H, D])

            def layernorm(k, c, out, done):
                xc = chunk(c)
                for i in range(G):
                    n = did(dve.bn_stats(st[k][:, i, :], xc[:, i, :]))
                after(n)
                for i in range(G):
                    last = dve.bn_aggr(mv[k][:, i, :], st[k][:, i, :])
                    if i < G - 1:
                        did(last)
                last.then_inc(lnstat[k], 1)
                dve.wait_ge(lny0[k], c + 1)
                after(did(dve.tensor_tensor(yy[k][:], y0[k][:], y0[k][:], ALU.mult)))
                after(did(dve.scalar_tensor_tensor(yy[k][:], mv[k][:, :, 1], EPS, yy[k][:], ALU.add, ALU.mult)))
                after(did(dve.tensor_scalar(yy[k][:], yy[k][:], -0.5, 1.5, ALU.mult, ALU.add)))
                after(did(dve.tensor_tensor(rstd[k][:], yy[k][:], y0[k][:], ALU.mult)))
                for i in range(G):
                    last = dve.tensor_scalar(out[:, i, :], xc[:, i, :], mv[k][:, i, 0:1], rstd[k][:, i:i + 1],
                                             ALU.subtract, ALU.mult)
                    if i < G - 1:
                        did(last)
                last.then_inc(done, 1)

            def make_x1(c):
                dve.wait_ge(xin_in[c % 2], 16 * (c // 2 + 1))
                dve.tensor_tensor(chunk(c), chunk(c), xin[c % 2][:], ALU.add).then_inc(sum_done, 1)
                dve.wait_ge(sum_done, c + 1)
                layernorm(1, c, chunk(c), x1_ready)

            def q_softmax(c):
                if c:
                    dve.wait_ge(q_turned, CB * c)
                for i in range(2):
                    dve.wait_ge(q_done, 2 * c + i + 1)
                    dve.tensor_tensor(q[:, 2 * i:2 * i + 2, :], tiles(2 + i), over_tokens(bq, 2), ALU.add)\
                        .then_inc(qbias_done, 1)
                dve.wait_ge(qbias_done, 2 * c + 2)
                after(did(dve.tensor_reduce(top[:], heads(q[:]), AX.X, ALU.max)))
                dve.tensor_tensor(heads(q[:]), heads(q[:]), spread(top), ALU.subtract).then_inc(arg_ready, 1)
                dve.wait_ge(exp_ready, c + 1)
                after(did(dve.tensor_reduce(total[:], heads(q[:]), AX.X, ALU.add)))
                after(did(dve.reciprocal(rec[:], total[:])))
                dve.tensor_tensor(heads(q[:]), heads(q[:]), spread(rec), ALU.mult).then_inc(q_ready, 1)

            def attend(c):
                for b in range(CB):
                    dve.wait_ge(den_done, CB * c + b + 1)
                    if c:
                        dve.wait_ge(ot_ready, CB * c)
                    dve.reciprocal(rden[:, b, :], bank[b][:, 0:G * T]).then_inc(den_read, 1)
                n = [0] * CB
                for b in range(CB):
                    dve.wait_ge(den_read, CB * c + b + 1)
                    dve.wait_ge(num_done, CB * c + b + 1)
                    n[b] = did(dve.tensor_tensor(rden[:, b, :], rden[:, b, :], bank[6 + b][:, 0:G * T], ALU.mult))
                for b in range(CB):
                    after(n[b])
                    if c:
                        dve.wait_ge(pj_done, 2 * c)
                    dve.tensor_tensor(ot[:, b, :], rden[:, b, :], qt[c % 2][:, b, :], ALU.add).then_inc(ot_ready, 1)

            def make_x2(c):
                xc = chunk(c)
                if c:
                    dve.wait_ge(x2_ready, c)
                for i in range(2):
                    dve.wait_ge(pj_done, 2 * c + i + 1)
                    dve.tensor_tensor(pj[:, 2 * i:2 * i + 2, :], tiles(4 + i), over_tokens(bp, 2), ALU.add)\
                        .then_inc(pj_read, 1)
                dve.wait_ge(pj_read, 2 * c + 2)
                after(did(dve.tensor_tensor(xc, xc, pj[:], ALU.add)))
                layernorm(4, c, xc, x2_ready)

            dve.wait_ge(w_in, 64)
            for s in range(NS + 3):
                if valid(s):
                    make_x1(s)
                if valid(s - 2):
                    attend(s - 2)
                if valid(s - 1):
                    q_softmax(s - 1)
                if valid(s - 3):
                    make_x2(s - 3)

        @block.scalar
        def _(act):
            def rsqrt0(k, c):
                act.wait_ge(lnstat[k], c + 1)
                act.activation(lnv[k][:], mv[k][:, :, 1], ACT.Ln, bias=eps[0:T, :]).then_inc(lnlog[k], 1)
                act.wait_ge(lnlog[k], c + 1)
                act.activation(y0[k][:], lnv[k][:], ACT.Exp, scale=-0.5).then_inc(lny0[k], 1)

            act.preload_act_table_set("natural_log_exp_and_others")
            act.wait_ge(eps_set, 1)
            for s in range(NS + 3):
                c = s - 1
                if valid(s):
                    rsqrt0(1, s)
                if valid(c):
                    act.wait_ge(arg_ready, c + 1)
                    act.activation(q[:], q[:], ACT.Exp).then_inc(exp_ready, 1)
                if valid(s):
                    for b in range(CB):
                        act.wait_ge(x1_turned, CB * s + b + 1)
                        act.activation(xt[:, b, :], bank[b][:, 0:G * T], ACT.Copy).then_inc(xt_ready, 1)
                if valid(c):
                    for b in range(CB):
                        act.wait_ge(q_turned, CB * c + b + 1)
                        act.activation(qt[c % 2][:, b, :], bank[4 + b][:, 0:G * T], ACT.Copy).then_inc(qt_ready, 1)
                if valid(s - 3):
                    rsqrt0(4, s - 3)

        @block.tensor
        def _(pe):
            def turn(src, first_bank, done):
                for b in range(CB):
                    for i in range(G):
                        ins = pe.transpose(bank[first_bank + b][:, i * T:(i + 1) * T], src[:, i, b * P:(b + 1) * P],
                                           ident[0:T, 0:T])
                    ins.then_inc(done, 1)

            def tokens_out(first_bank, src, w, done):
                for i in range(G):
                    for b in range(CB):
                        ins = pe.matmul(bank[first_bank + i // 2][0:T, (i % 2) * C:(i % 2 + 1) * C],
                                        src[:, b, i * T:(i + 1) * T], w[:, b, :], start=b == 0, stop=b == CB - 1)
                    if i % 2:
                        ins.then_inc(done, 1)

            pe.wait_ge(w_in, 64)
            for s in range(NS + 3):
                if valid(s):
                    if s >= 2:
                        pe.wait_ge(den_read, CB * (s - 1))
                    pe.wait_ge(x1_ready, s + 1)
                    turn(x[:, s * G:(s + 1) * G, :], 0, x1_turned)
                c = s - 1
                if valid(c) and valid(s):
                    pe.wait_ge(qbias_done, 2 * s)
                if valid(s):
                    pe.wait_ge(xt_ready, CB * (s + 1))
                    tokens_out(2, xt, wq, q_done)
                if valid(c):
                    pe.wait_ge(q_ready, c + 1)
                    if c >= 2:
                        pe.wait_ge(pj_read, 2 * (c - 1))
                    turn(q, 4, q_turned)
                    pe.wait_ge(qt_ready, CB * (c + 1))
                    if c:
                        pe.wait_ge(ot_ready, CB * c)
                    if not valid(s):
                        pe.wait_ge(xt_ready, CB * NS)
                    for mat, first_bank, done in ((kcbd, 0, den_done), (kvbd, 6, num_done)):
                        for b in range(CB):
                            for i in range(G):
                                ins = pe.matmul(bank[first_bank + b][:, i * T:(i + 1) * T], mat[:, c * G + i, b, :],
                                                qt[c % 2][:, b, i * T:(i + 1) * T], start=True, stop=True)
                            ins.then_inc(done, 1)
                c = s - 2
                if valid(c):
                    pe.wait_ge(ot_ready, CB * (c + 1))
                    if not valid(s - 1):
                        pe.wait_ge(qt_ready, CB * NS)
                        pe.wait_ge(pj_read, 2 * c)
                    tokens_out(4, ot, wp, pj_done)

def expert_phase(nc, g, io):
    ctx = ExitStack()
    with ctx:
        def sb(name, shape, dt=FP32):
            return ctx.enter_context(nc.sbuf_tensor(name, shape, dt))

        def sem(name):
            return ctx.enter_context(nc.semaphore(name))

        x, ident, raw, raw_in, x2_kept = g["x"], g["ident"], g["raw"], g["raw_in"], g["x2_kept"]
        wrt = sb("wrt", [P, CB, 2 * E])
        eps = sb("eps4", [P, 1])
        xh, xl = sb("xh", [P, CB, N], F32R), sb("xl", [P, CB, N], F32R)
        logit = sb("logit", [P, 2, TILES, E])
        top, total, rec = (sb(n, [P, 2 * TILES]) for n in ("ltop", "ltotal", "lrec"))
        cw = sb("cw", [P, E, TILES])
        cws, cwr = sb("cws", [P, TILES]), sb("cwr", [P, TILES])
        wh = [sb(f"wh{i}", [P, WH], F32R) for i in range(2)]
        wl = [sb(f"wl{i}", [P, WH], F32R) for i in range(2)]
        sil = [sb(f"sil{i}", [P, COLS]) for i in range(2)]
        hf = [sb(f"hf{i}", [P, COLS]) for i in range(2)]
        hh = [sb(f"hh{i}", [P, FB, COLS], F32R) for i in range(2)]
        hl = [sb(f"hl{i}", [P, FB, COLS], F32R) for i in range(2)]
        acc = sb("acc", [P, TILES, C])
        xt = acc[:].rearrange("p k c -> p (k c)").rearrange("p (b n) -> p b n", b=CB)
        xk = sb("xk", [P, TILES, C])
        st, mv = sb("fst", [P, 4, 6]), sb("fmv", [P, 4, 2])
        lnv, y0, yy, rstd = (sb(n, [P, 4]) for n in ("flnv", "fy0", "fyy", "frstd"))
        bank = [ctx.enter_context(nc.psum_tensor(f"fbank{i}", [P, 512], FP32)) for i in range(8)]

        r_in, eps_set, xk_in = sem("r_in"), sem("feps_set"), sem("xk_in")
        x_turned, xt_ready, xh_ready, xl_ready = sem("x_turned"), sem("fxt_ready"), sem("xh_ready"), sem("xl_ready")
        r_done, logit_ready = sem("r_done"), sem("logit_ready")
        larg_ready, lexp_ready, cw_ready = sem("larg_ready"), sem("lexp_ready"), sem("cw_ready")
        wh_ready, wl_ready = sem("wh_ready"), sem("wl_ready")
        gu_done, sil_ready, hf_ready, hh_ready, hl_ready = (sem(n) for n in (
            "gu_done", "sil_ready", "hf_ready", "hh_ready", "hl_ready"))
        down_done, acc_done = sem("down_done"), sem("acc_done")
        lnstat, lnlog, lny0, out_ready, out_stored = (sem(n) for n in (
            "flnstat", "flnlog", "flny0", "out_ready", "out_stored"))
        dve_step = sem("fdve_step")

        GATE, UP, DOWN = 0, CB * FB * P, 2 * CB * FB * P
        STEPS_E = 2 * GROUPS
        HID_E = STEPS_E * FB
        DOWN_E = TILES
        ACC_E = 2 * TILES
        SPLIT_E = 6

        def columns(c):
            return slice(c * COLS, min((c + 1) * COLS, N))

        def tiles(c):
            return range(c * COLS // P, min((c + 1) * COLS, N) // P)

        def downs(t):
            return t // GROUPS * (TILES // 2) + 2 * (t % GROUPS)

        def accs(t):
            return t // GROUPS * TILES + 4 * (t % GROUPS)

        def reached(engine, semaphore, count):
            if not isinstance(count, int) or count > 0:
                engine.wait_ge(semaphore, count)

        def part(w, j):
            return w[:, j * UP:(j + 1) * UP]

        def following(e, h):
            return (e, 1) if h == 0 else (e + 1, 0)

        def experts(engine, body):
            body(0)
            with engine.Fori(1, E - 1) as e:
                body(e)
            body(E - 1)

        block = ctx.enter_context(nc.Block())

        @block.gpsimd
        def _(pool):
            pool.memset(eps[:], EPS).then_inc(eps_set, 1)

        @block.sync
        def _(sp):
            sp.dma_start(wrt[:], io["wrt"]).then_inc(r_in, 16)
            with sp.Fori(1, E) as e:
                for h in range(2):
                    sp.wait_ge(wh_ready, SPLIT_E * e - SPLIT_E + 3 * h + 3)
                    sp.wait_ge(wl_ready, SPLIT_E * e - SPLIT_E + 3 * h + 3)
                    load_half(sp, raw[h], io, e, h, raw_in[h])
            sp.wait_ge(x2_kept, 16 * GROUPS)
            sp.dma_start(xk[:], io["x2"].rearrange("(k p) c -> p k c", p=P)).then_inc(xk_in, 16)
            for c in range(GROUPS):
                k = slice(tiles(c).start, tiles(c).stop)
                sp.wait_ge(out_ready, c + 1)
                sp.dma_start(io["out"].rearrange("b t c -> (b t) c").rearrange("(k p) c -> p k c", p=P)[:, k, :],
                             acc[:, k, :]).then_inc(out_stored, 16)
            sp.wait_ge(out_stored, 16 * GROUPS)

        @block.vector
        def _(dve):
            steps = [0]

            def did(ins):
                ins.then_inc(dve_step, 1)
                steps[0] += 1
                return steps[0]

            def after(n):
                dve.wait_ge(dve_step, n)

            def split_x(c):
                cols = slice(c * G * T, (c + 1) * G * T)
                dve.wait_ge(xt_ready, CB * (c + 1))
                after(did(dve.tensor_copy(xh[:, :, cols], xt[:, :, cols])))
                dve.tensor_tensor(xl[:, :, cols], xt[:, :, cols], xh[:, :, cols], ALU.subtract).then_inc(xl_ready, 1)

            def low_weights(e, h, j):
                reached(dve, wh_ready, e * SPLIT_E + 3 * h + j + 1)
                reached(dve, down_done, e * DOWN_E + downs(h * GROUPS - GROUPS))
                dve.tensor_tensor(part(wl[h], j), part(raw[h], j), part(wh[h], j), ALU.subtract).then_inc(wl_ready, 1)

            def combine_weights():
                lf = logit[:].rearrange("p w k e -> p (w k) e")
                ct = cw[:].rearrange("p e k -> p k e")
                dve.wait_ge(logit_ready, 1)
                after(did(dve.tensor_scalar(logit[:, 1], logit[:, 1], 1.0 / GATE_TEMP, None, ALU.mult)))
                after(did(dve.tensor_reduce(top[:], lf, AX.X, ALU.max)))
                dve.tensor_tensor(lf, lf, top[:].unsqueeze(2).broadcast_to([P, 2 * TILES, E]), ALU.subtract)\
                    .then_inc(larg_ready, 1)
                dve.wait_ge(lexp_ready, 1)
                after(did(dve.tensor_reduce(total[:], lf, AX.X, ALU.add)))
                after(did(dve.reciprocal(rec[:], total[:])))
                after(did(dve.tensor_tensor(lf, lf, rec[:].unsqueeze(2).broadcast_to([P, 2 * TILES, E]), ALU.mult)))
                after(did(dve.tensor_tensor(ct, logit[:, 0], logit[:, 1], ALU.mult)))
                after(did(dve.tensor_reduce(cws[:], ct, AX.X, ALU.add)))
                after(did(dve.tensor_scalar(cws[:], cws[:], 1e-9, None, ALU.add)))
                after(did(dve.reciprocal(cwr[:], cws[:])))
                dve.tensor_tensor(ct, ct, cwr[:].unsqueeze(2).broadcast_to([P, TILES, E]), ALU.mult)\
                    .then_inc(cw_ready, 1)
                dve.wait_ge(cw_ready, 1)

            def times_up(e, t, f):
                n, i = t * FB + f, f % 2
                w = columns(t % GROUPS).stop - columns(t % GROUPS).start
                dve.wait_ge(sil_ready, e * HID_E + n + 1)
                dve.wait_ge(gu_done, e * (2 * HID_E) + 2 * n + 2)
                reached(dve, hh_ready, e * HID_E + n - 1)
                reached(dve, hl_ready, e * HID_E + n - 1)
                dve.tensor_tensor(hf[i][:, 0:w], sil[i][:, 0:w], bank[2 * i + 1][:, 0:w], ALU.mult).then_inc(hf_ready, 1)

            def low_h(e, n):
                t, f = n // FB, n % FB
                w = columns(t % GROUPS).stop - columns(t % GROUPS).start
                dve.wait_ge(hh_ready, e * HID_E + n + 1)
                dve.tensor_tensor(hl[t % 2][:, f, 0:w], hf[f % 2][:, 0:w], hh[t % 2][:, f, 0:w], ALU.subtract)\
                    .then_inc(hl_ready, 1)

            def accumulate(e, t, start):
                for i, k in enumerate(tiles(t % GROUPS)):
                    if i % 2 == 0:
                        dve.wait_ge(down_done, e * DOWN_E + downs(t) + i // 2 + 1)
                    ps = bank[4 + 2 * (t % 2) + i // 2][:, (i % 2) * C:(i % 2 + 1) * C]
                    own = e if t >= 0 else e - 1
                    a, w = acc[:, k, :], cw[:, own, k:k + 1]
                    if start:
                        ins = dve.tensor_scalar(a, ps, w, None, ALU.mult)
                    else:
                        if i == 0:
                            dve.wait_ge(acc_done, e * ACC_E + accs(t - GROUPS + 1))
                        ins = dve.scalar_tensor_tensor(a, ps, w, a, ALU.mult, ALU.add)
                    ins.then_inc(acc_done, 1)

            def expert(e):
                for t in range(STEPS_E):
                    for f in range(FB):
                        n = t * FB + f
                        times_up(e, t, f)
                        if n or not isinstance(e, int) or e:
                            low_h(e, n - 1)
                        if f == 1 and t % GROUPS and not (isinstance(e, int) and e == E - 1 and t > GROUPS):
                            e_, h_ = following(e, t // GROUPS)
                            low_weights(e_, h_, t % GROUPS - 1)
                        if f == FB - 1 and (t >= 2 or not isinstance(e, int) or e):
                            accumulate(e, t - 2, isinstance(e, int) and e == 0 and t - 2 < GROUPS)
                if isinstance(e, int) and e == E - 1:
                    low_h(e, HID_E - 1)
                    accumulate(e, STEPS_E - 2, False)
                    accumulate(e, STEPS_E - 1, False)

            def final_norm(c):
                k0, k1 = tiles(c).start, tiles(c).stop
                n = k1 - k0
                xc, ac = xk[:, k0:k1, :], acc[:, k0:k1, :]
                dve.wait_ge(acc_done, (E - 1) * ACC_E + accs(STEPS_E - GROUPS + c) + n)
                after(did(dve.tensor_tensor(xc, xc, ac, ALU.add)))
                for i in range(n):
                    last = did(dve.bn_stats(st[:, i, :], xc[:, i, :]))
                after(last)
                for i in range(n):
                    last = dve.bn_aggr(mv[:, i, :], st[:, i, :])
                    if i < n - 1:
                        did(last)
                last.then_inc(lnstat, 1)
                dve.wait_ge(lny0, c + 1)
                after(did(dve.tensor_tensor(yy[:, 0:n], y0[:, 0:n], y0[:, 0:n], ALU.mult)))
                after(did(dve.scalar_tensor_tensor(yy[:, 0:n], mv[:, 0:n, 1], EPS, yy[:, 0:n], ALU.add, ALU.mult)))
                after(did(dve.tensor_scalar(yy[:, 0:n], yy[:, 0:n], -0.5, 1.5, ALU.mult, ALU.add)))
                after(did(dve.tensor_tensor(rstd[:, 0:n], yy[:, 0:n], y0[:, 0:n], ALU.mult)))
                for i in range(n):
                    last = dve.tensor_scalar(ac[:, i, :], xc[:, i, :], mv[:, i, 0:1], rstd[:, i:i + 1],
                                             ALU.subtract, ALU.mult)
                    if i < n - 1:
                        did(last)
                last.then_inc(out_ready, 1)
                dve.wait_ge(out_ready, c + 1)

            for c in range(GROUPS):
                split_x(c)
            for j in range(3):
                low_weights(0, 0, j)
            combine_weights()
            experts(dve, expert)
            dve.wait_ge(xk_in, 16)
            for c in range(GROUPS):
                final_norm(c)

        @block.scalar
        def _(act):
            def high_weights(e, h, j):
                if j == 0:
                    act.wait_ge(raw_in[h], 48 * e + 48)
                reached(act, down_done, e * DOWN_E + downs(h * GROUPS - GROUPS))
                act.activation(part(wh[h], j), part(raw[h], j), ACT.Copy).then_inc(wh_ready, 1)

            def high_h(e, n):
                t, f = n // FB, n % FB
                w = columns(t % GROUPS).stop - columns(t % GROUPS).start
                if f == 0:
                    reached(act, down_done, e * DOWN_E + downs(t - 1))
                act.wait_ge(hf_ready, e * HID_E + n + 1)
                act.activation(hh[t % 2][:, f, 0:w], hf[f % 2][:, 0:w], ACT.Copy).then_inc(hh_ready, 1)

            def expert(e):
                for t in range(STEPS_E):
                    w = columns(t % GROUPS).stop - columns(t % GROUPS).start
                    for f in range(FB):
                        n = t * FB + f
                        act.wait_ge(gu_done, e * (2 * HID_E) + 2 * n + 1)
                        reached(act, hf_ready, e * HID_E + n - 1)
                        act.activation(sil[f % 2][:, 0:w], bank[2 * (f % 2)][:, 0:w], ACT.Silu).then_inc(sil_ready, 1)
                        if n or not isinstance(e, int) or e:
                            high_h(e, n - 1)
                        if f == 1 and t % GROUPS and not (isinstance(e, int) and e == E - 1 and t > GROUPS):
                            e_, h_ = following(e, t // GROUPS)
                            high_weights(e_, h_, t % GROUPS - 1)

            act.preload_act_table_set(LN_EXP)
            for c in range(GROUPS):
                for b in range(CB):
                    act.wait_ge(x_turned, CB * c + b + 1)
                    act.activation(xt[:, b, c * G * T:(c + 1) * G * T], bank[2 * (c % 2) + b][:, 0:G * T], ACT.Copy)\
                        .then_inc(xt_ready, 1)
            for j in range(3):
                high_weights(0, 0, j)
            act.wait_ge(r_done, 1)
            act.activation(logit[:].rearrange("p w k e -> p k w e"),
                           bank[4][:, 0:TILES * 2 * E].rearrange("p (k w e) -> p k w e", w=2, e=E), ACT.Copy)\
                .then_inc(logit_ready, 1)
            act.wait_ge(larg_ready, 1)
            lf = logit[:].rearrange("p w k e -> p (w k e)")
            act.activation(lf, lf, ACT.Exp).then_inc(lexp_ready, 1)
            experts(act, expert)
            high_h(E - 1, HID_E - 1)
            act.wait_ge(eps_set, 1)
            for c in range(GROUPS):
                n = len(tiles(c))
                act.wait_ge(lnstat, c + 1)
                act.activation(lnv[:, 0:n], mv[:, 0:n, 1], ACT.Ln, bias=eps[:]).then_inc(lnlog, 1)
                act.wait_ge(lnlog, c + 1)
                act.activation(y0[:, 0:n], lnv[:, 0:n], ACT.Exp, scale=-0.5).then_inc(lny0, 1)

        @block.tensor
        def _(pe):
            def gate_up(e, t):
                h, c = t // GROUPS, t % GROUPS
                w = columns(c).stop - columns(c).start
                if c == 0:
                    pe.wait_ge(wl_ready, e * SPLIT_E + 3 * h + 3)
                if isinstance(e, int) and e == 0 and h == 0:
                    pe.wait_ge(xl_ready, -(-columns(c).stop // (G * T)))
                for f in range(FB):
                    reached(pe, hf_ready, e * HID_E + t * FB + f - 1)
                    for k, w0 in ((0, GATE), (1, UP)):
                        n = 0
                        for a, m in ((xh, wh), (xl, wh), (xh, wl)):
                            for b in range(CB):
                                o = w0 + b * FB * P + f * P
                                ins = pe.matmul(bank[2 * (f % 2) + k][:, 0:w], m[h][:, o:o + P], a[:, b, columns(c)],
                                                start=n == 0, stop=n == 3 * CB - 1)
                                n += 1
                        ins.then_inc(gu_done, 1)

            def down(e, t):
                h = t // GROUPS % 2
                reached(pe, acc_done, e * ACC_E + accs(t - 1))
                for i, k in enumerate(tiles(t % GROUPS)):
                    n = 0
                    for f in range(FB):
                        if i == 0:
                            pe.wait_ge(hl_ready, e * HID_E + t * FB + f + 1)
                        for a, m in ((hh, wh), (hh, wl), (hl, wh)):
                            ins = pe.matmul(bank[4 + 2 * (t % 2) + i // 2][:, (i % 2) * C:(i % 2 + 1) * C],
                                            a[t % 2][:, f, i * P:(i + 1) * P],
                                            m[h][:, DOWN + f * C:DOWN + (f + 1) * C], start=n == 0,
                                            stop=n == 3 * FB - 1)
                            n += 1
                    if i % 2:
                        ins.then_inc(down_done, 1)

            def expert(e):
                for t in range(STEPS_E):
                    gate_up(e, t)
                    if t or not isinstance(e, int) or e:
                        down(e, t - 1)

            for c in range(GROUPS):
                if c >= 2:
                    pe.wait_ge(xt_ready, CB * (c - 1))
                for b in range(CB):
                    for i in range(G):
                        ins = pe.transpose(bank[2 * (c % 2) + b][:, i * T:(i + 1) * T],
                                           x[:, c * G + i, b * P:(b + 1) * P], ident[0:T, 0:T])
                    ins.then_inc(x_turned, 1)
            pe.wait_ge(r_in, 16)
            pe.wait_ge(xt_ready, CB * GROUPS)
            for k in range(TILES):
                for b in range(CB):
                    ins = pe.matmul(bank[4][:, k * 2 * E:(k + 1) * 2 * E], xt[:, b, k * P:(k + 1) * P], wrt[:, b, :],
                                    start=b == 0, stop=b == CB - 1)
            ins.then_inc(r_done, 1)
            experts(pe, expert)
            down(E - 1, STEPS_E - 1)

def build(nc, io):
    with ExitStack() as ctx:
        g = {
            "x": ctx.enter_context(nc.sbuf_tensor("x", [T, B, C], FP32)),
            "ident": ctx.enter_context(nc.sbuf_tensor("ident", [P, P], FP32)),
            "raw_in": [ctx.enter_context(nc.semaphore(f"raw_in{i}")) for i in range(2)],
            "x2_kept": ctx.enter_context(nc.semaphore("x2_kept")),
        }
        rwkv_phase(nc, g, io)
        g["raw"] = [ctx.enter_context(nc.sbuf_tensor(f"raw{i}", [P, WH], FP32)) for i in range(2)]
        with ExitStack() as held:
            for n in ("kvbd", "kcbd"):
                g[n] = held.enter_context(nc.sbuf_tensor(n, [P, B, CB, P], FP32))
            context_phase(nc, g, io)
            attention_phase(nc, g, io)
        expert_phase(nc, g, io)

def lay_out(inputs):
    import numpy as np

    def rows(w):
        *lead, k, n = w.shape
        return np.ascontiguousarray(np.moveaxis(w.reshape(*lead, k // P, P, n), -3, -2))

    a = {k.removeprefix("L0_"): np.asarray(v) for k, v in inputs.items()}
    out = {"x": a["x"], "ln0_w": a["attn_ln0_w"], "ln0_b": a["attn_ln0_b"]}
    for n, name in (("k", "Wk"), ("v", "Wv"), ("r", "Wr"), ("o", "Wo"), ("ck", "Wck"), ("cr", "Wcr"), ("cv", "Wcv")):
        out["w_" + n] = rows(np.swapaxes(a["attn_" + name], -1, -2))
    prm = [a["attn_" + n] for n in ("ln1_w", "ln1_b", "tmk", "tmv", "tmr", "time_decay", "time_first", "ln2_w",
                                    "ln2_b", "cmk", "cmr")]
    out["prm"] = np.ascontiguousarray(np.stack(prm).reshape(len(prm), L, CB, P).transpose(3, 1, 2, 0))
    out["ctx_t"] = np.ascontiguousarray(a["ctx_1024"].reshape(B * S, CB, P).transpose(2, 1, 0))
    out["wkv"] = np.concatenate([rows(a["xattn_Wk"].T), rows(a["xattn_Wv"].T)], axis=-1)
    out["wq"], out["wp"] = rows(a["xattn_Wq"].T), rows(a["xattn_Wp"].T)
    for n in "kvqp":
        out["b" + n] = a["xattn_b" + n]
    out["wrt"] = np.concatenate([rows(a["ffn_w_router"]), rows(a["ffn_w_gating"])], axis=-1)
    for n in ("w_gate", "w_up", "w_down"):
        out[n] = a["ffn_" + n]
    return out

def kernel(**inputs):
    import concourse.bacc as bacc
    from concourse.bass_utils import run_bass_kernel_spmd

    nc = bacc.Bacc("TRN2", target_bir_lowering=False, num_devices=1)
    arrays = lay_out(inputs)
    io = {n: nc.dram_tensor(f"in_{n}", a.shape, mybir.dt.from_np(a.dtype), kind="ExternalInput").ap()
          for n, a in arrays.items()}
    io["x2"] = nc.dram_tensor("x2_kept", (N, C), FP32, kind="Internal").ap()
    io["out"] = nc.dram_tensor("out_x", (B, T, C), FP32, kind="ExternalOutput").ap()
    build(nc, io)
    r = run_bass_kernel_spmd(nc, [{f"in_{n}": a for n, a in arrays.items()}], core_ids=[0])
    return r.results[0]["out_x"]
```

```python
from contextlib import ExitStack

import concourse.bass as bass
from concourse import mybir
from concourse.alu_op_type import AluOpType as ALU

FP32 = mybir.dt.float32
F32R = mybir.dt.float32r
ACT = mybir.ActivationFunctionType
AX = mybir.AxisListType

P = 128
B, T, C = 16, 112, 256
L, F = 4, 1024
CB = C // P
G = 4
GROUPS = B // G
STEPS = L * GROUPS
T1 = T + 1
EPS = 1e-5
NEVER = -1e38
LN_EXP, EXP_TANH = "natural_log_exp_and_others", "exp_and_others"
SPLIT = 2
NAMES = ["ln1w", "ln1b", "tmk", "tmv", "tmr", "td", "u", "ln2w", "ln2b", "cmk", "cmr", "w"]
PRM = {n: i for i, n in enumerate(NAMES)}
NPRM = len(NAMES)
S = 375
STILES = 3
ST = S // STILES
CG = 2
H, D = 16, 16
E = 8
FB = F // P // 2
WH = 2 * CB * FB * P + FB * C
GATE_TEMP = 0.1
N = B * T
TILES = N // P
COLS = 512

GATE, UP, DOWN = 0, CB * FB * P, 2 * CB * FB * P

def part(w, j):
    return w[:, j * UP:(j + 1) * UP]

def route(pe, out, g, tiles):
    for i, k in enumerate(tiles):
        for b in range(CB):
            ins = pe.matmul(out[:, i * 2 * E:(i + 1) * 2 * E], g["x2t"][:, b, k * P:(k + 1) * P], g["wrt"][:, b, :],
                            start=b == 0, stop=b == CB - 1)
    ins.then_inc(g["r_done"], 1)

def logits_out(act, out, g, tiles):
    act.activation(g["logit"][:, :, tiles.start:tiles.stop, :].rearrange("p w k e -> p k w e"),
                   out[:, 0:len(tiles) * 2 * E].rearrange("p (k w e) -> p k w e", w=2, e=E), ACT.Copy)\
        .then_inc(g["logit_ready"], 1)

EARLY = range((GROUPS - 1) * G * T // P)
LATE = range(EARLY.stop, TILES)

def load_half(engine, raw, io, e, h, loaded):
    f = slice(h * FB * P, (h + 1) * FB * P)
    for j, name in enumerate(("w_gate", "w_up")):
        w = io[name].rearrange("e (b p) f -> p e b f", p=P)
        engine.dma_start(raw[:, j * CB * FB * P:(j + 1) * CB * FB * P].rearrange("p (b f) -> p b f", b=CB),
                         w[:, e, :, f]).then_inc(loaded, 16)
    w = io["w_down"].rearrange("e (f p) c -> p e f c", p=P)
    engine.dma_start(raw[:, 2 * CB * FB * P:WH].rearrange("p (f c) -> p f c", f=FB),
                     w[:, e, h * FB:(h + 1) * FB, :]).then_inc(loaded, 16)

def load_context(engine, io, ct, ct_in, j):
    engine.dma_start(ct[j % 2], io["ctx_t"][:, :, j * CG * S:(j + 1) * CG * S]).then_inc(ct_in[j % 2], 16)

def rwkv_phase(nc, g, io):
    ctx = ExitStack()
    with ctx:
        def sb(name, shape, dt=FP32):
            return ctx.enter_context(nc.sbuf_tensor(name, shape, dt))

        def sem(name):
            return ctx.enter_context(nc.semaphore(name))

        x = g["x"]
        ident = g["ident"]
        wk, wv, wr, wo, wcr = (sb(n, [P, CB, C]) for n in ("wk", "wv", "wr", "wo", "wcr"))
        stage = g["stage"]
        wckh, wckl = sb("wckh", [P, CB * F], F32R), sb("wckl", [P, CB * F], F32R)
        wcvh, wcvl = sb("wcvh", [P, SPLIT * C], F32R), sb("wcvl", [P, SPLIT * C], F32R)
        wcv = sb("wcv", [P, (F // P - SPLIT) * C])
        prm = sb("prm", [P, L, CB, NPRM])
        ln0w, ln0b = sb("ln0w", [T, C]), sb("ln0b", [T, C])
        eps = sb("eps", [P, 1])
        xn = {1: sb("xn1", [T, G, C]), 2: sb("xn2", [T, G, C])}
        st = {k: sb(f"st{k}", [T, G, 6]) for k in (0, 1, 2)}
        mv = {k: sb(f"mv{k}", [T, G, 2]) for k in (0, 1, 2)}
        lnv = {k: sb(f"lnv{k}", [T, G]) for k in (0, 1, 2)}
        y0 = {k: sb(f"y0{k}", [T, G]) for k in (0, 1, 2)}
        yy = {k: sb(f"yy{k}", [T, G]) for k in (0, 1, 2)}
        rstd = {k: sb(f"rstd{k}", [T, G]) for k in (0, 1, 2)}
        shift = sb("shift", [T, G])
        h = {1: sb("h1", [P, CB, G, T1]), 2: sb("h2", [P, CB, G, T1])}
        diff = sb("diff", [P, CB, G, T])
        mixed = {n: sb("mix_" + n, [P, CB, G, T]) for n in ("k", "v", "r", "ck", "cr")}
        kp = sb("kp", [P, CB, G, T1])
        v = sb("v", [P, CB, G, T])
        th = sb("th", [P, CB, G, T])
        pp = sb("pp", [P, CB, G, T1])
        reset = sb("reset", [P, G, T1])
        decay = sb("decay", [P, CB, G, T1])
        dp, dk = sb("dp", [P, CB, G, T]), sb("dk", [P, CB, G, T])
        rw = [sb(f"rw{i}", [P, CB, G, T]) for i in range(2)]
        e1, e2 = sb("e1", [P, CB, G, T]), sb("e2", [P, CB, G, T])
        e1b, e2b = sb("e1b", [P, CB, G, T1]), sb("e2b", [P, CB, G, T1])
        lnden, rec = e2b[:, :, :, 1:T1], e1b[:, :, :, 1:T1]
        aa = sb("aa", [P, CB, G, T1])
        bb = sb("bb", [P, CB, G, T1])
        ckh, ckl = sb("ckh", [P, CB, G * T], F32R), sb("ckl", [P, CB, G * T], F32R)
        kf = [sb(f"kf{i}", [P, 2, G * T]) for i in range(4)]
        kfh, kfl = sb("kfh", [P, SPLIT, G * T], F32R), sb("kfl", [P, SPLIT, G * T], F32R)
        cth = sb("cth", [T, G, C])

        pair = [ctx.enter_context(nc.psum_tensor(f"pair{i}", [P, 2, 512], FP32)) for i in range(4)]

        params_in = sem("params_in")
        x_in = [sem(f"x_in{c}") for c in range(GROUPS)]
        wexp_done, w_ready = sem("wexp_done"), sem("w_ready")
        w_in = {n: sem("w_in_" + n) for n in ("k", "v", "r", "o", "cr", "cv")}
        stage_in, whi_ready, wlo_ready = sem("stage_in"), sem("whi_ready"), sem("wlo_ready")
        const_set = sem("const_set")
        lnstat = {k: sem(f"lnstat{k}") for k in (0, 1, 2)}
        lnlog = {k: sem(f"lnlog{k}") for k in (0, 1, 2)}
        lny0 = {k: sem(f"lny0{k}") for k in (0, 1, 2)}
        xn_ready = {k: sem(f"xn_ready{k}") for k in (1, 2)}
        turned = {k: sem(f"turned{k}") for k in (1, 2)}
        h_ready = {k: sem(f"h_ready{k}") for k in (1, 2)}
        shift_ready = sem("shift_ready")
        mix1_ready, mix2_ready = sem("mix1_ready"), sem("mix2_ready")
        ckh_ready, ckl_ready = sem("ckh_ready"), sem("ckl_ready")
        kvr_done, k_out, v_out, th_ready = sem("kvr_done"), sem("k_out"), sem("v_out"), sem("th_ready")
        arg_ready, side_ready, exp_ready = sem("arg_ready"), sem("side_ready"), sem("exp_ready")
        den_ready, num_ready, denlog, rec_ready = sem("den_ready"), sem("num_ready"), sem("denlog"), sem("rec_ready")
        wkv_ready = sem("wkv_ready")
        wo_done = sem("wo_done")
        ck_done, relu_done, square_done = sem("ck_done"), sem("relu_done"), sem("square_done")
        kfh_ready, kfl_ready = sem("kfh_ready"), sem("kfl_ready")
        cr_done, cth_ready = sem("cr_done"), sem("cth_ready")
        cv_done, cq_done, x_done = sem("cv_done"), sem("cq_done"), sem("x_done")
        dve_step = sem("dve_step")

        KVR = (1, 2, 0)
        HIDDEN = (1, 0, 2, 1)

        def valid(m):
            return 0 <= m < STEPS

        block = ctx.enter_context(nc.Block())

        @block.gpsimd
        def _(pool):
            for t in (h[1], h[2], e1b, e2b, aa):
                pool.memset(t[:, :, :, 0:1], 0.0).then_inc(const_set, 1)
            pool.memset(kp[:, :, :, 0:1], NEVER).then_inc(const_set, 1)
            pool.memset(eps[:], EPS).then_inc(const_set, 1)
            pool.memset(reset[:], 0.0).then_inc(const_set, 1)
            pool.memset(ident[:], 0.0).then_inc(const_set, 1)
            pool.wait_ge(const_set, 9)
            pool.memset(reset[:, :, 0:1], 2 * NEVER).then_inc(const_set, 1)
            pool.affine_select(out=ident[:], in_=ident[:], compare_op=ALU.not_equal, fill=1.0, base=0,
                               pattern=[[-1, P]], channel_multiplier=1).then_inc(const_set, 1)

        @block.sync
        def _(sp):
            xv = io["x"].rearrange("b t c -> t b c")
            for c in range(GROUPS):
                sp.dma_start(x[:, c * G:(c + 1) * G, :], xv[:, c * G:(c + 1) * G, :]).then_inc(x_in[c], 16)
                if c == 0:
                    sp.dma_start(ln0w[:], io["ln0_w"].partition_broadcast(T)).then_inc(params_in, 16)
                    sp.dma_start(ln0b[:], io["ln0_b"].partition_broadcast(T)).then_inc(params_in, 16)
                    sp.dma_start(prm[:, :, :, 0:NPRM - 1], io["prm"]).then_inc(params_in, 16)
            uses = (("k", wk, kvr_done, 3), ("v", wv, kvr_done, 3), ("r", wr, kvr_done, 3), ("o", wo, wo_done, 1),
                    ("cr", wcr, cr_done, 1), ("cv", wcv, cv_done, 2))

            def load_stage(l, name):
                n = 2 * l + (name == "cv")
                if n:
                    sp.wait_ge(whi_ready, n)
                    sp.wait_ge(wlo_ready, n)
                w = io["w_" + name][l].rearrange("p b c -> p (b c)")
                if name == "cv":
                    w = w[:, 0:SPLIT * C]
                sp.dma_start(stage[:, 0:w.shape[1]], w).then_inc(stage_in, 16)

            for l in range(STEPS // GROUPS):
                if l:
                    load_stage(l, "ck")
                for n, tile, used, per in uses:
                    if l:
                        sp.wait_ge(used, per * GROUPS * l)
                    w = io["w_" + n][l].rearrange("p b c -> p (b c)")
                    t = tile if n == "cv" else tile[:].rearrange("p b c -> p (b c)")
                    sp.dma_start(t[:, :], w[:, -t.shape[1]:]).then_inc(w_in[n], 16)
                    if l == 0 and n == "r":
                        load_stage(l, "ck")
                load_stage(l, "cv")
            sp.dma_start(g["wkv"][:], io["wkv"]).then_inc(g["wkv_in"], 16)
            load_context(sp, io, g["ct"], g["ct_in"], 0)

        @block.vector
        def _(dve):
            steps = [0]

            def did(ins):
                ins.then_inc(dve_step, 1)
                steps[0] += 1
                return steps[0]

            def after(n):
                dve.wait_ge(dve_step, n)

            def chunk(m):
                c = m % GROUPS
                return x[:, c * G:(c + 1) * G, :]

            def param(m, b, name):
                return prm[:, m // GROUPS, b, PRM[name]:PRM[name] + 1]

            def stats(k, xc):
                for i in range(G):
                    n = did(dve.bn_stats(st[k][:, i, :], xc[:, i, :]))
                after(n)
                for i in range(G):
                    last = dve.bn_aggr(mv[k][:, i, :], st[k][:, i, :])
                    if i < G - 1:
                        did(last)
                last.then_inc(lnstat[k], 1)

            def rsqrt(k, m):
                dve.wait_ge(lny0[k], m + 1)
                after(did(dve.tensor_tensor(yy[k][:], y0[k][:], y0[k][:], ALU.mult)))
                after(did(dve.scalar_tensor_tensor(yy[k][:], mv[k][:, :, 1], EPS, yy[k][:], ALU.add, ALU.mult)))
                after(did(dve.tensor_scalar(yy[k][:], yy[k][:], -0.5, 1.5, ALU.mult, ALU.add)))
                after(did(dve.tensor_tensor(rstd[k][:], yy[k][:], y0[k][:], ALU.mult)))

            def normalise(k, out, xc, done=None):
                for i in range(G):
                    last = dve.tensor_scalar(out[:, i, :], xc[:, i, :], mv[k][:, i, 0:1], rstd[k][:, i:i + 1],
                                             ALU.subtract, ALU.mult)
                    if i < G - 1 or done is None:
                        n = did(last)
                if done is not None:
                    last.then_inc(done, 1)
                return n

            def set_shift(m):
                dve.scalar_tensor_tensor(shift[:], mv[1][:, :, 0], -1.0, rstd[1][:], ALU.mult, ALU.mult)\
                    .then_inc(shift_ready, 1)

            def first_norm(m):
                xc = chunk(m)
                dve.wait_ge(x_in[m], 16)
                stats(0, xc)
                rsqrt(0, m)
                after(normalise(0, xc, xc))
                dve.wait_ge(params_in, 48)
                n = did(dve.tensor_tensor(xc, xc, ln0w[:].unsqueeze(1).broadcast_to([T, G, C]), ALU.mult))
                after(n)
                after(did(dve.tensor_tensor(xc, xc, ln0b[:].unsqueeze(1).broadcast_to([T, G, C]), ALU.add)))

            def difference(k, m):
                n = 0
                if m:
                    dve.wait_ge(*((kvr_done, 3 * m) if k == 1 else (cr_done, m)))
                if k == 2:
                    dve.wait_ge(mix1_ready, 6 * min(m + 3, STEPS))
                for b in range(CB):
                    dve.wait_ge(h_ready[k], CB * m + b + 1)
                    n = did(dve.tensor_tensor(diff[:, b], h[k][:, b, :, 1:T1], h[k][:, b, :, 0:T], ALU.subtract))
                return n

            def mix(k, m, names, params, done, n):
                after(n)
                for name, mu in zip(names, params):
                    for b in range(CB):
                        dve.scalar_tensor_tensor(mixed[name][:, b], diff[:, b], param(m, b, mu),
                                                 h[k][:, b, :, 0:T], ALU.mult, ALU.add).then_inc(done, 1)

            def flat(t):
                return t[:].rearrange("p b g t -> p (b g t)")

            def at(t, first):
                return t[:, :, :, first:first + T].rearrange("p b g t -> p (b g) t")

            def tokens(t):
                return t[:].rearrange("p b g t -> p (b g) t")

            def wkv_arguments(m):
                n = 0
                if m % GROUPS == 0:
                    for b in range(CB):
                        n = did(dve.tensor_scalar(decay[:, b], reset[:], param(m, b, "w"), None, ALU.add))
                    after(n)
                dve.wait_ge(k_out, m + 1)
                n = did(dve.tensor_tensor_scan(flat(pp), flat(decay), flat(kp), 0.0, ALU.add, ALU.max))
                du = rw[m % 2]
                after(n)
                dve.tensor_tensor(tokens(dp), at(pp, 0), at(pp, 1), ALU.subtract).then_inc(arg_ready, 1)
                dve.tensor_tensor(tokens(dk), at(kp, 1), at(pp, 1), ALU.subtract).then_inc(arg_ready, 1)
                for b in range(CB):
                    dve.scalar_tensor_tensor(du[:, b], kp[:, b, :, 1:T1], param(m, b, "u"),
                                             pp[:, b, :, 0:T], ALU.add, ALU.subtract).then_inc(arg_ready, 1)

            def wkv_sums(m):
                dve.wait_ge(exp_ready, 5 * m + 3)
                did(dve.tensor_tensor_scan(flat(bb), flat(e1b), flat(e2b), 0.0, ALU.mult, ALU.add))
                dve.wait_ge(v_out, m + 1)
                n = did(dve.tensor_tensor(at(aa, 1), at(e2b, 1), tokens(v), ALU.mult))
                after(n)
                did(dve.tensor_tensor_scan(flat(aa), flat(e1b), flat(aa), 0.0, ALU.mult, ALU.add))

            def wkv_denominator(m):
                dve.wait_ge(exp_ready, 5 * m + 5)
                n = did(dve.tensor_tensor(tokens(dp), tokens(e1), at(bb, 0), ALU.mult))
                after(n)
                dve.tensor_tensor(dp[:], dp[:], e2[:], ALU.add).then_inc(den_ready, 1)

            def wkv_numerator(m):
                du = rw[m % 2]
                n = did(dve.tensor_tensor(tokens(dk), tokens(e2), tokens(v), ALU.mult))
                n = did(dve.tensor_tensor(tokens(du), tokens(e1), at(aa, 0), ALU.mult))
                after(n)
                n = did(dve.tensor_tensor(du[:], du[:], dk[:], ALU.add))
                dve.wait_ge(th_ready, m + 1)
                after(n)
                dve.scalar_tensor_tensor(du[:], th[:], 1.0, du[:], ALU.add, ALU.mult).then_inc(num_ready, 1)

            def wkv_out(m):
                q = [0] * CB
                for b in range(CB):
                    dve.wait_ge(rec_ready, CB * m + b + 1)
                    q[b] = did(dve.tensor_tensor(dk[:, b], dp[:, b], rec[:, b], ALU.mult))
                for b in range(CB):
                    after(q[b])
                    q[b] = did(dve.scalar_tensor_tensor(dk[:, b], dk[:, b], 2.0, rec[:, b], ALU.subtract, ALU.mult))
                dve.wait_ge(num_ready, m + 1)
                for b in range(CB):
                    after(q[b])
                    dve.scalar_tensor_tensor(rw[m % 2][:, b], rw[m % 2][:, b], -0.5, dk[:, b], ALU.mult, ALU.mult)\
                        .then_inc(wkv_ready, 1)

            def add_wkv(m):
                xc = chunk(m)
                dve.wait_ge(wo_done, m + 1)
                return did(dve.tensor_tensor(xc.rearrange("p (i g) c -> p i (g c)", i=2),
                                             xc.rearrange("p (i g) c -> p i (g c)", i=2), pair[0][0:T], ALU.add))

            def low_ck(m):
                dve.wait_ge(ckh_ready, m + 1)
                dve.tensor_tensor(ckl[:], mixed["ck"][:].rearrange("p b g t -> p b (g t)"), ckh[:], ALU.subtract)\
                    .then_inc(ckl_ready, 1)

            def low_kf(m, j):
                dve.wait_ge(kfh_ready, SPLIT // 2 * m + j + 1)
                dve.tensor_tensor(kfl[:, 2 * j:2 * j + 2], kf[j][:], kfh[:, 2 * j:2 * j + 2], ALU.subtract)\
                    .then_inc(kfl_ready, 1)

            def low_weights(n, tile, high, used, count):
                dve.wait_ge(whi_ready, n + 1)
                if count:
                    dve.wait_ge(used, count)
                dve.tensor_tensor(tile[:], stage[:, 0:tile.shape[1]], high[:], ALU.subtract).then_inc(wlo_ready, 1)

            def gate_channel(m):
                for i in range(2):
                    g2 = slice(2 * i, 2 * i + 2)
                    if i == 0:
                        dve.wait_ge(cth_ready, m + 1)
                    dve.wait_ge(cv_done, 2 * m + i + 1)
                    dve.scalar_tensor_tensor(cth[:, g2], cth[:, g2], 1.0,
                                             pair[3][0:T, i].rearrange("p (g c) -> p g c", c=C),
                                             ALU.add, ALU.mult).then_inc(cq_done, 1)

            def add_channel(m):
                xc = chunk(m)
                for i in range(2):
                    g2 = slice(2 * i, 2 * i + 2)
                    dve.wait_ge(cq_done, 2 * m + i + 1)
                    dve.scalar_tensor_tensor(xc[:, g2], cth[:, g2], 0.5, xc[:, g2], ALU.mult, ALU.add)\
                        .then_inc(x_done, 1)

            dve.wait_ge(const_set, 11)
            dve.wait_ge(wexp_done, 1)
            pw = PRM["w"]
            dve.tensor_scalar(prm[:, :, :, pw:pw + 1], prm[:, :, :, pw:pw + 1], -1.0, None, ALU.mult).then_inc(w_ready, 1)
            dve.wait_ge(w_ready, 1)
            first_norm(0)
            for s in range(-3, STEPS + 1):
                if valid(s):
                    after(add_wkv(s))
                    stats(2, chunk(s))
                    if s % GROUPS == 0:
                        l = s // GROUPS
                        low_weights(2 * l, wckl, wckh, ck_done, 4 * GROUPS * l)
                if valid(s + 1):
                    wkv_denominator(s + 1)
                if valid(s):
                    rsqrt(2, s)
                    normalise(2, xn[2], chunk(s), xn_ready[2])
                if valid(s + 2):
                    n = difference(1, s + 2)
                    mix(1, s + 2, ("k", "v", "r"), ("tmk", "tmv", "tmr"), mix1_ready, n)
                if valid(s):
                    n = difference(2, s)
                    mix(2, s, ("cr",), ("cmr",), mix2_ready, n)
                if valid(s - 1):
                    gate_channel(s - 1)
                if valid(s):
                    mix(2, s, ("ck",), ("cmk",), mix2_ready, n)
                if valid(s + 1):
                    wkv_numerator(s + 1)
                if valid(s - 1):
                    add_channel(s - 1)
                if valid(s):
                    low_ck(s)
                if valid(s + 3):
                    if s + 3 >= GROUPS:
                        dve.wait_ge(x_done, 2 * (s + 3 - GROUPS + 1))
                    stats(1, chunk(s + 3))
                if valid(s + 1):
                    wkv_out(s + 1)
                if valid(s + 2):
                    wkv_arguments(s + 2)
                if valid(s) and s % GROUPS == 0:
                    l = s // GROUPS
                    low_weights(2 * l + 1, wcvl, wcvh, cv_done, 2 * GROUPS * l)
                if valid(s):
                    low_kf(s, 0)
                if valid(s + 3):
                    rsqrt(1, s + 3)
                    set_shift(s + 3)
                if valid(s):
                    for j in range(1, SPLIT // 2):
                        low_kf(s, j)
                if valid(s + 2):
                    wkv_sums(s + 2)
                if s + 4 < GROUPS:
                    first_norm(s + 4)

        @block.scalar
        def _(act):
            def param(m, b, name):
                return prm[:, m // GROUPS, b, PRM[name]:PRM[name] + 1]

            def padded(t):
                return t.rearrange("p (g t) -> p g t", t=T)

            def rsqrt0(k, m):
                act.wait_ge(lnstat[k], m + 1)
                act.activation(lnv[k][:], mv[k][:, :, 1], ACT.Ln, bias=eps[0:T, :]).then_inc(lnlog[k], 1)
                act.wait_ge(lnlog[k], m + 1)
                act.activation(y0[k][:], lnv[k][:], ACT.Exp, scale=-0.5).then_inc(lny0[k], 1)

            def norm_out(k, m, banks, w, b_):
                for b in range(CB):
                    act.wait_ge(turned[k], CB * m + b + 1)
                    act.activation(h[k][:, b, :, 1:T1], padded(banks[:, b, 0:G * T]), ACT.Identity,
                                   bias=param(m, b, b_), scale=param(m, b, w)).then_inc(h_ready[k], 1)

            def normalise1(m):
                act.wait_ge(shift_ready, m + 1)
                xc = x[:, (m % GROUPS) * G:(m % GROUPS + 1) * G, :]
                for i in range(G):
                    ins = act.activation(xn[1][:, i, :], xc[:, i, :], ACT.Identity, bias=shift[:, i:i + 1],
                                         scale=rstd[1][:, i:i + 1])
                ins.then_inc(xn_ready[1], 1)

            def out(m, which, dst, done, func=ACT.Copy, scale=1.0):
                act.wait_ge(kvr_done, 3 * m + which + 1)
                act.activation(dst, pair[KVR[which]][:, :, 0:G * T].rearrange("p b (g t) -> p b g t", t=T), func,
                               scale=scale).then_inc(done, 1)

            def high_ck(m):
                act.wait_ge(mix2_ready, 4 * m + 4)
                act.activation(ckh[:], mixed["ck"][:].rearrange("p b g t -> p b (g t)"), ACT.Copy).then_inc(ckh_ready, 1)

            def hidden(m, j):
                act.wait_ge(ck_done, 4 * m + j + 1)
                split = 2 * j < SPLIT
                if m and split:
                    act.wait_ge(kfl_ready, SPLIT // 2 * (m - 1) + j + 1)
                if m and not split:
                    act.wait_ge(cv_done, 2 * m)
                t = kf[j]
                act.activation(t[:], pair[HIDDEN[j]][:, :, 0:G * T], ACT.Relu).then_inc(relu_done, 1)
                act.wait_ge(relu_done, 4 * m + j + 1)
                act.activation(t[:], t[:], ACT.Square).then_inc(square_done, 1)
                if not split:
                    return
                act.wait_ge(square_done, 4 * m + j + 1)
                if m and j == 0:
                    act.wait_ge(cv_done, 2 * m)
                act.activation(kfh[:, 2 * j:2 * j + 2], t[:], ACT.Copy).then_inc(kfh_ready, 1)

            def high_weights(n, tile, used, count):
                act.wait_ge(stage_in, 16 * (n + 1))
                if count:
                    act.wait_ge(used, count)
                act.activation(tile[:], stage[:, 0:tile.shape[1]], ACT.Copy).then_inc(whi_ready, 1)

            def wkv_exp(m, what):
                if what < 2:
                    act.wait_ge(arg_ready, 4 * m + what + 1)
                if what == 0:
                    for b in range(CB):
                        act.activation(e1b[:, b, :, 1:T1], dp[:, b], ACT.Exp, bias=param(m, b, "w"))\
                            .then_inc(exp_ready, 1)
                elif what == 1:
                    act.activation(e2b[:, :, :, 1:T1], dk[:], ACT.Exp).then_inc(exp_ready, 1)
                else:
                    act.wait_ge(arg_ready, 4 * m + 4)
                    for t, sign in ((e1, 1.0), (e2, -1.0)):
                        act.activation(t[:], rw[m % 2][:], ACT.Relu, scale=sign).then_inc(side_ready, 1)
                    for i, t in enumerate((e1, e2)):
                        act.wait_ge(side_ready, 2 * m + i + 1)
                        act.activation(t[:], t[:], ACT.Exp, scale=-1.0).then_inc(exp_ready, 1)

            def reciprocal0(m):
                act.wait_ge(den_ready, m + 1)
                for b in range(CB):
                    act.activation(lnden[:, b], dp[:, b], ACT.Ln).then_inc(denlog, 1)
                for b in range(CB):
                    act.wait_ge(denlog, CB * m + b + 1)
                    act.activation(rec[:, b], lnden[:, b], ACT.Exp, scale=-1.0).then_inc(rec_ready, 1)

            def gate(m):
                act.wait_ge(cr_done, m + 1)
                if m:
                    act.wait_ge(x_done, 2 * m)
                act.activation(cth[:], pair[3][0:T].rearrange("p i (g c) -> p (i g) c", c=C), ACT.Tanh,
                               scale=0.5).then_inc(cth_ready, 1)

            act.wait_ge(const_set, 11)
            act.wait_ge(params_in, 48)
            act.preload_act_table_set(LN_EXP)
            act.activation(prm[:, :, :, PRM["w"]:PRM["w"] + 1], prm[:, :, :, PRM["td"]:PRM["td"] + 1],
                           ACT.Exp).then_inc(wexp_done, 1)
            act.wait_ge(w_ready, 1)
            rsqrt0(0, 0)
            for s in range(-3, STEPS + 1):
                if valid(s) and s % GROUPS == 0:
                    l = s // GROUPS
                    high_weights(2 * l, wckh, ck_done, 4 * GROUPS * l)
                if valid(s + 1):
                    wkv_exp(s + 1, 2)
                if valid(s):
                    rsqrt0(2, s)
                if valid(s + 2):
                    normalise1(s + 2)
                if valid(s + 1):
                    reciprocal0(s + 1)
                if valid(s + 2):
                    norm_out(1, s + 2, pair[2], "ln1w", "ln1b")
                if valid(s):
                    norm_out(2, s, pair[0], "ln2w", "ln2b")
                if s < 0:
                    rsqrt0(1, s + 3)
                if valid(s + 2):
                    out(s + 2, 0, kp[:, :, :, 1:T1], k_out)
                if valid(s):
                    high_ck(s)
                if valid(s + 2):
                    if s + 2:
                        act.wait_ge(num_ready, s + 2)
                    out(s + 2, 1, v[:], v_out)
                if valid(s + 2) or valid(s):
                    act.preload_act_table_set(EXP_TANH)
                if valid(s + 2):
                    out(s + 2, 2, th[:], th_ready, ACT.Tanh, 0.5)
                if valid(s):
                    gate(s)
                if valid(s + 2) or valid(s):
                    act.preload_act_table_set(LN_EXP)
                if s >= 0 and valid(s + 3):
                    rsqrt0(1, s + 3)
                if valid(s):
                    hidden(s, 0)
                if valid(s):
                    hidden(s, 1)
                if valid(s + 2):
                    wkv_exp(s + 2, 0)
                    wkv_exp(s + 2, 1)
                if valid(s) and s % GROUPS == 0:
                    l = s // GROUPS
                    high_weights(2 * l + 1, wcvh, cv_done, 2 * GROUPS * l)
                if s + 4 < GROUPS:
                    rsqrt0(0, s + 4)
                if valid(s):
                    hidden(s, 2)
                    hidden(s, 3)

        @block.tensor
        def _(pe):
            pe.wait_ge(const_set, 11)

            def turn(k, m, banks):
                pe.wait_ge(xn_ready[k], m + 1)
                for b in range(CB):
                    for i in range(G):
                        ins = pe.transpose(banks[:, b, i * T:(i + 1) * T], xn[k][:, i, b * P:(b + 1) * P],
                                           ident[0:T, 0:T])
                    ins.then_inc(turned[k], 1)

            def project(m, which, w, src, name):
                pe.wait_ge(w_in[name], 16 * (m // GROUPS + 1))
                for o in range(CB):
                    for b in range(CB):
                        if o == 0:
                            pe.wait_ge(mix1_ready, 6 * m + CB * which + b + 1)
                        ins = pe.matmul(pair[KVR[which]][:, o, 0:G * T], w[:, b, o * P:(o + 1) * P],
                                        src[:, b].rearrange("p g t -> p (g t)"), start=b == 0, stop=b == CB - 1)
                ins.then_inc(kvr_done, 1)

            def tokens_out(banks, src, w, ready, count):
                for i in range(G):
                    for b in range(CB):
                        if i == 0:
                            pe.wait_ge(ready, count + b + 1)
                        ins = pe.matmul(banks[0:T, i // 2, (i % 2) * C:(i % 2 + 1) * C], src[:, b, i, :], w[:, b, :],
                                        start=b == 0, stop=b == CB - 1)
                return ins

            def hidden(m, j):
                banks = pair[HIDDEN[j]]
                for i in range(2):
                    n = 0
                    o = (2 * j + i) * P
                    for w, a in ((wckh, ckh), (wckl, ckh), (wckh, ckl)):
                        if i == 0 and j == 0 and a is ckl:
                            pe.wait_ge(ckl_ready, m + 1)
                        for b in range(CB):
                            ins = pe.matmul(banks[:, i, 0:G * T], w[:, b * F + o:b * F + o + P], a[:, b, :],
                                            start=n == 0, stop=n == 3 * CB - 1)
                            n += 1
                ins.then_inc(ck_done, 1)

            def channel_out(m, sequences):
                for i in sequences:
                    n = 0
                    for j in range(F // P):
                        if i == 0 and j % 2 == 0 and j < SPLIT:
                            pe.wait_ge(kfl_ready, SPLIT // 2 * m + j // 2 + 1)
                        elif i == 0 and j % 2 == 0:
                            pe.wait_ge(square_done, 4 * m + j // 2 + 1)
                        if j < SPLIT:
                            parts = [(a[:, j], w[:, j * C:(j + 1) * C]) for a, w in ((kfh, wcvh), (kfh, wcvl), (kfl, wcvh))]
                        else:
                            parts = [(kf[j // 2][:, j % 2], wcv[:, (j - SPLIT) * C:(j - SPLIT + 1) * C])]
                        for a, w in parts:
                            ins = pe.matmul(pair[3][0:T, i // 2, (i % 2) * C:(i % 2 + 1) * C], a[:, i * T:(i + 1) * T],
                                            w, start=n == 0, stop=j == F // P - 1)
                            n += 1
                    if i % 2:
                        ins.then_inc(cv_done, 1)

            for s in range(-3, STEPS + 1):
                m = s
                if valid(m):
                    pe.wait_ge(w_in["o"], 16 * (m // GROUPS + 1))
                    if m:
                        pe.wait_ge(relu_done, 4 * m - 2)
                    else:
                        pe.wait_ge(th_ready, 2)
                    tokens_out(pair[0], rw[m % 2], wo, wkv_ready, CB * m).then_inc(wo_done, 1)
                m = s - 1
                if valid(m):
                    pe.wait_ge(wlo_ready, 2 * (m // GROUPS) + 2)
                    pe.wait_ge(w_in["cv"], 16 * (m // GROUPS + 1))
                    pe.wait_ge(cth_ready, m + 1)
                    channel_out(m, (0, 1, 2))
                m = s + 2
                if valid(m):
                    if m and s < 1:
                        pe.wait_ge(v_out, m)
                    turn(1, m, pair[2])
                m = s - 1
                if valid(m):
                    channel_out(m, (3,))
                m = s
                if valid(m):
                    turn(2, m, pair[0])
                m = s + 2
                if valid(m):
                    if m == 1:
                        pe.wait_ge(k_out, 1)
                    project(m, 0, wk, mixed["k"], "k")
                    project(m, 1, wv, mixed["v"], "v")
                    if m >= 2:
                        pe.wait_ge(h_ready[2], CB * (s + 1))
                    elif m:
                        pe.wait_ge(th_ready, 1)
                    project(m, 2, wr, mixed["r"], "r")
                m = s
                if valid(m):
                    pe.wait_ge(w_in["cr"], 16 * (m // GROUPS + 1))
                    if m:
                        pe.wait_ge(cq_done, 2 * m)
                    tokens_out(pair[3], mixed["cr"], wcr, mix2_ready, 4 * m).then_inc(cr_done, 1)
                    pe.wait_ge(wlo_ready, 2 * (m // GROUPS) + 1)
                    pe.wait_ge(ckh_ready, m + 1)
                    if valid(m + 2):
                        pe.wait_ge(k_out, m + 3)
                    hidden(m, 0)
                    if valid(m + 2):
                        pe.wait_ge(th_ready, m + 3)
                    hidden(m, 1)
                    if valid(m + 2):
                        pe.wait_ge(v_out, m + 3)
                    hidden(m, 2)
                    pe.wait_ge(relu_done, 4 * m + 1)
                    hidden(m, 3)

def attention_phase(nc, g, io):
    ctx = ExitStack()
    with ctx:
        def sb(name, shape, dt=FP32):
            return ctx.enter_context(nc.sbuf_tensor(name, shape, dt))

        def sem(name):
            return ctx.enter_context(nc.semaphore(name))

        x, ident = g["x"], g["ident"]
        wkv, bk, bv = g["wkv"], sb("bk", [ST, C]), sb("bv", [P, C])
        mask = sb("mask", [P, P])
        bvm = sb("bvm", [P, CB, P])
        ct = g["ct"] + [sb("ct1", [P, CB, CG * S])[:]]
        k = [sb(f"k{i}", [ST, STILES, C]) for i in range(2)]
        v = [sb(f"v{i}", [ST, STILES, CB, P + 1]) for i in range(2)]
        top, total, rec = (sb(n, [ST, STILES * H]) for n in ("top", "total", "rec"))
        kc = sb("kc", [P, CB])
        kvm = sb("kvm", [P, CB, P])
        kvbd, kcbd = (sb(n, [P, 2 * G, CB, P]) for n in ("kvbd", "kcbd"))
        wq, wp = sb("wq", [P, CB, C]), sb("wp", [P, CB, C])
        bq, bp = sb("bq", [T, C]), sb("bp", [T, C])
        eps = sb("eps3", [P, 1])
        xin = [sb(f"xin{i}", [T, G, C]) for i in range(2)]
        st, mv = ({i: sb(f"{n}{i}", [T, G, w]) for i in (1, 2)} for n, w in (("ast", 6), ("amv", 2)))
        lnv, y0, yy, rstd = ({i: sb(f"{n}{i}", [T, G]) for i in (1, 2)} for n in ("alnv", "ay0", "ayy", "arstd"))
        xt = sb("xt", [P, CB, G * T])
        q = sb("q", [T, G, C])
        qtop, qtotal, qrec = (sb(n, [T, G * H]) for n in ("qtop", "qtotal", "qrec"))
        qt = [sb(f"qt{i}", [P, CB, G * T]) for i in range(2)]
        den, lnden, rden = (sb(n, [P, CB, G * T]) for n in ("den", "alnden", "rden"))
        ot = sb("ot", [P, CB, G * T])
        pj = sb("pj", [T, G, C])
        proj = ctx.enter_context(nc.psum_tensor("proj", [P, STILES, 512], FP32))
        kvp = ctx.enter_context(nc.psum_tensor("kvp", [P, 512], FP32))
        qbanks = ctx.enter_context(nc.psum_tensor("qbanks", [P, 2, 512], FP32))
        abanks = ctx.enter_context(nc.psum_tensor("abanks", [P, 2, 512], FP32))

        wkv_in, b_in, ct_in = g["wkv_in"], sem("b_in"), g["ct_in"]
        const_set, mask_set, bvm_ready = sem("aconst_set"), sem("mask_set"), sem("bvm_ready")
        proj_done, kv_done = sem("proj_done"), sem("kv_done")
        v_ready, arg_ready, exp_ready, k_ready = sem("v_ready"), sem("karg_ready"), sem("kexp_ready"), sem("k_ready")
        kbias_done, kc_ready, bd_ready = sem("kbias_done"), sem("kc_ready"), sem("bd_ready")
        w_in = sem("aw_in")
        xin_in = [sem(f"xin_in{i}") for i in range(2)]
        sum_done = sem("sum_done")
        lnstat, lnlog, lny0 = ({i: sem(f"{n}{i}") for i in (1, 2)} for n in ("alnstat", "alnlog", "alny0"))
        x1_ready, x1_turned, xt_ready = sem("x1_ready"), sem("x1_turned"), sem("xt_ready")
        q_done, qbias_done, qarg_ready, qexp_ready, q_ready = (sem(n) for n in (
            "q_done", "qbias_done", "qarg_ready", "qexp_ready", "q_ready"))
        q_turned, qt_ready, den_done, num_done = sem("q_turned"), sem("qt_ready"), sem("aden_done"), sem("num_done")
        den_read, rden_ready, ot_ready = sem("den_read"), sem("rden_ready"), sem("ot_ready")
        pj_done, pj_read, x2_ready = sem("pj_done"), sem("pj_read"), sem("x2_ready")
        dve_step = sem("adve_step")
        SLOTS = B + G

        def stage(n):
            i, c = n % G, n // G
            return i, (c if c < GROUPS else None), (c - 1 if c else None)

        block = ctx.enter_context(nc.Block())

        @block.gpsimd
        def _(pool):
            pool.memset(eps[:], EPS).then_inc(const_set, 1)
            pool.memset(mask[:], 1.0).then_inc(mask_set, 1)
            for i in range(2):
                pool.memset(v[i][:, :, :, P:P + 1], 1.0).then_inc(const_set, 1)
            m = mask[:].rearrange("p (a b) -> p a b", b=D)
            pool.wait_ge(mask_set, 1)
            pool.affine_select(out=m, in_=m, compare_op=ALU.is_ge, fill=0.0, base=0, pattern=[[-D, P // D], [0, D]],
                               channel_multiplier=1).then_inc(mask_set, 1)
            pool.wait_ge(mask_set, 2)
            pool.affine_select(out=m, in_=m, compare_op=ALU.is_ge, fill=0.0, base=D - 1,
                               pattern=[[D, P // D], [0, D]], channel_multiplier=-1).then_inc(mask_set, 1)

        @block.sync
        def _(sp):
            xv = io["x"].rearrange("b t c -> t b c")

            def load_x(c):
                sp.dma_start(xin[c % 2][:], xv[:, c * G:(c + 1) * G, :]).then_inc(xin_in[c % 2], 16)

            sp.dma_start(bk[:], io["bk"].partition_broadcast(ST)).then_inc(b_in, 16)
            sp.dma_start(bv[:], io["bv"].partition_broadcast(P)).then_inc(b_in, 16)
            load_x(0)
            for tile, name in ((wq, "wq"), (wp, "wp")):
                sp.dma_start(tile[:], io[name]).then_inc(w_in, 16)
            for tile, name in ((bq, "bq"), (bp, "bp")):
                sp.dma_start(tile[:], io[name].partition_broadcast(T)).then_inc(w_in, 16)
            load_x(1)
            load_context(sp, io, ct, ct_in, 1)
            sp.dma_start(g["wrt"][:], io["wrt"]).then_inc(g["wrt_in"], 16)
            load_half(sp, g["raw"][0], io, 0, 0, g["raw_in"][0])
            for j in range(2, B // CG):
                sp.wait_ge(proj_done, CG * (j - 1))
                load_context(sp, io, ct, ct_in, j)
                if j * CG % G == 0 and j * CG // G >= 2:
                    c = j * CG // G
                    sp.wait_ge(sum_done, c - 1)
                    load_x(c)
            for c in range(GROUPS):
                sp.wait_ge(x2_ready, c + 1)
                sp.dma_start(io["x2"].rearrange("(s t) c -> t s c", t=T)[:, c * G:(c + 1) * G, :],
                             x[:, c * G:(c + 1) * G, :]).then_inc(g["x2_kept"], 16)

        @block.vector
        def _(dve):
            steps = [0]

            def did(ins):
                ins.then_inc(dve_step, 1)
                steps[0] += 1
                return steps[0]

            def after(n):
                dve.wait_ge(dve_step, n)

            def chunk(c):
                return x[:, c * G:(c + 1) * G, :]

            def tiles(banks):
                return banks[0:T].rearrange("p i (g c) -> p (i g) c", c=C)

            def over_tokens(t):
                return t[:].unsqueeze(1).broadcast_to([T, G, C])

            def heads(t):
                return t[:].rearrange("p t (h d) -> p (t h) d", d=D)

            def spread(t):
                return t[:].unsqueeze(2).broadcast_to([t.shape[0], t.shape[1], D])

            def block_diagonals(s):
                ps = kvp[:, 0:CB * (P + 1)].rearrange("p (b n) -> p b n", b=CB)
                o = s % (2 * G)
                dve.wait_ge(kc_ready, s + 1)
                if s:
                    dve.wait_ge(bd_ready, 2 * s)
                if s >= 2 * G:
                    dve.wait_ge(num_done, s // G - 1)
                n = did(dve.tensor_tensor(kvm[:], ps[:, :, 0:P], mask[:].unsqueeze(1).broadcast_to([P, CB, P]), ALU.mult))
                for b in range(CB):
                    did(dve.tensor_scalar(kcbd[:, o, b, :], mask[:], kc[:, b:b + 1], None, ALU.mult))
                after(n)
                for b in range(CB):
                    dve.scalar_tensor_tensor(kvbd[:, o, b, :], bvm[:, b, :], kc[:, b:b + 1], kvm[:, b, :],
                                             ALU.mult, ALU.add).then_inc(bd_ready, 1)

            def k_arguments(s):
                ks = k[s % 2]
                dve.wait_ge(v_ready, s + 1)
                if s >= 2:
                    dve.wait_ge(kv_done, s - 1)
                if s:
                    dve.wait_ge(k_ready, s)
                dve.tensor_tensor(ks[:], proj[0:ST, :, 0:C], bk[:].unsqueeze(1).broadcast_to([ST, STILES, C]),
                                  ALU.add).then_inc(kbias_done, 1)
                dve.wait_ge(kbias_done, s + 1)
                after(did(dve.tensor_reduce(top[:], heads(ks), AX.X, ALU.max)))
                dve.tensor_tensor(heads(ks), heads(ks), spread(top), ALU.subtract).then_inc(arg_ready, 1)

            def k_normalise(s):
                ks = k[s % 2]
                dve.wait_ge(exp_ready, s + 1)
                after(did(dve.tensor_reduce(total[:], heads(ks), AX.X, ALU.add)))
                after(did(dve.reciprocal(rec[:], total[:])))
                dve.tensor_tensor(heads(ks), heads(ks), spread(rec), ALU.mult).then_inc(k_ready, 1)

            def stats(i, c):
                xc = chunk(c)
                for j in range(G):
                    n = did(dve.bn_stats(st[i][:, j, :], xc[:, j, :]))
                after(n)
                for j in range(G):
                    last = dve.bn_aggr(mv[i][:, j, :], st[i][:, j, :])
                    if j < G - 1:
                        did(last)
                last.then_inc(lnstat[i], 1)

            def normalise(i, c, done):
                xc = chunk(c)
                dve.wait_ge(lny0[i], c + 1)
                after(did(dve.tensor_tensor(yy[i][:], y0[i][:], y0[i][:], ALU.mult)))
                after(did(dve.scalar_tensor_tensor(yy[i][:], mv[i][:, :, 1], EPS, yy[i][:], ALU.add, ALU.mult)))
                after(did(dve.tensor_scalar(yy[i][:], yy[i][:], -0.5, 1.5, ALU.mult, ALU.add)))
                after(did(dve.tensor_tensor(rstd[i][:], yy[i][:], y0[i][:], ALU.mult)))
                for j in range(G):
                    last = dve.tensor_scalar(xc[:, j, :], xc[:, j, :], mv[i][:, j, 0:1], rstd[i][:, j:j + 1],
                                             ALU.subtract, ALU.mult)
                    if j < G - 1:
                        did(last)
                last.then_inc(done, 1)

            def add_input(c):
                dve.wait_ge(xin_in[c % 2], 16 * (c // 2 + 1))
                dve.tensor_tensor(chunk(c), chunk(c), xin[c % 2][:], ALU.add).then_inc(sum_done, 1)
                dve.wait_ge(sum_done, c + 1)
                stats(1, c)

            def q_arguments(c):
                if c:
                    dve.wait_ge(q_turned, CB * c)
                dve.wait_ge(q_done, c + 1)
                dve.tensor_tensor(q[:], tiles(qbanks), over_tokens(bq), ALU.add).then_inc(qbias_done, 1)
                dve.wait_ge(qbias_done, c + 1)
                after(did(dve.tensor_reduce(qtop[:], heads(q), AX.X, ALU.max)))
                dve.tensor_tensor(heads(q), heads(q), spread(qtop), ALU.subtract).then_inc(qarg_ready, 1)

            def q_normalise(c):
                dve.wait_ge(qexp_ready, c + 1)
                after(did(dve.tensor_reduce(qtotal[:], heads(q), AX.X, ALU.add)))
                after(did(dve.reciprocal(qrec[:], qtotal[:])))
                dve.tensor_tensor(heads(q), heads(q), spread(qrec), ALU.mult).then_inc(q_ready, 1)

            def attend(c):
                dve.wait_ge(rden_ready, c + 1)
                after(did(dve.tensor_tensor(den[:], den[:], rden[:], ALU.mult)))
                after(did(dve.scalar_tensor_tensor(den[:], den[:], 2.0, rden[:], ALU.subtract, ALU.mult)))
                dve.wait_ge(num_done, c + 1)
                after(did(dve.tensor_tensor(den[:], den[:], abanks[:, :, 0:G * T], ALU.mult)))
                if c:
                    dve.wait_ge(pj_done, c)
                dve.tensor_tensor(ot[:], qt[c % 2][:], den[:], ALU.subtract).then_inc(ot_ready, 1)

            def add_attention(c):
                dve.wait_ge(pj_done, c + 1)
                dve.tensor_tensor(pj[:], tiles(abanks), over_tokens(bp), ALU.add).then_inc(pj_read, 1)
                dve.wait_ge(pj_read, c + 1)
                after(did(dve.tensor_tensor(chunk(c), chunk(c), pj[:], ALU.add)))
                stats(2, c)

            def split_x2(c):
                cols = slice(c * G * T, (c + 1) * G * T)
                dve.wait_ge(g["x2t_ready"], c + 1)
                after(did(dve.tensor_copy(g["xh"][:, :, cols], g["x2t"][:, :, cols])))
                dve.tensor_tensor(g["xl"][:, :, cols], g["x2t"][:, :, cols], g["xh"][:, :, cols], ALU.subtract)\
                    .then_inc(g["xl_ready"], 1)

            def low_weights(j):
                dve.wait_ge(g["wh_ready"], j + 1)
                dve.tensor_tensor(part(g["wl"][0], j), part(g["raw"][0], j), part(g["wh"][0], j), ALU.subtract)\
                    .then_inc(g["wl_ready"], 1)

            dve.wait_ge(mask_set, 3)
            dve.wait_ge(b_in, 32)
            dve.tensor_tensor(bvm[:], bv[:].rearrange("p (b c) -> p b c", b=CB),
                              mask[:].unsqueeze(1).broadcast_to([P, CB, P]), ALU.mult).then_inc(bvm_ready, 1)
            dve.wait_ge(bvm_ready, 1)
            dve.wait_ge(w_in, 64)
            for n in range(SLOTS):
                i, c1, c2 = stage(n)
                if n < B:
                    k_arguments(n)
                if 0 < n <= B:
                    block_diagonals(n - 1)
                if i == 0 and c1 is not None:
                    add_input(c1)
                if i == 2 and c1 is not None:
                    q_normalise(c1)
                if i == 3 and c2 is not None:
                    add_attention(c2)
                if n < B:
                    k_normalise(n)
                if i == 0 and c1 is not None:
                    normalise(1, c1, x1_ready)
                if i == 1 and c2 is not None:
                    attend(c2)
                if i == 1 and c1 is not None:
                    q_arguments(c1)
                if i == 3 and c2 is not None:
                    normalise(2, c2, x2_ready)
                if B < n < B + GROUPS:
                    split_x2(n - B - 1)
                    low_weights(n - B - 1)

        @block.scalar
        def _(act):
            def v_out(s):
                act.wait_ge(proj_done, s + 1)
                if s >= 2:
                    act.wait_ge(kv_done, s - 1)
                act.activation(v[s % 2][:, :, :, 0:P], proj[0:ST, :, C:2 * C].rearrange("p t (b c) -> p t b c", b=CB),
                               ACT.Copy).then_inc(v_ready, 1)

            def sums_out(s):
                act.wait_ge(kv_done, s + 1)
                if s:
                    act.wait_ge(bd_ready, 2 * s)
                act.activation(kc[:], kvp[:, P:2 * P + 2:P + 1], ACT.Copy).then_inc(kc_ready, 1)

            def rsqrt0(i, c):
                act.wait_ge(lnstat[i], c + 1)
                act.activation(lnv[i][:], mv[i][:, :, 1], ACT.Ln, bias=eps[0:T, :]).then_inc(lnlog[i], 1)
                act.wait_ge(lnlog[i], c + 1)
                act.activation(y0[i][:], lnv[i][:], ACT.Exp, scale=-0.5).then_inc(lny0[i], 1)

            def denominator_out(c):
                act.wait_ge(den_done, c + 1)
                if c:
                    act.wait_ge(ot_ready, c)
                act.activation(lnden[:], abanks[:, :, 0:G * T], ACT.Ln).then_inc(den_read, 1)
                act.activation(den[:], abanks[:, :, 0:G * T], ACT.Copy).then_inc(den_read, 1)
                act.wait_ge(den_read, 2 * c + 1)
                act.activation(rden[:], lnden[:], ACT.Exp, scale=-1.0).then_inc(rden_ready, 1)

            def x2_out(c):
                act.wait_ge(g["x2_turned"], CB * (c + 1))
                act.activation(g["x2t"][:, :, c * G * T:(c + 1) * G * T], qbanks[:, :, 0:G * T], ACT.Copy)\
                    .then_inc(g["x2t_ready"], 1)

            def high_weights(j):
                if j == 0:
                    act.wait_ge(g["raw_in"][0], 48)
                act.activation(part(g["wh"][0], j), part(g["raw"][0], j), ACT.Copy).then_inc(g["wh_ready"], 1)

            act.preload_act_table_set(LN_EXP)
            act.wait_ge(const_set, 3)
            v_out(0)
            for n in range(SLOTS):
                i, c1, c2 = stage(n)
                if 0 < n <= B:
                    sums_out(n - 1)
                if n < B:
                    act.wait_ge(arg_ready, n + 1)
                    act.activation(k[n % 2][:], k[n % 2][:], ACT.Exp).then_inc(exp_ready, 1)
                if i == 0 and c1 is not None:
                    rsqrt0(1, c1)
                if i == 3 and c2 is not None:
                    rsqrt0(2, c2)
                if i == 3 and c1 is not None:
                    act.wait_ge(q_turned, CB * (c1 + 1))
                    act.activation(qt[c1 % 2][:], qbanks[:, :, 0:G * T], ACT.Copy).then_inc(qt_ready, 1)
                if n + 1 < B:
                    v_out(n + 1)
                if i == 1 and c1 is not None:
                    act.wait_ge(qarg_ready, c1 + 1)
                    act.activation(q[:], q[:], ACT.Exp).then_inc(qexp_ready, 1)
                if i == 0 and c2 is not None:
                    denominator_out(c2)
                if i == 0 and c1 is not None:
                    act.wait_ge(x1_turned, CB * (c1 + 1))
                    act.activation(xt[:], qbanks[:, :, 0:G * T], ACT.Copy).then_inc(xt_ready, 1)
                if B <= n < B + GROUPS - 1:
                    x2_out(n - B)
                    high_weights(n - B)
            act.wait_ge(g["r_done"], 1)
            logits_out(act, kvp, g, EARLY)

        @block.tensor
        def _(pe):
            def project(s):
                if s % CG == 0:
                    j = s // CG
                    pe.wait_ge(ct_in[j % 2], 16 * (j // 2 + 1))
                if s:
                    pe.wait_ge(kbias_done, s)
                    pe.wait_ge(v_ready, s)
                c0 = (s % CG) * S
                for t in range(STILES):
                    for b in range(CB):
                        ins = pe.matmul(proj[0:ST, t, :], ct[(s // CG) % 2][:, b, c0 + t * ST:c0 + (t + 1) * ST],
                                        wkv[:, b, :], start=b == 0, stop=b == CB - 1)
                ins.then_inc(proj_done, 1)

            def turn(src, done):
                for b in range(CB):
                    for i in range(G):
                        ins = pe.transpose(qbanks[:, b, i * T:(i + 1) * T], src[:, i, b * P:(b + 1) * P], ident[0:T, 0:T])
                    ins.then_inc(done, 1)

            def tokens_out(banks, src, w, done):
                for i in range(G):
                    for b in range(CB):
                        ins = pe.matmul(banks[0:T, i // 2, (i % 2) * C:(i % 2 + 1) * C], src[:, b, i * T:(i + 1) * T],
                                        w[:, b, :], start=b == 0, stop=b == CB - 1)
                ins.then_inc(done, 1)

            def by_heads(mat, c, done):
                for b in range(CB):
                    for i in range(G):
                        ins = pe.matmul(abanks[:, b, i * T:(i + 1) * T], mat[:, (c * G + i) % (2 * G), b, :],
                                        qt[c % 2][:, b, i * T:(i + 1) * T], start=True, stop=True)
                ins.then_inc(done, 1)

            pe.wait_ge(wkv_in, 16)
            project(0)
            pe.wait_ge(w_in, 64)
            for n in range(SLOTS):
                i, c1, c2 = stage(n)
                if i == 1 and c1 is not None:
                    pe.wait_ge(xt_ready, c1 + 1)
                    tokens_out(qbanks, xt, wq, q_done)
                if i == 1 and c2 is not None:
                    pe.wait_ge(den_read, 2 * (c2 + 1))
                    by_heads(kvbd, c2, num_done)
                if i == 2 and c2 is not None:
                    pe.wait_ge(ot_ready, c2 + 1)
                    tokens_out(abanks, ot, wp, pj_done)
                if i == 3 and c1 is not None:
                    pe.wait_ge(q_ready, c1 + 1)
                    turn(q, q_turned)
                if n + 1 < B:
                    project(n + 1)
                if i == 0 and c2 is not None:
                    pe.wait_ge(bd_ready, 2 * n)
                    pe.wait_ge(qt_ready, c2 + 1)
                    if c2:
                        pe.wait_ge(pj_read, c2)
                    by_heads(kcbd, c2, den_done)
                if n < B:
                    pe.wait_ge(k_ready, n + 1)
                    if n:
                        pe.wait_ge(bd_ready, 2 * n)
                    for b in range(CB):
                        for t in range(STILES):
                            ins = pe.matmul(kvp[:, b * (P + 1):(b + 1) * (P + 1)], k[n % 2][:, t, b * P:(b + 1) * P],
                                            v[n % 2][:, t, b, :], start=t == 0, stop=t == STILES - 1)
                    ins.then_inc(kv_done, 1)
                if i == 0 and c1 is not None:
                    pe.wait_ge(x1_ready, c1 + 1)
                    if c1:
                        pe.wait_ge(qt_ready, c1)
                    turn(x[:, c1 * G:(c1 + 1) * G, :], x1_turned)
                if B <= n < B + GROUPS - 1:
                    c = n - B
                    if c:
                        pe.wait_ge(g["x2t_ready"], c)
                    else:
                        pe.wait_ge(qt_ready, GROUPS)
                    pe.wait_ge(x2_ready, c + 1)
                    turn(x[:, c * G:(c + 1) * G, :], g["x2_turned"])
            pe.wait_ge(g["wrt_in"], 16)
            pe.wait_ge(g["x2t_ready"], GROUPS - 1)
            pe.wait_ge(bd_ready, 2 * B)
            route(pe, kvp, g, EARLY)

def expert_phase(nc, g, io):
    ctx = ExitStack()
    with ctx:
        def sb(name, shape, dt=FP32):
            return ctx.enter_context(nc.sbuf_tensor(name, shape, dt))

        def sem(name):
            return ctx.enter_context(nc.semaphore(name))

        x, ident, raw, raw_in, x2_kept = g["x"], g["ident"], g["raw"], g["raw_in"], g["x2_kept"]
        eps = sb("eps4", [P, 1])
        xh, xl, xt, logit, acc = g["xh"], g["xl"], g["x2t"], g["logit"], g["acc"]
        top, total, rec = (sb(n, [P, 2 * TILES]) for n in ("ltop", "ltotal", "lrec"))
        cw = sb("cw", [P, E, TILES])
        cws, cwr = sb("cws", [P, TILES]), sb("cwr", [P, TILES])
        wh, wl = g["wh"] + [sb("wh1", [P, WH], F32R)], g["wl"] + [sb("wl1", [P, WH], F32R)]
        sil = [sb(f"sil{i}", [P, COLS]) for i in range(2)]
        hf = [sb(f"hf{i}", [P, COLS]) for i in range(2)]
        hh = [sb(f"hh{i}", [P, FB, COLS], F32R) for i in range(2)]
        hl = [sb(f"hl{i}", [P, FB, COLS], F32R) for i in range(2)]
        xk = sb("xk", [P, TILES, C])
        st, mv = sb("fst", [P, TILES, 6]), sb("fmv", [P, TILES, 2])
        lnv, y0, yy, rstd, shift = (sb(n, [P, TILES]) for n in ("flnv", "fy0", "fyy", "frstd", "fshift"))
        turned = ctx.enter_context(nc.psum_tensor("fbanks01", [P, 2, 512], FP32))
        bank = [turned[:, 0], turned[:, 1]]
        bank += [ctx.enter_context(nc.psum_tensor(f"fbank{i}", [P, 512], FP32)) for i in range(2, 8)]

        eps_set, xk_in = sem("feps_set"), sem("xk_in")
        x_turned, xt_ready, xl_ready, logit_ready = g["x2_turned"], g["x2t_ready"], g["xl_ready"], g["logit_ready"]
        larg_ready, lexp_ready, cw_ready = sem("larg_ready"), sem("lexp_ready"), sem("cw_ready")
        wh_ready, wl_ready = g["wh_ready"], g["wl_ready"]
        gu_done, sil_ready, hf_ready, hh_ready, hl_ready = (sem(n) for n in (
            "gu_done", "sil_ready", "hf_ready", "hh_ready", "hl_ready"))
        down_done, acc_done = sem("down_done"), sem("acc_done")
        lnstat, lnlog, lny0, shift_ready, out_ready, out_stored = (sem(n) for n in (
            "flnstat", "flnlog", "flny0", "fshift_ready", "out_ready", "out_stored"))
        dve_step = sem("fdve_step")

        STEPS_E = 2 * GROUPS
        HID_E = STEPS_E * FB
        DOWN_E = TILES
        ACC_E = 2 * TILES
        SPLIT_E = 6

        def columns(c):
            return slice(c * COLS, min((c + 1) * COLS, N))

        def tiles(c):
            return range(c * COLS // P, min((c + 1) * COLS, N) // P)

        def downs(t):
            return t // GROUPS * (TILES // 2) + 2 * (t % GROUPS)

        def accs(t):
            return t // GROUPS * TILES + 4 * (t % GROUPS)

        def reached(engine, semaphore, count):
            if not isinstance(count, int) or count > 0:
                engine.wait_ge(semaphore, count)

        def following(e, h):
            return (e, 1) if h == 0 else (e + 1, 0)

        def experts(engine, body):
            body(0)
            with engine.Fori(1, E - 1) as e:
                body(e)
            body(E - 1)

        block = ctx.enter_context(nc.Block())

        @block.gpsimd
        def _(pool):
            pool.memset(eps[:], EPS).then_inc(eps_set, 1)

        @block.sync
        def _(sp):
            load_half(sp, raw[1], io, 0, 1, raw_in[1])
            with sp.Fori(1, E) as e:
                for h in range(2):
                    sp.wait_ge(wh_ready, SPLIT_E * e - SPLIT_E + 3 * h + 3)
                    sp.wait_ge(wl_ready, SPLIT_E * e - SPLIT_E + 3 * h + 3)
                    load_half(sp, raw[h], io, e, h, raw_in[h])
            sp.wait_ge(x2_kept, 16 * GROUPS)
            sp.dma_start(xk[:], io["x2"].rearrange("(k p) c -> p k c", p=P)).then_inc(xk_in, 16)
            for c in range(GROUPS):
                k = slice(tiles(c).start, tiles(c).stop)
                sp.wait_ge(out_ready, c + 1)
                sp.dma_start(io["out"].rearrange("b t c -> (b t) c").rearrange("(k p) c -> p k c", p=P)[:, k, :],
                             acc[:, k, :]).then_inc(out_stored, 16)
            sp.wait_ge(out_stored, 16 * GROUPS)

        @block.vector
        def _(dve):
            steps = [0]

            def did(ins):
                ins.then_inc(dve_step, 1)
                steps[0] += 1
                return steps[0]

            def after(n):
                dve.wait_ge(dve_step, n)

            def split_x(c):
                cols = slice(c * G * T, (c + 1) * G * T)
                dve.wait_ge(xt_ready, c + 1)
                after(did(dve.tensor_copy(xh[:, :, cols], xt[:, :, cols])))
                dve.tensor_tensor(xl[:, :, cols], xt[:, :, cols], xh[:, :, cols], ALU.subtract).then_inc(xl_ready, 1)

            def low_weights(e, h, j):
                reached(dve, wh_ready, e * SPLIT_E + 3 * h + j + 1)
                reached(dve, down_done, e * DOWN_E + downs(h * GROUPS - GROUPS))
                dve.tensor_tensor(part(wl[h], j), part(raw[h], j), part(wh[h], j), ALU.subtract).then_inc(wl_ready, 1)

            def combine_weights():
                lf = logit[:].rearrange("p w k e -> p (w k) e")
                ct = cw[:].rearrange("p e k -> p k e")
                dve.wait_ge(logit_ready, 2)
                after(did(dve.tensor_scalar(logit[:, 1], logit[:, 1], 1.0 / GATE_TEMP, None, ALU.mult)))
                after(did(dve.tensor_reduce(top[:], lf, AX.X, ALU.max)))
                dve.tensor_tensor(lf, lf, top[:].unsqueeze(2).broadcast_to([P, 2 * TILES, E]), ALU.subtract)\
                    .then_inc(larg_ready, 1)
                dve.wait_ge(lexp_ready, 1)
                after(did(dve.tensor_reduce(total[:], lf, AX.X, ALU.add)))
                after(did(dve.reciprocal(rec[:], total[:])))
                after(did(dve.tensor_tensor(lf, lf, rec[:].unsqueeze(2).broadcast_to([P, 2 * TILES, E]), ALU.mult)))
                after(did(dve.tensor_tensor(ct, logit[:, 0], logit[:, 1], ALU.mult)))
                after(did(dve.tensor_reduce(cws[:], ct, AX.X, ALU.add)))
                after(did(dve.tensor_scalar(cws[:], cws[:], 1e-9, None, ALU.add)))
                after(did(dve.reciprocal(cwr[:], cws[:])))
                dve.tensor_tensor(ct, ct, cwr[:].unsqueeze(2).broadcast_to([P, TILES, E]), ALU.mult)\
                    .then_inc(cw_ready, 1)
                dve.wait_ge(cw_ready, 1)

            def times_up(e, t, f):
                n, i = t * FB + f, f % 2
                w = columns(t % GROUPS).stop - columns(t % GROUPS).start
                dve.wait_ge(sil_ready, e * HID_E + n + 1)
                dve.wait_ge(gu_done, e * (2 * HID_E) + 2 * n + 2)
                reached(dve, hh_ready, e * HID_E + n - 1)
                reached(dve, hl_ready, e * HID_E + n - 1)
                dve.tensor_tensor(hf[i][:, 0:w], sil[i][:, 0:w], bank[2 * i + 1][:, 0:w], ALU.mult).then_inc(hf_ready, 1)

            def low_h(e, n):
                t, f = n // FB, n % FB
                w = columns(t % GROUPS).stop - columns(t % GROUPS).start
                dve.wait_ge(hh_ready, e * HID_E + n + 1)
                dve.tensor_tensor(hl[t % 2][:, f, 0:w], hf[f % 2][:, 0:w], hh[t % 2][:, f, 0:w], ALU.subtract)\
                    .then_inc(hl_ready, 1)

            def accumulate(e, t, start):
                for i, k in enumerate(tiles(t % GROUPS)):
                    if i % 2 == 0:
                        dve.wait_ge(down_done, e * DOWN_E + downs(t) + i // 2 + 1)
                    ps = bank[4 + 2 * (t % 2) + i // 2][:, (i % 2) * C:(i % 2 + 1) * C]
                    own = e if t >= 0 else e - 1
                    a, w = acc[:, k, :], cw[:, own, k:k + 1]
                    if start:
                        ins = dve.tensor_scalar(a, ps, w, None, ALU.mult)
                    else:
                        if i == 0:
                            dve.wait_ge(acc_done, e * ACC_E + accs(t - GROUPS + 1))
                        ins = dve.scalar_tensor_tensor(a, ps, w, a, ALU.mult, ALU.add)
                    ins.then_inc(acc_done, 1)

            def expert(e):
                for t in range(STEPS_E):
                    for f in range(FB):
                        n = t * FB + f
                        times_up(e, t, f)
                        if n or not isinstance(e, int) or e:
                            low_h(e, n - 1)
                        if f == 1 and t % GROUPS and not (isinstance(e, int) and e == E - 1 and t > GROUPS):
                            e_, h_ = following(e, t // GROUPS)
                            low_weights(e_, h_, t % GROUPS - 1)
                        if f == FB - 1 and (t >= 2 or not isinstance(e, int) or e):
                            accumulate(e, t - 2, isinstance(e, int) and e == 0 and t - 2 < GROUPS)
                    if isinstance(e, int) and e == E - 1 and t == STEPS_E - 2:
                        final_stats(0)

            def final_stats(c):
                k = tiles(c)
                xc = xk[:, k.start:k.stop, :]
                dve.wait_ge(xk_in, 16)
                dve.wait_ge(acc_done, (E - 1) * ACC_E + accs(STEPS_E - GROUPS + c) + len(k))
                after(did(dve.tensor_tensor(xc, xc, acc[:, k.start:k.stop, :], ALU.add)))
                for i in k:
                    last = did(dve.bn_stats(st[:, i, :], xk[:, i, :]))
                after(last)
                for i in k:
                    last = dve.bn_aggr(mv[:, i, :], st[:, i, :])
                    if i < k.stop - 1:
                        did(last)
                last.then_inc(lnstat, 1)

            def final_scale(c):
                k = slice(tiles(c).start, tiles(c).stop)
                dve.wait_ge(lny0, c + 1)
                after(did(dve.tensor_tensor(yy[:, k], y0[:, k], y0[:, k], ALU.mult)))
                after(did(dve.scalar_tensor_tensor(yy[:, k], mv[:, k, 1], EPS, yy[:, k], ALU.add, ALU.mult)))
                after(did(dve.tensor_scalar(yy[:, k], yy[:, k], -0.5, 1.5, ALU.mult, ALU.add)))
                after(did(dve.tensor_tensor(rstd[:, k], yy[:, k], y0[:, k], ALU.mult)))
                dve.scalar_tensor_tensor(shift[:, k], mv[:, k, 0], -1.0, rstd[:, k], ALU.mult, ALU.mult)\
                    .then_inc(shift_ready, 1)

            split_x(GROUPS - 1)
            combine_weights()
            experts(dve, expert)
            low_h(E - 1, HID_E - 1)
            final_stats(1)
            accumulate(E - 1, STEPS_E - 2, False)
            final_scale(0)
            final_stats(2)
            accumulate(E - 1, STEPS_E - 1, False)
            final_scale(1)
            final_stats(3)
            final_scale(2)
            final_scale(3)

        @block.scalar
        def _(act):
            def high_weights(e, h, j):
                if j == 0:
                    act.wait_ge(raw_in[h], 48 * e + 48)
                reached(act, down_done, e * DOWN_E + downs(h * GROUPS - GROUPS))
                act.activation(part(wh[h], j), part(raw[h], j), ACT.Copy).then_inc(wh_ready, 1)

            def high_h(e, n):
                t, f = n // FB, n % FB
                w = columns(t % GROUPS).stop - columns(t % GROUPS).start
                if f == 0:
                    reached(act, down_done, e * DOWN_E + downs(t - 1))
                act.wait_ge(hf_ready, e * HID_E + n + 1)
                act.activation(hh[t % 2][:, f, 0:w], hf[f % 2][:, 0:w], ACT.Copy).then_inc(hh_ready, 1)

            def expert(e):
                for t in range(STEPS_E):
                    w = columns(t % GROUPS).stop - columns(t % GROUPS).start
                    for f in range(FB):
                        n = t * FB + f
                        act.wait_ge(gu_done, e * (2 * HID_E) + 2 * n + 1)
                        reached(act, hf_ready, e * HID_E + n - 1)
                        act.activation(sil[f % 2][:, 0:w], bank[2 * (f % 2)][:, 0:w], ACT.Silu).then_inc(sil_ready, 1)
                        if n or not isinstance(e, int) or e:
                            high_h(e, n - 1)
                        if f == 1 and t % GROUPS and not (isinstance(e, int) and e == E - 1 and t > GROUPS):
                            e_, h_ = following(e, t // GROUPS)
                            high_weights(e_, h_, t % GROUPS - 1)

            act.preload_act_table_set(LN_EXP)
            act.wait_ge(x_turned, CB * GROUPS)
            act.activation(xt[:, :, (GROUPS - 1) * G * T:N], turned[:, :, 0:G * T], ACT.Copy).then_inc(xt_ready, 1)
            act.wait_ge(g["r_done"], 2)
            logits_out(act, bank[4], g, LATE)
            act.wait_ge(larg_ready, 1)
            lf = logit[:].rearrange("p w k e -> p (w k e)")
            act.activation(lf, lf, ACT.Exp).then_inc(lexp_ready, 1)
            experts(act, expert)
            high_h(E - 1, HID_E - 1)
            act.wait_ge(eps_set, 1)
            act.preload_act_table_set(LN_EXP)

            def rsqrt0(c):
                k = slice(tiles(c).start, tiles(c).stop)
                act.wait_ge(lnstat, c + 1)
                act.activation(lnv[:, k], mv[:, k, 1], ACT.Ln, bias=eps[:]).then_inc(lnlog, 1)
                act.wait_ge(lnlog, c + 1)
                act.activation(y0[:, k], lnv[:, k], ACT.Exp, scale=-0.5).then_inc(lny0, 1)

            def final_norm(c):
                act.wait_ge(shift_ready, c + 1)
                for k in tiles(c):
                    ins = act.activation(acc[:, k, :], xk[:, k, :], ACT.Identity, bias=shift[:, k:k + 1],
                                         scale=rstd[:, k:k + 1])
                ins.then_inc(out_ready, 1)

            rsqrt0(0)
            rsqrt0(1)
            for c in range(GROUPS):
                final_norm(c)
                if c + 2 < GROUPS:
                    rsqrt0(c + 2)

        @block.tensor
        def _(pe):
            def gate_up(e, t):
                h, c = t // GROUPS, t % GROUPS
                w = columns(c).stop - columns(c).start
                if c == 0:
                    pe.wait_ge(wl_ready, e * SPLIT_E + 3 * h + 3)
                if isinstance(e, int) and e == 0 and h == 0:
                    pe.wait_ge(xl_ready, -(-columns(c).stop // (G * T)))
                for f in range(FB):
                    reached(pe, hf_ready, e * HID_E + t * FB + f - 1)
                    for k, w0 in ((0, GATE), (1, UP)):
                        n = 0
                        for a, m in ((xh, wh), (xl, wh), (xh, wl)):
                            for b in range(CB):
                                o = w0 + b * FB * P + f * P
                                ins = pe.matmul(bank[2 * (f % 2) + k][:, 0:w], m[h][:, o:o + P], a[:, b, columns(c)],
                                                start=n == 0, stop=n == 3 * CB - 1)
                                n += 1
                        ins.then_inc(gu_done, 1)

            def down(e, t):
                h = t // GROUPS % 2
                reached(pe, acc_done, e * ACC_E + accs(t - 1))
                for i, k in enumerate(tiles(t % GROUPS)):
                    n = 0
                    for f in range(FB):
                        if i == 0:
                            pe.wait_ge(hl_ready, e * HID_E + t * FB + f + 1)
                        for a, m in ((hh, wh), (hh, wl), (hl, wh)):
                            ins = pe.matmul(bank[4 + 2 * (t % 2) + i // 2][:, (i % 2) * C:(i % 2 + 1) * C],
                                            a[t % 2][:, f, i * P:(i + 1) * P],
                                            m[h][:, DOWN + f * C:DOWN + (f + 1) * C], start=n == 0,
                                            stop=n == 3 * FB - 1)
                            n += 1
                    if i % 2:
                        ins.then_inc(down_done, 1)

            def expert(e):
                for t in range(STEPS_E):
                    gate_up(e, t)
                    if t or not isinstance(e, int) or e:
                        down(e, t - 1)

            for b in range(CB):
                for i in range(G):
                    ins = pe.transpose(turned[:, b, i * T:(i + 1) * T], x[:, (GROUPS - 1) * G + i, b * P:(b + 1) * P],
                                       ident[0:T, 0:T])
                ins.then_inc(x_turned, 1)
            pe.wait_ge(xt_ready, GROUPS)
            route(pe, bank[4], g, LATE)
            experts(pe, expert)
            down(E - 1, STEPS_E - 1)

def build(nc, io):
    with ExitStack() as ctx:
        g = {
            "x": ctx.enter_context(nc.sbuf_tensor("x", [T, B, C], FP32)),
            "ident": ctx.enter_context(nc.sbuf_tensor("ident", [P, P], FP32)),
            "raw": [ctx.enter_context(nc.sbuf_tensor(f"raw{i}", [P, WH], FP32)) for i in range(2)],
            "ct_in": [ctx.enter_context(nc.semaphore(f"ct_in{i}")) for i in range(2)],
            "wkv_in": ctx.enter_context(nc.semaphore("wkv_in")),
            "raw_in": [ctx.enter_context(nc.semaphore(f"raw_in{i}")) for i in range(2)],
            "x2_kept": ctx.enter_context(nc.semaphore("x2_kept")),
        }
        for n in ("x2_turned", "x2t_ready", "xl_ready", "wh_ready", "wl_ready", "wrt_in", "r_done", "logit_ready"):
            g[n] = ctx.enter_context(nc.semaphore(n))
        g["stage"] = g["raw"][0][:, 0:CB * F]
        cols = CB * CG * S
        g["ct"] = [g["raw"][1][:, 0:cols].rearrange("p (b n) -> p b n", b=CB)]
        g["wkv"] = g["raw"][1][:, cols:cols + CB * 2 * C].rearrange("p (b n) -> p b n", b=CB)
        rwkv_phase(nc, g, io)
        g["xh"], g["xl"] = (ctx.enter_context(nc.sbuf_tensor(n, [P, CB, N], F32R)) for n in ("xh", "xl"))
        g["wh"], g["wl"] = ([ctx.enter_context(nc.sbuf_tensor(n, [P, WH], F32R))] for n in ("wh0", "wl0"))
        g["acc"] = ctx.enter_context(nc.sbuf_tensor("acc", [P, TILES, C], FP32))
        g["x2t"] = g["acc"][:].rearrange("p k c -> p (k c)").rearrange("p (b n) -> p b n", b=CB)
        g["wrt"] = ctx.enter_context(nc.sbuf_tensor("wrt", [P, CB, 2 * E], FP32))
        g["logit"] = ctx.enter_context(nc.sbuf_tensor("logit", [P, 2, TILES, E], FP32))
        attention_phase(nc, g, io)
        expert_phase(nc, g, io)

def lay_out(inputs):
    import numpy as np

    def rows(w):
        *lead, k, n = w.shape
        return np.ascontiguousarray(np.moveaxis(w.reshape(*lead, k // P, P, n), -3, -2))

    a = {k.removeprefix("L0_"): np.asarray(v) for k, v in inputs.items()}
    out = {"x": a["x"], "ln0_w": a["attn_ln0_w"], "ln0_b": a["attn_ln0_b"]}
    for n, name in (("k", "Wk"), ("v", "Wv"), ("r", "Wr"), ("o", "Wo"), ("ck", "Wck"), ("cr", "Wcr"), ("cv", "Wcv")):
        out["w_" + n] = rows(np.swapaxes(a["attn_" + name], -1, -2))
    prm = [a["attn_" + n] for n in ("ln1_w", "ln1_b", "tmk", "tmv", "tmr", "time_decay", "time_first", "ln2_w",
                                    "ln2_b", "cmk", "cmr")]
    out["prm"] = np.ascontiguousarray(np.stack(prm).reshape(len(prm), L, CB, P).transpose(3, 1, 2, 0))
    out["ctx_t"] = np.ascontiguousarray(a["ctx_1024"].reshape(B * S, CB, P).transpose(2, 1, 0))
    out["wkv"] = np.concatenate([rows(a["xattn_Wk"].T), rows(a["xattn_Wv"].T)], axis=-1)
    out["wq"], out["wp"] = rows(a["xattn_Wq"].T), rows(a["xattn_Wp"].T)
    for n in "kvqp":
        out["b" + n] = a["xattn_b" + n]
    out["wrt"] = np.concatenate([rows(a["ffn_w_router"]), rows(a["ffn_w_gating"])], axis=-1)
    for n in ("w_gate", "w_up", "w_down"):
        out[n] = a["ffn_" + n]
    return out

def kernel(**inputs):
    import concourse.bacc as bacc
    from concourse.bass_utils import run_bass_kernel_spmd

    nc = bacc.Bacc("TRN2", target_bir_lowering=False, num_devices=1)
    arrays = lay_out(inputs)
    io = {n: nc.dram_tensor(f"in_{n}", a.shape, mybir.dt.from_np(a.dtype), kind="ExternalInput").ap()
          for n, a in arrays.items()}
    io["x2"] = nc.dram_tensor("x2_kept", (N, C), FP32, kind="Internal").ap()
    io["out"] = nc.dram_tensor("out_x", (B, T, C), FP32, kind="ExternalOutput").ap()
    build(nc, io)
    r = run_bass_kernel_spmd(nc, [{f"in_{n}": a for n, a in arrays.items()}], core_ids=[0])
    return r.results[0]["out_x"]
```
